# Optimizing a Trainium2 kernel written in Bass

```python
import numpy as np
import jax
import jax.numpy as jnp

def _softmax(x, axis=-1):
    return jax.nn.softmax(x, axis=axis)

def _gelu(x):
    return jax.nn.gelu(x, approximate=True)

def _silu(x):
    return jax.nn.silu(x)

def _sigmoid(x):
    return jax.nn.sigmoid(x)

def _layernorm(x, axis=-1, eps=1e-05):
    m = jnp.mean(x, axis=axis, keepdims=True)
    v = jnp.var(x, axis=axis, keepdims=True)
    return (x - m) / jnp.sqrt(v + eps)

def _scatter_add(tgt, idx, src, axis=0):
    return tgt.at[idx].add(src)

def _segment_sum(src, seg, n):
    return jax.ops.segment_sum(src, seg, n)
kernel_name = 'mk_xattn_ffn_d2_seqx_r8_3692de'

def setup_inputs(seed: int=0):
    np.random.seed(seed)
    _w = jnp.asarray

    def _rec_inputs():
        import jax
        import jax.numpy as jnp
        _rk = jax.random.key(seed)
        x = -0.000125 + 0.9999 * jax.random.normal(jax.random.fold_in(_rk, 1), (4, 256, 256), jnp.float32)
        _lenS = 256 - jax.random.randint(jax.random.fold_in(_rk, 7), (4,), 0, max(1, 256 // 4) + 1, jnp.int32)
        _lenS2 = 256 - jax.random.randint(jax.random.fold_in(_rk, 8), (4,), 0, max(1, 256 // 4) + 1, jnp.int32)
        fside_BxS2xS2_0 = -3.05549e-07 + 0.0199987 * jax.random.normal(jax.random.fold_in(_rk, 11), (4, 256, 256), jnp.float32)
        _ctx_1024P = jax.random.normal(jax.random.fold_in(_rk, 12), (4, 16, 128), jnp.float32)
        _ctx_1024c = jax.random.dirichlet(jax.random.fold_in(_rk, 512), 0.3 * jnp.ones((16,), jnp.float32), (4, 256))
        _ctx_1024t = jnp.einsum('bsk,bkd->bsd', _ctx_1024c, _ctx_1024P)
        _ctx_1024t = _ctx_1024t * jax.lax.rsqrt(jnp.mean(jnp.square(_ctx_1024t)) + 1e-12) * 0.953939
        ctx_1024 = 6.82029e-06 + 0.0200006 * (_ctx_1024t + 0.3 * jax.random.normal(jax.random.fold_in(_rk, 612), (4, 256, 128), jnp.float32))
        _validS = jnp.arange(256)[None, :] < _lenS[:, None]
        _validS2 = jnp.arange(256)[None, :] < _lenS2[:, None]
        _causal = jnp.tril(jnp.ones((256, 256), dtype=bool))
        mask_BxS2_bf1 = jnp.ones((4, 256), dtype=bool)
        return (x, fside_BxS2xS2_0, ctx_1024, mask_BxS2_bf1)
    x, fside_BxS2xS2_0, ctx_1024, mask_BxS2_bf1 = _rec_inputs()

    def _L0_xattn_setup():
        import jax, jax.numpy as jnp
        import numpy as np
        EPS = 1e-06
        QMAX = 127.0

        def _smooth_quant_linear(x, w):
            amax_x = jnp.max(jnp.abs(x), axis=0)
            amax_w = jnp.max(jnp.abs(w), axis=0)
            s = jnp.sqrt(jnp.maximum(amax_x, EPS) / jnp.maximum(amax_w, EPS))
            s = jnp.maximum(s, EPS)
            xs = x / s
            ws = w * s
            x_scale = jnp.maximum(jnp.max(jnp.abs(xs), axis=-1, keepdims=True), EPS) / QMAX
            w_scale = jnp.maximum(jnp.max(jnp.abs(ws), axis=-1, keepdims=True), EPS) / QMAX
            x_q = jnp.clip(jnp.round(xs / x_scale), -QMAX, QMAX)
            w_q = jnp.clip(jnp.round(ws / w_scale), -QMAX, QMAX)
            return x_q @ w_q.T * x_scale * w_scale.T

        def _expert_forward(xe, guw, dw):
            h = _smooth_quant_linear(xe, guw)
            gate, up = jnp.split(h, 2, axis=-1)
            a = jax.nn.silu(gate) * up
            return _smooth_quant_linear(a, dw)
        key = jax.random.key(seed)
        k1, k2, k3 = jax.random.split(key, 3)
        E, T, D, I = (8, 256, 256, 128)
        x = jax.random.normal(k1, (E, T, D), dtype=jnp.float32)
        gate_up_weight = jax.random.normal(k2, (E, 2 * I, D), dtype=jnp.float32) * 0.02
        down_weight = jax.random.normal(k3, (E, D, I), dtype=jnp.float32) * 0.02
        return {'x': x, 'gate_up_weight': gate_up_weight, 'down_weight': down_weight}
    _L0_xattn_all = _L0_xattn_setup()
    _L0_xattn_in = {k: v for k, v in _L0_xattn_all.items() if k in ()}
    del _L0_xattn_all

    def _L0_ffn_setup():
        import jax, jax.numpy as jnp
        import numpy as np
        EPS = 1e-08

        def _quantize(w):
            gamma = jnp.mean(jnp.abs(w))
            return jnp.clip(jnp.round(w / (gamma + EPS)), -1.0, 1.0)

        def _bitlinear(x, w):
            return jnp.matmul(x, _quantize(w).T)
        key = jax.random.key(seed)
        k1, k2, k3, k4 = jax.random.split(key, 4)
        d, h = (256, 704)
        x = jax.random.normal(k1, (4, 256, d), dtype=jnp.float32)
        w1 = jax.random.normal(k2, (h, d), dtype=jnp.float32)
        w2 = jax.random.normal(k3, (h, d), dtype=jnp.float32)
        w3 = jax.random.normal(k4, (d, h), dtype=jnp.float32)
        return {'x': x, 'w1': w1, 'w2': w2, 'w3': w3}
    _L0_ffn_all = _L0_ffn_setup()
    _L0_ffn_in = {k: v for k, v in _L0_ffn_all.items() if k in ('w1', 'w2', 'w3')}
    del _L0_ffn_all

    def _L1_xattn_setup():
        import jax, jax.numpy as jnp
        import numpy as np
        N_HEADS = 16
        N_KV_HEADS = 8
        HEAD_DIM = 128
        D_TEXT = 256
        D_VISION = 128
        GROUPS = N_HEADS // N_KV_HEADS
        key = jax.random.key(seed)
        ks = jax.random.split(key, 6)
        B, T_text, T_vis = (4, 256, 72)
        text_hidden = jax.random.normal(ks[0], (B, T_text, D_TEXT), dtype=jnp.float32)
        vision_tokens = jax.random.normal(ks[1], (B, T_vis, D_VISION), dtype=jnp.float32)
        vision_mask = jnp.ones((B, T_vis), dtype=bool)
        s = 0.02
        Wq = jax.random.normal(ks[2], (D_TEXT, N_HEADS * HEAD_DIM), dtype=jnp.float32) * s
        Wk = jax.random.normal(ks[3], (D_VISION, N_KV_HEADS * HEAD_DIM), dtype=jnp.float32) * s
        Wv = jax.random.normal(ks[4], (D_VISION, N_KV_HEADS * HEAD_DIM), dtype=jnp.float32) * s
        Wo = jax.random.normal(ks[5], (N_HEADS * HEAD_DIM, D_TEXT), dtype=jnp.float32) * s
        return {'text_hidden': text_hidden, 'vision_tokens': vision_tokens, 'vision_mask': vision_mask, 'Wq': Wq, 'Wk': Wk, 'Wv': Wv, 'Wo': Wo}
    _L1_xattn_all = _L1_xattn_setup()
    _L1_xattn_in = {k: v for k, v in _L1_xattn_all.items() if k in ('Wq', 'Wk', 'Wv', 'Wo')}
    del _L1_xattn_all

    def _L1_ffn_setup():
        import jax, jax.numpy as jnp
        import numpy as np
        HIDDEN = 256
        INTER = 1024
        MOE_INTER = 128
        N_ROUTED = 8
        NUM_LOCAL = 8
        TOP_K = 2
        B, S = (4, 256)

        def _mlp(x, gw, uw, dw):
            g = x @ gw.T
            u = x @ uw.T
            return g * jax.nn.sigmoid(g) * u @ dw.T
        key = jax.random.key(seed)
        ks = jax.random.split(key, 8)
        std = 0.02
        return {'hidden_states': jax.random.normal(ks[0], (B, S, HIDDEN), jnp.float32), 'router_weight': jax.random.normal(ks[1], (N_ROUTED, HIDDEN), jnp.float32) * std, 'sh_gate': jax.random.normal(ks[2], (INTER, HIDDEN), jnp.float32) * std, 'sh_up': jax.random.normal(ks[3], (INTER, HIDDEN), jnp.float32) * std, 'sh_down': jax.random.normal(ks[4], (HIDDEN, INTER), jnp.float32) * std, 'r_gate': jax.random.normal(ks[5], (MOE_INTER, HIDDEN), jnp.float32) * std, 'r_up': jax.random.normal(ks[6], (MOE_INTER, HIDDEN), jnp.float32) * std, 'r_down': jax.random.normal(ks[7], (HIDDEN, MOE_INTER), jnp.float32) * std}
    _L1_ffn_all = _L1_ffn_setup()
    _L1_ffn_in = {k: v for k, v in _L1_ffn_all.items() if k in ('router_weight', 'sh_gate', 'sh_up', 'sh_down', 'r_gate', 'r_up', 'r_down')}
    del _L1_ffn_all
    return {'x': x, 'fside_BxS2xS2_0': fside_BxS2xS2_0, 'ctx_1024': ctx_1024, 'mask_BxS2_bf1': mask_BxS2_bf1, 'L0_ffn_w1': _L0_ffn_in['w1'], 'L0_ffn_w2': _L0_ffn_in['w2'], 'L0_ffn_w3': _L0_ffn_in['w3'], 'L1_xattn_Wq': _L1_xattn_in['Wq'], 'L1_xattn_Wk': _L1_xattn_in['Wk'], 'L1_xattn_Wv': _L1_xattn_in['Wv'], 'L1_xattn_Wo': _L1_xattn_in['Wo'], 'L1_ffn_router_weight': _L1_ffn_in['router_weight'], 'L1_ffn_sh_gate': _L1_ffn_in['sh_gate'], 'L1_ffn_sh_up': _L1_ffn_in['sh_up'], 'L1_ffn_sh_down': _L1_ffn_in['sh_down'], 'L1_ffn_r_gate': _L1_ffn_in['r_gate'], 'L1_ffn_r_up': _L1_ffn_in['r_up'], 'L1_ffn_r_down': _L1_ffn_in['r_down']}

def reference(x, fside_BxS2xS2_0, ctx_1024, mask_BxS2_bf1, L0_ffn_w1, L0_ffn_w2, L0_ffn_w3, L1_xattn_Wq, L1_xattn_Wk, L1_xattn_Wv, L1_xattn_Wo, L1_ffn_router_weight, L1_ffn_sh_gate, L1_ffn_sh_up, L1_ffn_sh_down, L1_ffn_r_gate, L1_ffn_r_up, L1_ffn_r_down):
    import jax
    import jax.numpy as jnp

    def _L0_xattn_ref(x, gate_up_weight, down_weight):
        import jax, jax.numpy as jnp
        import numpy as np
        EPS = 1e-06
        QMAX = 127.0

        def _smooth_quant_linear(x, w):
            amax_x = jnp.max(jnp.abs(x), axis=0)
            amax_w = jnp.max(jnp.abs(w), axis=0)
            s = jnp.sqrt(jnp.maximum(amax_x, EPS) / jnp.maximum(amax_w, EPS))
            s = jnp.maximum(s, EPS)
            xs = x / s
            ws = w * s
            x_scale = jnp.maximum(jnp.max(jnp.abs(xs), axis=-1, keepdims=True), EPS) / QMAX
            w_scale = jnp.maximum(jnp.max(jnp.abs(ws), axis=-1, keepdims=True), EPS) / QMAX
            x_q = jnp.clip(jnp.round(xs / x_scale), -QMAX, QMAX)
            w_q = jnp.clip(jnp.round(ws / w_scale), -QMAX, QMAX)
            return x_q @ w_q.T * x_scale * w_scale.T

        def _expert_forward(xe, guw, dw):
            h = _smooth_quant_linear(xe, guw)
            gate, up = jnp.split(h, 2, axis=-1)
            a = jax.nn.silu(gate) * up
            return _smooth_quant_linear(a, dw)
        return jax.vmap(_expert_forward)(x, gate_up_weight, down_weight)

    def _L0_ffn_ref(x, w1, w2, w3):
        import jax, jax.numpy as jnp
        import numpy as np
        EPS = 1e-08

        def _quantize(w):
            gamma = jnp.mean(jnp.abs(w))
            return jnp.clip(jnp.round(w / (gamma + EPS)), -1.0, 1.0)

        def _bitlinear(x, w):
            return jnp.matmul(x, _quantize(w).T)
        x1 = _bitlinear(x, w1)
        x2 = _bitlinear(x, w2)
        hidden = jax.nn.sigmoid(x1) * x2
        return _bitlinear(hidden, w3)

    def _L1_xattn_ref(text_hidden, vision_tokens, vision_mask, Wq, Wk, Wv, Wo):
        import jax, jax.numpy as jnp
        import numpy as np
        N_HEADS = 16
        N_KV_HEADS = 8
        HEAD_DIM = 128
        D_TEXT = 256
        D_VISION = 128
        GROUPS = N_HEADS // N_KV_HEADS
        B, T_text, _ = text_hidden.shape
        T_vis = vision_tokens.shape[1]
        scale = jnp.float32(np.sqrt(HEAD_DIM))
        q = (text_hidden @ Wq).reshape(B, T_text, N_HEADS, HEAD_DIM).transpose(0, 2, 1, 3)
        k = (vision_tokens @ Wk).reshape(B, T_vis, N_KV_HEADS, HEAD_DIM).transpose(0, 2, 1, 3)
        v = (vision_tokens @ Wv).reshape(B, T_vis, N_KV_HEADS, HEAD_DIM).transpose(0, 2, 1, 3)
        k = jnp.repeat(k, GROUPS, axis=1)
        v = jnp.repeat(v, GROUPS, axis=1)
        scores = jnp.einsum('bhtd,bhsd->bhts', q, k) / scale
        mask = vision_mask[:, None, None, :]
        scores = jnp.where(mask, scores, -jnp.inf)
        attn = jax.nn.softmax(scores, axis=-1)
        attn = jnp.nan_to_num(attn, nan=0.0)
        out = jnp.einsum('bhts,bhsd->bhtd', attn, v)
        out = out.transpose(0, 2, 1, 3).reshape(B, T_text, N_HEADS * HEAD_DIM)
        return out @ Wo

    def _L1_ffn_ref(hidden_states, router_weight, sh_gate, sh_up, sh_down, r_gate, r_up, r_down):
        import jax, jax.numpy as jnp
        import numpy as np
        HIDDEN = 256
        INTER = 1024
        MOE_INTER = 128
        N_ROUTED = 8
        NUM_LOCAL = 8
        TOP_K = 2
        B, S = (4, 256)

        def _mlp(x, gw, uw, dw):
            g = x @ gw.T
            u = x @ uw.T
            return g * jax.nn.sigmoid(g) * u @ dw.T
        Bsz, Seq, H = hidden_states.shape
        x = hidden_states.reshape(-1, H)
        logits = x.astype(jnp.float32) @ router_weight.astype(jnp.float32).T
        topk_vals, topk_idx = jax.lax.top_k(logits, TOP_K)
        topk_w = jax.nn.softmax(topk_vals, axis=-1)
        slot_mask = (topk_idx < NUM_LOCAL).astype(topk_w.dtype)
        comb_w = jnp.sum(topk_w * slot_mask, axis=-1).astype(x.dtype)
        shared = _mlp(x, sh_gate, sh_up, sh_down)
        routed = _mlp(x, r_gate, r_up, r_down) * comb_w[:, None]
        return (shared + routed).reshape(Bsz, Seq, H)
    x = x + _L0_xattn_ref(_layernorm(x, axis=-1), fside_BxS2xS2_0, ctx_1024)
    x = x + _L0_ffn_ref(_layernorm(x, axis=-1), L0_ffn_w1, L0_ffn_w2, L0_ffn_w3)
    x = x + _L1_xattn_ref(_layernorm(x, axis=-1), ctx_1024, mask_BxS2_bf1, L1_xattn_Wq, L1_xattn_Wk, L1_xattn_Wv, L1_xattn_Wo)
    x = x + _L1_ffn_ref(_layernorm(x, axis=-1), L1_ffn_router_weight, L1_ffn_sh_gate, L1_ffn_sh_up, L1_ffn_sh_down, L1_ffn_r_gate, L1_ffn_r_up, L1_ffn_r_down)
    return x

_drawn_inputs = setup_inputs


def setup_inputs(seed=0):
    import zlib

    import numpy as np

    out = dict(_drawn_inputs(seed))
    spreads = {}
    factors = {'fside_BxS2xS2_0': 3.264,
     'ctx_1024': 3.165,
     'L1_xattn_Wq': 64.0,
     'L1_xattn_Wk': 64.0,
     'L1_xattn_Wv': 64.0,
     'L1_xattn_Wo': 64.0,
     'L1_ffn_sh_gate': 8.0,
     'L1_ffn_sh_up': 8.0,
     'L1_ffn_sh_down': 8.0,
     'L1_ffn_r_gate': 8.0,
     'L1_ffn_r_up': 8.0,
     'L1_ffn_r_down': 8.0,
     'L1_ffn_router_weight': 8.0}
    for name, (base, spread) in spreads.items():
        noise = np.random.default_rng([zlib.crc32(name.encode()), seed]).standard_normal(out[name].shape)
        drawn = base * np.exp(spread * noise) if base else spread * noise
        out[name] = jnp.asarray(drawn.astype(out[name].dtype))
    for name, factor in factors.items():
        out[name] = (out[name] * factor).astype(out[name].dtype)
    return out
```

```python
from contextlib import ExitStack

import concourse.bass as bass
from concourse import mybir

F32 = mybir.dt.float32
F32R = mybir.dt.float32r
BF16 = mybir.dt.bfloat16
U8 = mybir.dt.uint8
ALU = mybir.AluOpType
ACT = mybir.ActivationFunctionType
AX = mybir.AxisListType

P = 128
NB, T, D = 4, 256, 256
NT, ND = T // P, D // P
I = 128
H, DH = 16, 128
PAIRS = H // 2
BIT = 704
BIT_FULL = BIT // P
BIT_REST = BIT - BIT_FULL * P
BIT_CHUNKS = BIT_FULL + 1
INTER, ROUTED = 1024, 128
FFN = INTER + ROUTED
FFN_CHUNKS = FFN // P
NR = 8
LN_EPS, Q_EPS, BIT_EPS = 1e-5, 1e-6, 1e-8
QMAX = 127.0
MAGIC = 1.5 * 2.0 ** 23
MASKED = 1e30
SCALE = float(DH) ** -0.5
LINKS = 44
UNIT = 2 * FFN // 4
SLOTS = 4
ATT_UNITS = 2 * PAIRS
FFN_UNITS = 12


def build(nc, x_in, gu_in, guT_in, ctx_in, ctxT_in, mask_in, w12T_in, w3T_in, wqT_in, wkT_in,
          wvT_in, wo_in, routerT_in, gateT_in, upT_in, downT_in, out):
    with ExitStack() as ctx:
        def sb(name, shape, dt=F32, stack=ctx):
            return stack.enter_context(nc.sbuf_tensor(name, shape, dt))

        def sem(name):
            return ctx.enter_context(nc.semaphore(name))

        bank = {n: ctx.enter_context(nc.psum_tensor("bank_" + n, [P, 512], F32))
                for n in ("qa", "s0", "s1", "pt", "u", "o", "x0", "x1")}
        CHUNK_BANKS = (bank["s0"], bank["s1"], bank["pt"])
        PREP_BANKS = (bank["qa"], bank["o"])

        a_hi = sb("a_hi", [P, H, ND, P], F32R)
        a_lo = sb("a_lo", [P, H, ND, P], F32R)
        c_hi = sb("c_hi", [P, H, D], F32R)
        c_lo = sb("c_lo", [P, H, D], F32R)
        gate_hi = sb("gate_hi", [P, ND, FFN], F32R)
        gate_lo = sb("gate_lo", [P, ND, FFN], F32R)
        up_hi = sb("up_hi", [P, ND, FFN], F32R)
        up_lo = sb("up_lo", [P, ND, FFN], F32R)
        down_hi = sb("down_hi", [P, FFN_CHUNKS, D], F32R)
        down_lo = sb("down_lo", [P, FFN_CHUNKS, D], F32R)
        router_raw = sb("router_raw", [P, ND, NR])
        router_hi = sb("router_hi", [P, ND, NR], F32R)
        router_lo = sb("router_lo", [P, ND, NR], F32R)
        w12 = sb("w12", [P, ND, 2 * BIT], F32R)
        w3 = sb("w3", [P, BIT_CHUNKS, D], F32R)

        ident = sb("ident", [P, P])
        ones = sb("ones", [P, P])
        half_exp = sb("half_exp", [P, 2, 2])
        x = sb("x", [P, NB, NT, D])
        mask8 = sb("mask8", [P, T], U8)
        valid_b = sb("valid_b", [P, 1])
        masked = sb("masked", [P, T])
        ln_stats = sb("ln_stats", [P, NT, 6])
        ln_mv = sb("ln_mv", [P, NT, 2])
        ln_ve = sb("ln_ve", [P, NT])
        ln_rstd = sb("ln_rstd", [P, NT])
        xn = sb("xn", [P, NT, D])
        xt_hi = sb("xt_hi", [P, ND, T], F32R)
        xt_lo = sb("xt_lo", [P, ND, T], F32R)
        gu = sb("gu", [P, 2, D])
        guT = sb("guT", [P, ND, 2 * I])
        cx = sb("cx", [P, 2, I])
        cxT = sb("cxT", [P, T])
        qw = sb("qw", [P, 4, D])
        dg = sb("dg", [P, 4, P])
        amax = sb("amax", [P, 4])
        ratio = sb("ratio", [P, 2])
        sroot = sb("sroot", [P, 2])
        sis = sb("sis", [P, 4])
        rowmax = sb("rowmax", [P, 4])
        qscale = sb("qscale", [P, 2, 4])
        qrecip = sb("qrecip", [P, 4])
        qT = sb("qT", [P, 4, D], BF16)
        wscale = sb("wscale", [P, D])
        hs = sb("hs", [P, NT, D])
        act1 = hs[:, :, I:2 * I]
        cx_hi = sb("cx_hi", [P, 2, I], F32R)
        cx_lo = sb("cx_lo", [P, 2, I], F32R)
        cxT_hi = sb("cxT_hi", [P, T], F32R)
        cxT_lo = sb("cxT_lo", [P, T], F32R)
        row_min = sb("row_min", [P, 2, NT])
        row_sum = sb("row_sum", [P, 2, NT])
        row_inv = sb("row_inv", [P, 2, NT])
        gsum = sb("gsum", [P, 4])
        gam = sb("gam", [P, 4])
        top8 = sb("top8", [P, NT, NR])
        top_d = sb("top_d", [P, NT, 2])
        top_w = sb("top_w", [P, NT, 2])
        comb = sb("comb", [P, NT])

        with ExitStack() as first:
            stream = sb("stream", [P, SLOTS, UNIT], F32, first)
            w12_raw = sb("w12_raw", [P, ND, 2 * BIT], F32, first)
            w3_raw = sb("w3_raw", [P, BIT_CHUNKS, D], F32, first)
            wkT = sb("wkT", [P, PAIRS, P], F32, first)
            wvT = sb("wvT", [P, PAIRS, P], F32, first)
        qa_hi = sb("qa_hi", [P, 2, 2 * T], F32R)
        qa_lo = sb("qa_lo", [P, 2, 2 * T], F32R)
        ut_hi = sb("ut_hi", [P, T], F32R)
        prob = sb("prob", [P, 2, NT, T])
        act_raw = sb("act_raw", [P, 3, T])
        act_hi = sb("act_hi", [P, 3, T], F32R)
        act_lo = sb("act_lo", [P, 3, T], F32R)
        sig = sb("sig", [P, 3, T])
        pt_hi = sb("pt_hi", [P, 2, T], F32R)
        pt_lo = sb("pt_lo", [P, 2, T], F32R)
        yt_hi = sb("yt_hi", [P, ND, T], F32R)
        yt_lo = sb("yt_lo", [P, ND, T], F32R)
        ut_lo = sb("ut_lo", [P, T], F32R)

        S = {}
        for n in """consts x0_in x_in mask_in gu_in cx_in w12_in w3_in wk_in router_in out_done
                    abs_done gamma_mm bit_q w12_ready w3_ready
                    prep_mm prep_hi prep_lo stream_hi stream_lo router_ready
                    lnq_ve lnq_pow lnq_xn lnb_ve lnb_pow lnb_xn lna_ve lna_pow lna_xn lnf_ve lnf_pow lnf_xn
                    lnb_t lnb_hi lnb_lo lna_t lna_hi lna_lo lnf_t lnf_hi lnf_lo
                    q_xt q_ratio q_root q_diag q_spread q_rounded q_turned q_bf q_prod q_wscale q_hs
                    q_exp q_gu q_act dve_self
                    bit_mm bit_sig bit_prod bit_hi bit_lo bit_y bit_x
                    ctx_hi ctx_lo mask_row
                    qa_mm qa_h qa_l s_mm s_min s_exp s_inv s_norm t_mm t_h t_l u_mm u_h u_l o_mm
                    att_x route_mm route_d route_sig route_w
                    ffn_mm ffn_sig ffn_prod ffn_hi ffn_lo ffn_y ffn_x""".split():
            S[n] = sem(n)
        for i in range(SLOTS):
            S[f"slot{i}"] = sem(f"slot{i}_in")

        def f32(ap):
            return ap.bitcast(F32)

        def unit_source(k):
            if k < ATT_UNITS:
                p, which = k // 2, k % 2
                src = (wqT_in, wo_in)[which].rearrange("(h p) d -> p h d", p=P)[:, 2 * p:2 * p + 2, :]
                return src, stream[:, k % SLOTS, 0:2 * D].rearrange("p (h d) -> p h d", h=2)
            k2 = k - ATT_UNITS
            which, part = k2 // 4, k2 % 4
            slot = stream[:, k % SLOTS, :]
            if which < 2:
                c = FFN // 4
                src = (gateT_in, upT_in)[which].rearrange("(k p) n -> p k n", p=P)
                return src[:, :, part * c:(part + 1) * c], slot.rearrange("p (k n) -> p k n", k=ND)
            src = downT_in.rearrange("(p c) d -> p (c d)", p=P)
            return src[:, part * UNIT:(part + 1) * UNIT], slot

        def unit_target(k, tensors):
            k2 = k - ATT_UNITS
            which, part = k2 // 4, k2 % 4
            slot = stream[:, k % SLOTS, :]
            if which < 2:
                c = FFN // 4
                return tensors[which][:, :, part * c:(part + 1) * c], slot.rearrange("p (k n) -> p k n", k=ND)
            flat = tensors[2][:, :, :].rearrange("p c d -> p (c d)")
            return flat[:, part * UNIT:(part + 1) * UNIT], slot

        block = ctx.enter_context(nc.Block())

        @block.sync
        def _(sp):
            def expert_weights(b):
                if not (isinstance(b, int) and b == 0):
                    sp.wait_ge(S["q_rounded"], 2 * b)
                    sp.wait_ge(S["ctx_lo"], b)
                sp.dma_start(gu[:, :, :], gu_in[b].rearrange("(o p) d -> p o d", p=P)).then_inc(S["gu_in"], 16)
                sp.dma_start(guT[:, :, :], guT_in[b].rearrange("(k p) o -> p k o", p=P)).then_inc(S["gu_in"], 16)
                sp.dma_start(cx[:, :, :], ctx_in[b].rearrange("(o p) d -> p o d", p=P)).then_inc(S["cx_in"], 16)
                sp.dma_start(cxT[:, :], ctxT_in[b]).then_inc(S["cx_in"], 16)
                sp.dma_start(mask8[:, :], mask_in[b].partition_broadcast(P)).then_inc(S["mask_in"], 16)

            def x_rows(dram, b):
                return dram[b].rearrange("(t p) d -> p t d", p=P)

            def store(b):
                sp.wait_ge(S["ffn_x"], b + 1)
                sp.dma_start(x_rows(out, b), x[:, b, :, :]).then_inc(S["out_done"], 16)

            sp.dma_start(x[:, 0, :, :], x_rows(x_in, 0)).then_inc(S["x0_in"], 16)
            expert_weights(0)
            sp.dma_start(w12_raw[:, :, :], w12T_in.rearrange("(k p) n -> p k n", p=P)).then_inc(S["w12_in"], 16)
            sp.dma_start(w3_raw[:, 0:BIT_FULL, :], w3T_in[0:BIT_FULL * P].rearrange("(c p) d -> p c d", p=P)
                         ).then_inc(S["w3_in"], 16)
            sp.dma_start(w3_raw[0:BIT_REST, BIT_FULL, :], w3T_in[BIT_FULL * P:BIT]).then_inc(S["w3_in"], 16)
            sp.dma_start(wkT[:, :, :], wkT_in.rearrange("(g p) d -> p g d", p=P)).then_inc(S["wk_in"], 16)
            sp.dma_start(wvT[:, :, :], wvT_in.rearrange("(g p) d -> p g d", p=P)).then_inc(S["wk_in"], 16)
            for k in range(ATT_UNITS + FFN_UNITS):
                if k >= SLOTS:
                    old = k - SLOTS
                    if old < ATT_UNITS:
                        sp.wait_ge(S["prep_mm"], old + 1)
                    else:
                        sp.wait_ge(S["stream_lo"], old - ATT_UNITS + 1)
                src, dst = unit_source(k)
                sp.dma_start(dst, src).then_inc(S[f"slot{k % SLOTS}"], 16)
                if k == SLOTS - 1:
                    sp.dma_start(router_raw[:, :, :], routerT_in.rearrange("(k p) n -> p k n", p=P)
                                 ).then_inc(S["router_in"], 16)
                    for b in range(1, NB):
                        sp.dma_start(x[:, b, :, :], x_rows(x_in, b)).then_inc(S["x_in"], 16)
            with sp.Fori(0, NB - 1) as b:
                expert_weights(b + 1)
                store(b)
            store(NB - 1)
            sp.wait_ge(S["out_done"], 16 * NB)

        @block.tensor
        def _(pe):
            def split_mm(out_ap, w_hi, w_lo, r_hi, r_lo, start, stop):
                passes = [(w_hi, r_hi), (w_hi, r_lo), (w_lo, r_hi)]
                passes = [(w, r) for w, r in passes if w is not None and r is not None]
                for n, (w, r) in enumerate(passes):
                    last = pe.matmul(out_ap, w, r, start=start and n == 0, stop=stop and n == len(passes) - 1,
                                     skip_group_check=True)
                return last

            def turn_xn(dst):
                for t in range(NT):
                    for k in range(ND):
                        last = pe.transpose(dst[:, k * T + t * P:k * T + (t + 1) * P],
                                            xn[:, t, k * P:(k + 1) * P], ident[:, :])
                return last

            def q_turn_x(b):
                pe.wait_ge(S["lnq_xn"], b + 1)
                turn_xn(bank["x0"]).then_inc(S["q_xt"], 1)

            def q_spread(b, s):
                pe.wait_ge(S["q_diag"], 4 * b + 2 * s + 1)
                w = 512 if s == 0 else 256
                dst = bank["x0"] if s == 0 else bank["x1"]
                pe.matmul(dst[:, 0:w], ones[:, :], dg[:, 0:w // P, :].rearrange("p a c -> p (a c)"),
                          start=True, stop=True).then_inc(S["q_spread"], 1)

            def q_turn_rounded(b, s):
                pe.wait_ge(S["q_rounded"], 2 * b + s + 1)
                if s == 0:
                    for j in range(4):
                        dst = bank["x0"] if j < 2 else bank["x1"]
                        for k in range(ND):
                            last = pe.transpose(dst[:, k * 256 + (j % 2) * P:k * 256 + (j % 2 + 1) * P],
                                                qw[:, j, k * P:(k + 1) * P], ident[:, :])
                else:
                    for j in range(4):
                        last = pe.transpose(bank["x0"][:, j * P:(j + 1) * P], qw[:, j, 0:I], ident[:, :])
                last.then_inc(S["q_turned"], 1)

            def q_product(b, s):
                pe.wait_ge(S["q_bf"], 2 * b + s + 1)
                for t in range(NT):
                    if s == 0:
                        for k in range(ND):
                            last = pe.matmul(bank["x0"][:, t * D:(t + 1) * D], qT[:, k, t * P:(t + 1) * P],
                                             qT[:, 2 + k, :], start=(k == 0), stop=(k == ND - 1))
                    else:
                        last = pe.matmul(bank["x0"][:, t * D:(t + 1) * D], qT[:, 0, t * P:(t + 1) * P],
                                         qT[:, 1, :], start=True, stop=True)
                pe.wait_ge(S["q_diag"], 4 * b + 2 * s + 2)
                pe.matmul(bank["x1"][:, 0:D], ones[:, :], dg[:, 2:4, :].rearrange("p a c -> p (a c)"),
                          start=True, stop=True).then_inc(S["q_prod"], 1)

            def q_turn_act(b):
                pe.wait_ge(S["q_act"], b + 1)
                for t in range(NT):
                    last = pe.transpose(bank["x0"][:, t * P:(t + 1) * P], act1[:, t, :], ident[:, :])
                last.then_inc(S["q_xt"], 1)

            def q_piece(n, b):
                if n == 0:
                    q_turn_x(b)
                elif n == 1:
                    q_spread(b, 0)
                elif n == 2:
                    q_turn_rounded(b, 0)
                elif n == 3:
                    q_product(b, 0)
                elif n == 4:
                    q_turn_act(b)
                elif n == 5:
                    q_spread(b, 1)
                elif n == 6:
                    q_turn_rounded(b, 1)
                elif n == 7:
                    q_product(b, 1)

            def bit_up(b, c):
                if c >= 3:
                    pe.wait_ge(S["bit_prod"], BIT_CHUNKS * b + c - 2)
                dst = CHUNK_BANKS[c % 3]
                if c < BIT_FULL:
                    sides = ((0, c * P), (T, BIT + BIT_REST + c * P))
                else:
                    sides = ((0, BIT_FULL * P),)
                first = True
                for at, col in sides:
                    for k in range(ND):
                        w = w12[:, k, col:col + P]
                        last = split_mm(dst[:, at:at + T], w, None, xt_hi[:, k, :], xt_lo[:, k, :], first, k == ND - 1)
                        first = False
                last.then_inc(S["bit_mm"], 1)

            def bit_down(b, c):
                pe.wait_ge(S["bit_hi"], BIT_CHUNKS * b + c + 1)
                pe.wait_ge(S["bit_lo"], BIT_CHUNKS * b + c + 1)
                rows = P if c < BIT_FULL else BIT_REST
                for t in range(NT):
                    for half in (act_hi, act_lo):
                        last = pe.matmul(bank["u"][:, t * D:(t + 1) * D], half[0:rows, c % 3, t * P:(t + 1) * P],
                                         w3[0:rows, c, :], start=(c == 0 and t == 0 and half is act_hi),
                                         stop=(c == BIT_CHUNKS - 1), skip_group_check=True)
                last.then_inc(S["bit_y"], 1)

            def bit_turn(b):
                pe.wait_ge(S["lnb_xn"], b + 1)
                turn_xn(bank["x0"]).then_inc(S["lnb_t"], 1)

            def bit_layer(b, between=None):
                pe.wait_ge(S["lnb_hi"], b + 1)
                pe.wait_ge(S["lnb_lo"], b + 1)
                for c in range(BIT_CHUNKS + 2):
                    if c < BIT_CHUNKS:
                        bit_up(b, c)
                    if c >= 2:
                        bit_down(b, c - 2)
                    if between is not None:
                        between(c)

            def att_turn(b):
                pe.wait_ge(S["lna_xn"], b + 1)
                turn_xn(bank["x0"]).then_inc(S["lna_t"], 1)

            def queries(b, h):
                p = h // 2
                if h % 2 == 0 and p >= 1:
                    pe.wait_ge(S["qa_l"], PAIRS * b + p)
                dst = bank["qa"][:, (h % 2) * T:(h % 2 + 1) * T]
                for k in range(ND):
                    last = split_mm(dst, a_hi[:, h, k, :], a_lo[:, h, k, :], xt_hi[:, k, :], xt_lo[:, k, :],
                                    k == 0, k == ND - 1)
                if h % 2 == 1:
                    last.then_inc(S["qa_mm"], 1)

            def scores(b, h):
                pe.wait_ge(S["qa_l"], PAIRS * b + h // 2 + 1)
                if h >= 2:
                    pe.wait_ge(S["s_min"], H * b + h - 1)
                dst = bank["s0"] if h % 2 == 0 else bank["s1"]
                ring, col = (h // 2) % 2, (h % 2) * T
                for t in range(NT):
                    cols = slice(col + t * P, col + (t + 1) * P)
                    last = split_mm(dst[:, t * T:(t + 1) * T], qa_hi[:, ring, cols], qa_lo[:, ring, cols],
                                    cxT_hi[:, :], cxT_lo[:, :], True, True)
                last.then_inc(S["s_mm"], 1)

            def turn_probs(b, h):
                pe.wait_ge(S["s_norm"], H * b + h + 1)
                if h >= 1:
                    pe.wait_ge(S["t_l"], H * b + h)
                for t in range(NT):
                    for s in range(2):
                        last = pe.transpose(bank["pt"][:, s * T + t * P:s * T + (t + 1) * P],
                                            prob[:, h % 2, t, s * P:(s + 1) * P], ident[:, :])
                last.then_inc(S["t_mm"], 1)

            def mix(b, h):
                pe.wait_ge(S["t_l"], H * b + h + 1)
                if h >= 1:
                    pe.wait_ge(S["u_l"], H * b + h)
                for s in range(2):
                    last = split_mm(bank["u"][:, 0:T], cx_hi[:, s, :], cx_lo[:, s, :], pt_hi[:, s, :],
                                    pt_lo[:, s, :], s == 0, s == 1)
                last.then_inc(S["u_mm"], 1)

            def project(b, h):
                pe.wait_ge(S["u_l"], H * b + h + 1)
                for t in range(NT):
                    cols = slice(t * P, (t + 1) * P)
                    last = split_mm(bank["o"][:, t * D:(t + 1) * D], ut_hi[:, cols], ut_lo[:, cols],
                                    c_hi[:, h, :], c_lo[:, h, :], h == 0 and t == 0, h == H - 1)
                last.then_inc(S["o_mm"], 1)

            def attention(b, beside=None):
                for h in range(H):
                    turn_probs(b, h)
                    if h + 4 < H:
                        queries(b, h + 4)
                    if h + 2 < H:
                        scores(b, h + 2)
                    if h >= 1:
                        project(b, h - 1)
                    mix(b, h)
                    if beside is not None:
                        beside(h)

            def ffn_turn(b):
                pe.wait_ge(S["lnf_xn"], b + 1)
                turn_xn(bank["x0"]).then_inc(S["lnf_t"], 1)

            def route(b):
                pe.wait_ge(S["lnf_hi"], b + 1)
                pe.wait_ge(S["lnf_lo"], b + 1)
                for t in range(NT):
                    for k in range(ND):
                        cols = slice(t * P, (t + 1) * P)
                        last = split_mm(bank["x1"][:, t * NR:(t + 1) * NR], yt_hi[:, k, cols], yt_lo[:, k, cols],
                                        router_hi[:, k, :], router_lo[:, k, :], k == 0, k == ND - 1)
                last.then_inc(S["route_mm"], 1)

            def ffn_up(b, c):
                if c >= 3:
                    pe.wait_ge(S["ffn_prod"], FFN_CHUNKS * b + c - 2)
                dst = CHUNK_BANKS[c % 3]
                first = True
                for at, w_hi, w_lo in ((0, gate_hi, gate_lo), (T, up_hi, up_lo)):
                    for k in range(ND):
                        cols = slice(c * P, (c + 1) * P)
                        last = split_mm(dst[:, at:at + T], w_hi[:, k, cols], w_lo[:, k, cols], yt_hi[:, k, :],
                                        yt_lo[:, k, :], first, k == ND - 1)
                        first = False
                last.then_inc(S["ffn_mm"], 1)

            def ffn_down(b, c):
                pe.wait_ge(S["ffn_hi"], FFN_CHUNKS * b + c + 1)
                pe.wait_ge(S["ffn_lo"], FFN_CHUNKS * b + c + 1)
                routed = c == FFN_CHUNKS - 1
                dst = bank["o"] if routed else bank["u"]
                for t in range(NT):
                    cols = slice(t * P, (t + 1) * P)
                    last = split_mm(dst[:, t * D:(t + 1) * D], act_hi[:, c % 3, cols], act_lo[:, c % 3, cols],
                                    down_hi[:, c, :], down_lo[:, c, :], t == 0 and (c == 0 or routed),
                                    c >= FFN_CHUNKS - 2)
                last.then_inc(S["ffn_y"], 1)

            def ffn_layer(b, last):
                route(b)
                for c in range(FFN_CHUNKS + 2):
                    if c < FFN_CHUNKS:
                        ffn_up(b, c)
                    if not last and c == FFN_CHUNKS:
                        pe.wait_ge(S["ffn_prod"], FFN_CHUNKS * b + FFN_CHUNKS - 2)
                        pe.wait_ge(S["ctx_lo"], b + 2)
                        scores(b + 1, 0)
                    if not last and c == FFN_CHUNKS + 1:
                        pe.wait_ge(S["ffn_prod"], FFN_CHUNKS * b + FFN_CHUNKS - 1)
                        scores(b + 1, 1)
                    if c == 2 and not last:
                        pe.wait_ge(S["bit_x"], b + 2)
                    if c >= 2:
                        ffn_down(b, c - 2)
                    if not last and c == 2:
                        att_turn(b + 1)
                    if not last and c in (5, 6):
                        if c == 5:
                            pe.wait_ge(S["lna_hi"], b + 2)
                            pe.wait_ge(S["lna_lo"], b + 2)
                        queries(b + 1, 2 * (c - 5))
                        queries(b + 1, 2 * (c - 5) + 1)

            Q_STEPS = {1: 0, 3: 1, 5: 2, 6: 3, 8: 4, 10: 5, 11: 6, 12: 7}

            def batch(b, last):
                def beside(h):
                    if h in Q_STEPS:
                        q_piece(Q_STEPS[h], b + 1)
                    if h == 14:
                        bit_turn(b + 1)
                attention(b, None if last else beside)
                project(b, H - 1)
                if not last:
                    bit_layer(b + 1, lambda c: ffn_turn(b) if c == 3 else None)
                else:
                    ffn_turn(b)
                ffn_layer(b, last)

            def prep_unit(k):
                p = k // 2
                pe.wait_ge(S[f"slot{k % SLOTS}"], 16 * (k // SLOTS + 1))
                if k >= 2:
                    pe.wait_ge(S["prep_lo"], k - 1)
                dst = PREP_BANKS[k % 2]
                for j in range(2):
                    raw = stream[:, k % SLOTS, j * D:(j + 1) * D]
                    if k % 2 == 0:
                        for s in range(ND):
                            last = pe.matmul(dst[:, (j * ND + s) * P:(j * ND + s + 1) * P],
                                             raw[:, s * P:(s + 1) * P], wkT[:, p, :], start=True, stop=True)
                    else:
                        last = pe.matmul(dst[:, j * D:(j + 1) * D], wvT[:, p, :], raw, start=True, stop=True)
                last.then_inc(S["prep_mm"], 1)

            pe.wait_ge(S["consts"], 2)
            for n in range(3):
                q_piece(n, 0)
            pe.wait_ge(S["abs_done"], 4)
            pe.matmul(bank["u"][:, 0:4], ones[:, :], gsum[:, :], start=True, stop=True).then_inc(S["gamma_mm"], 1)
            q_piece(3, 0)
            pe.wait_ge(S["wk_in"], 32)
            for n in range(4, 8):
                prep_unit(2 * n - 8)
                prep_unit(2 * n - 7)
                q_piece(n, 0)
            for k in range(8, 12):
                prep_unit(k)
            bit_turn(0)
            for k in range(12, ATT_UNITS):
                prep_unit(k)
            pe.wait_ge(S["w12_ready"], 1)
            pe.wait_ge(S["w3_ready"], 2)
            bit_layer(0)
            att_turn(0)
            pe.wait_ge(S["router_ready"], 2)
            pe.wait_ge(S["stream_lo"], FFN_UNITS)
            pe.wait_ge(S["lna_hi"], 1)
            pe.wait_ge(S["lna_lo"], 1)
            for h in range(4):
                queries(0, h)
            pe.wait_ge(S["ctx_hi"], 1)
            pe.wait_ge(S["ctx_lo"], 1)
            scores(0, 0)
            scores(0, 1)
            with pe.Fori(0, NB - 1) as b:
                batch(b, False)
            batch(NB - 1, True)

        @block.scalar
        def _(act):
            def split_hi(dst, src, done, scale=1.0):
                act.activation(dst, src, ACT.Copy, scale=scale).then_inc(done, 1)

            def ln_hi(b, kind, dst):
                act.wait_ge(S[kind + "_t"], b + 1)
                split_hi(dst[:, :, :].rearrange("p k t -> p (k t)"), bank["x0"][:, :], S[kind + "_hi"])

            def q_exp(b):
                act.wait_ge(S["q_hs"], b + 1)
                act.activation(qw[:, 0:NT, 0:I], hs[:, :, 0:I], ACT.Exp, scale=-1.0).then_inc(S["q_exp"], 1)

            def q_bf(b, s):
                act.wait_ge(S["q_turned"], 2 * b + s + 1)
                flat = qT[:, :, :].rearrange("p a n -> p (a n)")
                if s == 0:
                    act.activation(flat[:, 0:512], bank["x0"][:, :], ACT.Copy, bias=-MAGIC)
                    act.activation(flat[:, 512:1024], bank["x1"][:, :], ACT.Copy, bias=-MAGIC
                                   ).then_inc(S["q_bf"], 1)
                else:
                    act.activation(flat[:, 0:512], bank["x0"][:, :], ACT.Copy, bias=-MAGIC
                                   ).then_inc(S["q_bf"], 1)

            def q_wscale(b, s):
                act.wait_ge(S["q_prod"], 2 * b + s + 1)
                act.copy(wscale[:, :], bank["x1"][:, 0:D]).then_inc(S["q_wscale"], 1)

            def ctx_split_hi(b):
                act.wait_ge(S["cx_in"], 32 * (b + 1))
                act.copy(cx_hi[:, :, :], cx[:, :, :])
                act.copy(cxT_hi[:, :], cxT[:, :]).then_inc(S["ctx_hi"], 1)

            def queries_hi(b, p):
                act.wait_ge(S["qa_mm"], PAIRS * b + p + 1)
                split_hi(qa_hi[:, p % 2, :], bank["qa"][:, :], S["qa_h"])

            def exps(b, h):
                act.wait_ge(S["s_min"], H * b + h + 1)
                for t in range(NT):
                    row = prob[:, h % 2, t, :]
                    last = act.activation(row, row, ACT.Exp, scale=-1.0, bias=row_min[:, h % 2, t:t + 1],
                                          accum_out=row_sum[:, h % 2, t:t + 1])
                last.then_inc(S["s_exp"], 1)

            def probs_hi(b, h):
                act.wait_ge(S["t_mm"], H * b + h + 1)
                split_hi(pt_hi[:, :, :].rearrange("p s t -> p (s t)"), bank["pt"][:, :], S["t_h"])

            def mix_hi(b, h):
                act.wait_ge(S["u_mm"], H * b + h + 1)
                split_hi(ut_hi[:, :], bank["u"][:, 0:T], S["u_h"])

            def attention(b, last):
                for h in range(H):
                    if not last and h == 7:
                        q_wscale(b + 1, 0)
                    if not last and h == 13:
                        q_wscale(b + 1, 1)
                    if not last and h == 15:
                        ln_hi(b + 1, "lnb", xt_hi)
                    if h >= 1:
                        mix_hi(b, h - 1)
                    probs_hi(b, h)
                    if h % 2 == 1 and h + 3 < H:
                        queries_hi(b, (h + 3) // 2)
                    if h + 2 < H:
                        exps(b, h + 2)
                    if not last and h == 6:
                        q_bf(b + 1, 0)
                    if not last and h == 7:
                        q_exp(b + 1)
                    if not last and h == 12:
                        q_bf(b + 1, 1)

            def bit_sig(b, c):
                act.wait_ge(S["bit_mm"], BIT_CHUNKS * b + c + 1)
                src = CHUNK_BANKS[c % 3]
                if c < BIT_FULL:
                    act.activation(sig[:, c % 3, :], src[:, 0:T], ACT.Sigmoid).then_inc(S["bit_sig"], 1)
                else:
                    act.activation(sig[BIT_REST:P, c % 3, :], src[0:BIT_REST, 0:T], ACT.Sigmoid
                                   ).then_inc(S["bit_sig"], 1)

            def ffn_sig(b, c):
                act.wait_ge(S["ffn_mm"], FFN_CHUNKS * b + c + 1)
                act.activation(sig[:, c % 3, :], CHUNK_BANKS[c % 3][:, 0:T], ACT.Sigmoid).then_inc(S["ffn_sig"], 1)


            def batch(b, last):
                attention(b, last)
                mix_hi(b, H - 1)
                if not last:
                    for c in range(4):
                        bit_sig(b + 1, c)
                        if c == 1:
                            ctx_split_hi(b + 1)
                ln_hi(b, "lnf", yt_hi)
                if not last:
                    for c in range(4, BIT_CHUNKS):
                        bit_sig(b + 1, c)
                for c in range(FFN_CHUNKS):
                    ffn_sig(b, c)
                    if c == 1:
                        act.wait_ge(S["route_d"], b + 1)
                        act.activation(top_w[:, :, :], top_d[:, :, :], ACT.Sigmoid).then_inc(S["route_sig"], 1)
                    if not last:
                        if c == 3:
                            ln_hi(b + 1, "lna", xt_hi)
                        if c == 5:
                            queries_hi(b + 1, 0)
                        if c == 6:
                            queries_hi(b + 1, 1)
                if not last:
                    exps(b + 1, 0)
                    exps(b + 1, 1)

            act.wait_ge(S["consts"], 2)
            act.wait_ge(S["w12_in"], 16)
            for j in range(2):
                act.activation(w12[:, :, j * BIT:(j + 1) * BIT], w12_raw[:, :, j * BIT:(j + 1) * BIT],
                               ACT.Abs, accum_out=gsum[:, j:j + 1]).then_inc(S["abs_done"], 1)
            act.wait_ge(S["w3_in"], 32)
            act.activation(w3[:, 0:BIT_FULL, :], w3_raw[:, 0:BIT_FULL, :],
                           ACT.Abs, accum_out=gsum[:, 2:3]).then_inc(S["abs_done"], 1)
            act.activation(w3[0:BIT_REST, BIT_FULL, :], w3_raw[0:BIT_REST, BIT_FULL, :],
                           ACT.Abs, accum_out=gsum[0:BIT_REST, 3:4]).then_inc(S["abs_done"], 1)

            def prep_hi(k):
                act.wait_ge(S["prep_mm"], k + 1)
                dst = (a_hi[:, 2 * (k // 2):2 * (k // 2) + 2, :, :].rearrange("p h s c -> p (h s c)") if k % 2 == 0 else
                       c_hi[:, 2 * (k // 2):2 * (k // 2) + 2, :].rearrange("p h d -> p (h d)"))
                split_hi(dst, PREP_BANKS[k % 2][:, :], S["prep_hi"], scale=-SCALE if k % 2 == 0 else 1.0)

            q_bf(0, 0)
            q_wscale(0, 0)
            q_exp(0)
            act.wait_ge(S["bit_q"], 1)
            act.activation(w12[:, :, :], w12_raw[:, :, :], ACT.Copy, bias=-MAGIC).then_inc(S["w12_ready"], 1)
            act.wait_ge(S["bit_q"], 3)
            act.activation(w3[:, 0:BIT_FULL, :], w3_raw[:, 0:BIT_FULL, :], ACT.Copy, bias=-MAGIC
                           ).then_inc(S["w3_ready"], 1)
            act.activation(w3[0:BIT_REST, BIT_FULL, :], w3_raw[0:BIT_REST, BIT_FULL, :], ACT.Copy,
                           bias=-MAGIC).then_inc(S["w3_ready"], 1)
            for k in range(6):
                prep_hi(k)
            q_bf(0, 1)
            prep_hi(6)
            prep_hi(7)
            q_wscale(0, 1)
            for k in range(8, 12):
                prep_hi(k)
            ln_hi(0, "lnb", xt_hi)
            for k in range(12, ATT_UNITS):
                prep_hi(k)
            for c in range(BIT_CHUNKS):
                bit_sig(0, c)
            ctx_split_hi(0)
            act.wait_ge(S["router_in"], 16)
            act.copy(router_hi[:, :, :], router_raw[:, :, :]).then_inc(S["router_ready"], 1)
            for k in range(ATT_UNITS, ATT_UNITS + FFN_UNITS):
                act.wait_ge(S[f"slot{k % SLOTS}"], 16 * (k // SLOTS + 1))
                dst, raw = unit_target(k, (gate_hi, up_hi, down_hi))
                act.copy(dst, raw).then_inc(S["stream_hi"], 1)
            ln_hi(0, "lna", xt_hi)
            queries_hi(0, 0)
            queries_hi(0, 1)
            exps(0, 0)
            exps(0, 1)
            with act.Fori(0, NB - 1) as b:
                batch(b, False)
            batch(NB - 1, True)

        @block.gpsimd
        def _(pool):
            def power(b, kind):
                pool.wait_ge(S[kind + "_ve"], b + 1)
                pool.tensor_tensor(ln_rstd[:, :], ln_ve[:, :], half_exp[:, 0, :], ALU.pow
                                   ).then_inc(S[kind + "_pow"], 1)

            def q_root(b, s):
                pool.wait_ge(S["q_ratio"], 2 * b + s + 1)
                n = ND if s == 0 else 1
                pool.tensor_tensor(sroot[:, 0:n], ratio[:, 0:n], half_exp[:, 1, 0:n], ALU.pow
                                   ).then_inc(S["q_root"], 1)

            def q_gate_up(b):
                pool.wait_ge(S["q_hs"], b + 1)
                pool.tensor_tensor(act1[:, :, :], hs[:, :, 0:I], hs[:, :, I:2 * I], ALU.mult).then_inc(S["q_gu"], 1)

            def normalise(b, h):
                pool.wait_ge(S["s_inv"], H * b + h + 1)
                pool.nop(nofuse=True)
                for t in range(NT):
                    row = prob[:, h % 2, t, :]
                    last = pool.tensor_scalar(row, row, row_inv[:, h % 2, t:t + 1], valid_b[:, 0:1],
                                              ALU.mult, ALU.mult)
                last.then_inc(S["s_norm"], 1)

            def bit_low(b, c):
                pool.wait_ge(S["bit_hi"], BIT_CHUNKS * b + c + 1)
                rows = P if c < BIT_FULL else BIT_REST
                pool.tensor_tensor(act_lo[0:rows, c % 3, :], act_raw[0:rows, c % 3, :],
                                   f32(act_hi[0:rows, c % 3, :]), ALU.subtract).then_inc(S["bit_lo"], 1)

            def ffn_low(b, c):
                pool.wait_ge(S["ffn_hi"], FFN_CHUNKS * b + c + 1)
                pool.tensor_tensor(act_lo[:, c % 3, :], act_raw[:, c % 3, :], f32(act_hi[:, c % 3, :]),
                                   ALU.subtract).then_inc(S["ffn_lo"], 1)

            def batch(b, last):
                for h in range(H):
                    if h + 1 < H:
                        normalise(b, h + 1)
                    if last:
                        continue
                    if h == 0:
                        power(b + 1, "lnq")
                    if h == 2:
                        q_root(b + 1, 0)
                    if h == 7:
                        q_gate_up(b + 1)
                    if h == 9:
                        q_root(b + 1, 1)
                    if h == 13:
                        power(b + 1, "lnb")
                power(b, "lnf")
                if not last:
                    for c in range(BIT_CHUNKS):
                        bit_low(b + 1, c)
                    power(b + 1, "lna")
                for c in range(FFN_CHUNKS):
                    ffn_low(b, c)
                if not last:
                    normalise(b + 1, 0)

            pool.memset(ones[:, :], 1.0).then_inc(S["consts"], 1)
            pool.memset(gsum[:, :], 0.0)
            pool.memset(half_exp[:, 0, :], -0.5)
            pool.memset(half_exp[:, 1, :], 0.5)
            pool.wait_ge(S["consts"], 1)
            pool.affine_select(out=ident[:, :], in_=ones[:, :], compare_op=ALU.is_equal, fill=0.0, base=0,
                               pattern=[[-1, P]], channel_multiplier=1).then_inc(S["consts"], 1)
            pool.wait_ge(S["consts"], 2)
            power(0, "lnq")
            q_root(0, 0)
            q_gate_up(0)
            q_root(0, 1)
            power(0, "lnb")
            for c in range(BIT_CHUNKS):
                bit_low(0, c)
            for k in range(ATT_UNITS, ATT_UNITS + FFN_UNITS):
                pool.wait_ge(S["stream_hi"], k - ATT_UNITS + 1)
                dst, raw = unit_target(k, (gate_lo, up_lo, down_lo))
                hi, _ = unit_target(k, (gate_hi, up_hi, down_hi))
                pool.tensor_tensor(dst, raw, f32(hi), ALU.subtract).then_inc(S["stream_lo"], 1)
                if k == ATT_UNITS + 1:
                    power(0, "lna")
            normalise(0, 0)
            with pool.Fori(0, NB - 1) as b:
                batch(b, False)
            batch(NB - 1, True)

        @block.vector
        def _(dve):
            links = {"base": 0, "n": 0}

            def link(ins):
                links["n"] += 1
                ins.then_inc(S["dve_self"], 1)
                dve.wait_ge(S["dve_self"], links["base"] + links["n"])

            def hold():
                dve.nop(nofuse=True)

            def ln_stats_of(b, kind):
                hold()
                for t in range(NT):
                    last = dve.bn_stats(ln_stats[:, t, :], x[:, b, t, :])
                link(last)
                hold()
                for t in range(NT):
                    last = dve.bn_aggr(ln_mv[:, t, :], ln_stats[:, t, :])
                link(last)
                dve.tensor_scalar(ln_ve[:, :], ln_mv[:, :, 1], LN_EPS, None, ALU.add).then_inc(S[kind + "_ve"], 1)

            def ln_apply(b, kind):
                dve.wait_ge(S[kind + "_pow"], b + 1)
                for t in range(NT):
                    last = dve.tensor_scalar(xn[:, t, :], x[:, b, t, :], ln_mv[:, t, 0:1], ln_rstd[:, t:t + 1],
                                             ALU.subtract, ALU.mult)
                last.then_inc(S[kind + "_xn"], 1)

            def ln_lo(b, kind, hi, lo):
                dve.wait_ge(S[kind + "_hi"], b + 1)
                dve.tensor_tensor(lo[:, :, :].rearrange("p k t -> p (k t)"), bank["x0"][:, :],
                                  f32(hi[:, :, :].rearrange("p k t -> p (k t)")), ALU.subtract
                                  ).then_inc(S[kind + "_lo"], 1)

            def q_ratio(b, s):
                n = ND if s == 0 else 1
                dve.wait_ge(S["q_xt"], 2 * b + s + 1)
                if s == 0:
                    dve.wait_ge(S["gu_in"], 32 * (b + 1))
                    dve.tensor_reduce(amax[:, n:2 * n], guT[:, :, :], AX.X, ALU.max, apply_absolute_value=True)
                    src = bank["x0"][:, :].rearrange("p (k t) -> p k t", k=ND)
                else:
                    dve.wait_ge(S["cx_in"], 32 * (b + 1))
                    dve.tensor_reduce(amax[:, n:2 * n], cxT[:, :], AX.X, ALU.max, apply_absolute_value=True)
                    src = bank["x0"][:, 0:T]
                link(dve.tensor_reduce(amax[:, 0:n], src, AX.X, ALU.max, apply_absolute_value=True))
                link(dve.tensor_scalar(amax[:, 0:2 * n], amax[:, 0:2 * n], Q_EPS, None, ALU.max))
                link(dve.reciprocal(amax[:, n:2 * n], amax[:, n:2 * n]))
                dve.tensor_tensor(ratio[:, 0:n], amax[:, 0:n], amax[:, n:2 * n], ALU.mult).then_inc(S["q_ratio"], 1)

            def q_diagonals(b, s):
                n = ND if s == 0 else 1
                dve.wait_ge(S["q_root"], 2 * b + s + 1)
                link(dve.tensor_scalar(sis[:, 0:n], sroot[:, 0:n], Q_EPS, None, ALU.max))
                link(dve.reciprocal(sis[:, n:2 * n], sis[:, 0:n]))
                for j in range(2 * n):
                    last = dve.tensor_scalar(dg[:, j, :], ident[:, :], sis[:, j:j + 1], None, ALU.mult)
                last.then_inc(S["q_diag"], 1)

            def q_scaled(b, s):
                dve.wait_ge(S["q_spread"], 2 * b + s + 1)
                w = D if s == 0 else I
                src = bank["x0"] if s == 0 else bank["x1"]
                s_row, inv_row = src[:, 0:w], src[:, w:2 * w]
                for j in range(2):
                    dve.tensor_tensor(qw[:, j, 0:w], xn[:, j, :] if s == 0 else act1[:, j, :], inv_row, ALU.mult)
                for j in range(2):
                    last = dve.tensor_tensor(qw[:, 2 + j, 0:w], gu[:, j, :] if s == 0 else cx[:, j, :], s_row,
                                             ALU.mult)
                link(last)
                link(dve.tensor_reduce(rowmax[:, :], qw[:, :, 0:w], AX.X, ALU.max, apply_absolute_value=True))

            def q_round(b, s):
                w = D if s == 0 else I
                link(dve.tensor_scalar(qscale[:, s, :], rowmax[:, :], Q_EPS, 1.0 / QMAX, ALU.max, ALU.mult))
                link(dve.reciprocal(qrecip[:, :], qscale[:, s, :]))
                for j in range(4):
                    last = dve.tensor_scalar(qw[:, j, 0:w], qw[:, j, 0:w], qrecip[:, j:j + 1], MAGIC,
                                             ALU.mult, ALU.add)
                link(last)
                dve.tensor_scalar(qw[:, :, 0:w], qw[:, :, 0:w], MAGIC + QMAX, MAGIC - QMAX, ALU.min, ALU.max
                                  ).then_inc(S["q_rounded"], 1)
                for j in (2, 3):
                    last = dve.tensor_scalar(dg[:, j, :], ident[:, :], qscale[:, s, j:j + 1], None, ALU.mult)
                last.then_inc(S["q_diag"], 1)

            def q_dequant(b, s):
                dve.wait_ge(S["q_wscale"], 2 * b + s + 1)
                for t in range(NT):
                    last = dve.scalar_tensor_tensor(out=hs[:, t, :], in0=bank["x0"][:, t * D:(t + 1) * D],
                                                    scalar=qscale[:, s, t:t + 1], in1=wscale[:, :],
                                                    op0=ALU.mult, op1=ALU.mult)
                return last

            def q_act(b):
                dve.wait_ge(S["q_exp"], b + 1)
                e = qw[:, 0:NT, 0:I]
                link(dve.tensor_scalar(e, e, 1.0, None, ALU.add))
                link(dve.reciprocal(e, e))
                dve.wait_ge(S["q_gu"], b + 1)
                dve.tensor_tensor(act1[:, :, :], act1[:, :, :], e, ALU.mult).then_inc(S["q_act"], 1)

            def q_residual(b):
                link(q_dequant(b, 1))
                link(dve.tensor_tensor(x[:, b, :, :], x[:, b, :, :], hs[:, :, :], ALU.add))

            def bit_act(b, c):
                n = BIT_CHUNKS * b + c + 1
                dve.wait_ge(S["bit_sig"], n)
                src, r = CHUNK_BANKS[c % 3], c % 3
                if c < BIT_FULL:
                    rows = P
                    last = dve.tensor_tensor(act_raw[:, r, :], sig[:, r, :], src[:, T:2 * T], ALU.mult)
                else:
                    rows = BIT_REST
                    last = dve.tensor_tensor(act_raw[0:rows, r, :], sig[rows:P, r, :], src[rows:P, 0:T], ALU.mult)
                last.then_inc(S["bit_prod"], 1)
                dve.wait_ge(S["bit_prod"], n)
                dve.tensor_copy(act_hi[0:rows, r, :], act_raw[0:rows, r, :]).then_inc(S["bit_hi"], 1)

            def add_bank(b, which, done):
                dve.tensor_tensor(x[:, b, :, :].rearrange("p t d -> p (t d)"), bank[which][:, :],
                                  x[:, b, :, :].rearrange("p t d -> p (t d)"), ALU.add).then_inc(S[done], 1)

            def bit_residual(b):
                dve.wait_ge(S["bit_y"], BIT_CHUNKS * (b + 1))
                add_bank(b, "u", "bit_x")
                dve.wait_ge(S["bit_x"], b + 1)

            def ctx_split_lo(b):
                dve.wait_ge(S["ctx_hi"], b + 1)
                dve.tensor_tensor(cx_lo[:, :, :], cx[:, :, :], f32(cx_hi[:, :, :]), ALU.subtract)
                dve.tensor_tensor(cxT_lo[:, :], cxT[:, :], f32(cxT_hi[:, :]), ALU.subtract).then_inc(S["ctx_lo"], 1)

            def mask_row(b):
                dve.wait_ge(S["mask_in"], 16 * (b + 1))
                dve.tensor_reduce(valid_b[:, :], mask8[:, :], AX.X, ALU.max)
                dve.tensor_scalar(masked[:, :], mask8[:, :], -MASKED, MASKED, ALU.mult, ALU.add
                                  ).then_inc(S["mask_row"], 1)

            def queries_lo(b, p):
                dve.wait_ge(S["qa_h"], PAIRS * b + p + 1)
                dve.tensor_tensor(qa_lo[:, p % 2, :], bank["qa"][:, :], f32(qa_hi[:, p % 2, :]), ALU.subtract
                                  ).then_inc(S["qa_l"], 1)

            def row_minima(b, h):
                if h == 0:
                    dve.wait_ge(S["mask_row"], b + 1)
                dve.wait_ge(S["s_mm"], H * b + h + 1)
                hold()
                src = bank["s0"] if h % 2 == 0 else bank["s1"]
                for t in range(NT):
                    last = dve.tensor_tensor_reduce(out=prob[:, h % 2, t, :], in0=src[:, t * T:(t + 1) * T],
                                                    in1=masked[:, :], scale=1.0, scalar=3.0e38, op0=ALU.add,
                                                    op1=ALU.min, accum_out=row_min[:, h % 2, t:t + 1])
                last.then_inc(S["s_min"], 1)

            def row_inverses(b, h):
                dve.wait_ge(S["s_exp"], H * b + h + 1)
                dve.reciprocal(row_inv[:, h % 2, :], row_sum[:, h % 2, :]).then_inc(S["s_inv"], 1)

            def probs_lo(b, h):
                dve.wait_ge(S["t_h"], H * b + h + 1)
                dve.tensor_tensor(pt_lo[:, :, :].rearrange("p s t -> p (s t)"), bank["pt"][:, :],
                                  f32(pt_hi[:, :, :].rearrange("p s t -> p (s t)")), ALU.subtract
                                  ).then_inc(S["t_l"], 1)

            def mix_lo(b, h):
                dve.wait_ge(S["u_h"], H * b + h + 1)
                dve.tensor_tensor(ut_lo[:, :], bank["u"][:, 0:T], f32(ut_hi[:, :]), ALU.subtract
                                  ).then_inc(S["u_l"], 1)

            def attention(b, beside):
                for h in range(H):
                    if h >= 1:
                        mix_lo(b, h - 1)
                    if h + 1 < H:
                        row_inverses(b, h + 1)
                    probs_lo(b, h)
                    if h + 2 < H:
                        row_minima(b, h + 2)
                    if h % 2 == 1 and h + 3 < H:
                        queries_lo(b, (h + 3) // 2)
                    beside(h)

            def ffn_act(b, c):
                n = FFN_CHUNKS * b + c + 1
                dve.wait_ge(S["ffn_sig"], n)
                src, r = CHUNK_BANKS[c % 3], c % 3
                link(dve.tensor_tensor(sig[:, r, :], sig[:, r, :], src[:, 0:T], ALU.mult))
                dve.tensor_tensor(act_raw[:, r, :], sig[:, r, :], src[:, T:2 * T], ALU.mult
                                  ).then_inc(S["ffn_prod"], 1)
                dve.wait_ge(S["ffn_prod"], n)
                dve.tensor_copy(act_hi[:, r, :], act_raw[:, r, :]).then_inc(S["ffn_hi"], 1)

            def route_top(b):
                dve.wait_ge(S["route_mm"], b + 1)
                hold()
                for t in range(NT):
                    last = dve.max(top8[:, t, :], bank["x1"][:, t * NR:(t + 1) * NR])
                link(last)
                dve.tensor_tensor(top_d[:, :, 0:1], top8[:, :, 0:1], top8[:, :, 1:2], ALU.subtract)
                dve.tensor_tensor(top_d[:, :, 1:2], top8[:, :, 1:2], top8[:, :, 0:1], ALU.subtract
                                  ).then_inc(S["route_d"], 1)

            def route_sum(b):
                dve.wait_ge(S["route_sig"], b + 1)
                link(dve.tensor_tensor(comb[:, :], top_w[:, :, 0], top_w[:, :, 1], ALU.add))

            def ffn_residual(b):
                dve.wait_ge(S["ffn_y"], FFN_CHUNKS * (b + 1))
                for t in range(NT):
                    last = dve.scalar_tensor_tensor(out=x[:, b, t, :], in0=bank["o"][:, t * D:(t + 1) * D],
                                                    scalar=comb[:, t:t + 1], in1=x[:, b, t, :],
                                                    op0=ALU.mult, op1=ALU.add)
                link(last)
                add_bank(b, "u", "ffn_x")

            def batch(b, last):
                nxt = b + 1

                def beside(h):
                    if last:
                        return
                    if h == 0:
                        ln_stats_of(nxt, "lnq")
                    elif h == 1:
                        ln_apply(nxt, "lnq")
                    elif h == 2:
                        q_ratio(nxt, 0)
                    elif h == 3:
                        q_diagonals(nxt, 0)
                    elif h == 4:
                        q_scaled(nxt, 0)
                    elif h == 5:
                        q_round(nxt, 0)
                    elif h == 7:
                        q_dequant(nxt, 0).then_inc(S["q_hs"], 1)
                    elif h == 8:
                        q_act(nxt)
                    elif h == 9:
                        q_ratio(nxt, 1)
                    elif h == 10:
                        q_diagonals(nxt, 1)
                    elif h == 11:
                        q_scaled(nxt, 1)
                        q_round(nxt, 1)
                    elif h == 13:
                        q_residual(nxt)
                        ln_stats_of(nxt, "lnb")
                    elif h == 14:
                        ln_apply(nxt, "lnb")
                    elif h == 15:
                        ln_lo(nxt, "lnb", xt_hi, xt_lo)

                attention(b, beside)
                mix_lo(b, H - 1)
                dve.wait_ge(S["o_mm"], H * (b + 1))
                add_bank(b, "o", "att_x")
                dve.wait_ge(S["att_x"], b + 1)
                ln_stats_of(b, "lnf")
                if not last:
                    bit_act(nxt, 0)
                ln_apply(b, "lnf")
                if not last:
                    bit_act(nxt, 1)
                    bit_act(nxt, 2)
                    mask_row(nxt)
                    bit_act(nxt, 3)
                    ctx_split_lo(nxt)
                    bit_act(nxt, 4)
                ln_lo(b, "lnf", yt_hi, yt_lo)
                if not last:
                    bit_act(nxt, 5)
                    bit_residual(nxt)
                    ln_stats_of(nxt, "lna")
                ffn_act(b, 0)
                if not last:
                    ln_apply(nxt, "lna")
                route_top(b)
                for c in range(1, FFN_CHUNKS):
                    ffn_act(b, c)
                    if c == 2:
                        route_sum(b)
                    if not last:
                        if c == 3:
                            ln_lo(nxt, "lna", xt_hi, xt_lo)
                        if c == 5:
                            queries_lo(nxt, 0)
                        if c == 6:
                            queries_lo(nxt, 1)
                if not last:
                    row_minima(nxt, 0)
                    row_minima(nxt, 1)
                    row_inverses(nxt, 0)
                ffn_residual(b)

            def prep_lo(k):
                dve.wait_ge(S["prep_hi"], k + 1)
                p = k // 2
                lo, hi = ((t[:, 2 * p:2 * p + 2, :, :].rearrange("p h s c -> p (h s c)") for t in (a_lo, a_hi))
                          if k % 2 == 0 else
                          (t[:, 2 * p:2 * p + 2, :].rearrange("p h d -> p (h d)") for t in (c_lo, c_hi)))
                dve.scalar_tensor_tensor(out=lo, in0=PREP_BANKS[k % 2][:, :], scalar=-SCALE if k % 2 == 0 else 1.0,
                                         in1=f32(hi), op0=ALU.mult, op1=ALU.subtract).then_inc(S["prep_lo"], 1)

            def ternary():
                n_w = float(BIT * D)
                dve.wait_ge(S["gamma_mm"], 1)
                link(dve.tensor_scalar(gam[:, :], bank["u"][:, 0:4], 1.0 / n_w, None, ALU.mult))
                link(dve.tensor_tensor(gam[:, 2:3], gam[:, 2:3], gam[:, 3:4], ALU.add))
                link(dve.tensor_scalar(gam[:, 0:3], gam[:, 0:3], BIT_EPS, None, ALU.add))
                link(dve.reciprocal(gam[:, 0:3], gam[:, 0:3]))
                lo, hi = MAGIC - 1.0, MAGIC + 1.0
                for j in range(2):
                    w = w12_raw[:, :, j * BIT:(j + 1) * BIT]
                    last = dve.tensor_scalar(w, w, gam[:, j:j + 1], MAGIC, ALU.mult, ALU.add)
                link(last)
                dve.tensor_scalar(w12_raw[:, :, :], w12_raw[:, :, :], hi, lo, ALU.min, ALU.max).then_inc(S["bit_q"], 1)
                main, rest = w3_raw[:, 0:BIT_FULL, :], w3_raw[0:BIT_REST, BIT_FULL, :]
                dve.tensor_scalar(main, main, gam[:, 2:3], MAGIC, ALU.mult, ALU.add)
                link(dve.tensor_scalar(rest, rest, gam[0:BIT_REST, 2:3], MAGIC, ALU.mult, ALU.add))
                dve.tensor_scalar(main, main, hi, lo, ALU.min, ALU.max).then_inc(S["bit_q"], 1)
                dve.tensor_scalar(rest, rest, hi, lo, ALU.min, ALU.max).then_inc(S["bit_q"], 1)

            dve.wait_ge(S["x0_in"], 16)
            ln_stats_of(0, "lnq")
            ln_apply(0, "lnq")
            dve.wait_ge(S["consts"], 2)
            q_ratio(0, 0)
            q_diagonals(0, 0)
            q_scaled(0, 0)
            q_round(0, 0)
            q_dequant(0, 0).then_inc(S["q_hs"], 1)
            q_act(0)
            ternary()
            prep_lo(0)
            prep_lo(1)
            q_ratio(0, 1)
            prep_lo(2)
            prep_lo(3)
            q_diagonals(0, 1)
            prep_lo(4)
            prep_lo(5)
            q_scaled(0, 1)
            q_round(0, 1)
            prep_lo(6)
            prep_lo(7)
            q_residual(0)
            ln_stats_of(0, "lnb")
            prep_lo(8)
            ln_apply(0, "lnb")
            for k in range(9, 12):
                prep_lo(k)
            ln_lo(0, "lnb", xt_hi, xt_lo)
            for k in range(12, ATT_UNITS):
                prep_lo(k)
            for c in range(BIT_CHUNKS):
                bit_act(0, c)
            bit_residual(0)
            ln_stats_of(0, "lna")
            mask_row(0)
            ctx_split_lo(0)
            ln_apply(0, "lna")
            dve.wait_ge(S["router_ready"], 1)
            dve.tensor_tensor(router_lo[:, :, :], router_raw[:, :, :], f32(router_hi[:, :, :]), ALU.subtract
                              ).then_inc(S["router_ready"], 1)
            ln_lo(0, "lna", xt_hi, xt_lo)
            queries_lo(0, 0)
            queries_lo(0, 1)
            row_minima(0, 0)
            row_minima(0, 1)
            row_inverses(0, 0)
            dve.wait_ge(S["x_in"], 16 * (NB - 1))
            start = links["n"]
            with dve.Fori(0, NB - 1) as b:
                links["base"], links["n"] = b * LINKS + start, 0
                batch(b, False)
                assert links["n"] == LINKS, links["n"]
            links["base"], links["n"] = start + (NB - 1) * LINKS, 0
            batch(NB - 1, True)


def kernel(**inputs):
    import numpy as np
    import concourse.bacc as bacc
    from concourse.bass_utils import run_bass_kernel_spmd

    def t(a):
        return np.ascontiguousarray(np.swapaxes(np.asarray(a), -1, -2))

    w1T, w2T = t(inputs["L0_ffn_w1"]), t(inputs["L0_ffn_w2"])
    full = BIT_FULL * P
    layout = {
        "x": inputs["x"],
        "gu": inputs["fside_BxS2xS2_0"],
        "guT": t(inputs["fside_BxS2xS2_0"]),
        "ctx": inputs["ctx_1024"],
        "ctxT": t(inputs["ctx_1024"]),
        "mask": np.asarray(inputs["mask_BxS2_bf1"]).view(np.uint8),
        "w12T": np.concatenate([w1T, w2T[:, full:], w2T[:, :full]], axis=1),
        "w3T": t(inputs["L0_ffn_w3"]),
        "wqT": t(inputs["L1_xattn_Wq"]),
        "wkT": t(inputs["L1_xattn_Wk"]),
        "wvT": t(inputs["L1_xattn_Wv"]),
        "wo": inputs["L1_xattn_Wo"],
        "routerT": t(inputs["L1_ffn_router_weight"]),
        "gateT": np.concatenate([t(inputs["L1_ffn_sh_gate"]), t(inputs["L1_ffn_r_gate"])], axis=1),
        "upT": np.concatenate([t(inputs["L1_ffn_sh_up"]), t(inputs["L1_ffn_r_up"])], axis=1),
        "downT": np.concatenate([t(inputs["L1_ffn_sh_down"]), t(inputs["L1_ffn_r_down"])], axis=0)
                   .reshape(FFN_CHUNKS, P, D).transpose(1, 0, 2).reshape(FFN, D),
    }
    nc = bacc.Bacc("TRN2", target_bir_lowering=False, num_devices=1)
    arrays, args = {}, []
    for name, a in layout.items():
        a = np.ascontiguousarray(a)
        arrays[f"in_{name}"] = a
        args.append(nc.dram_tensor(f"in_{name}", a.shape, mybir.dt.from_np(a.dtype), kind="ExternalInput").ap())
    args.append(nc.dram_tensor("out_x", (NB, T, D), F32, kind="ExternalOutput").ap())
    build(nc, *args)
    return run_bass_kernel_spmd(nc, [arrays], core_ids=[0]).results[0]["out_x"]
```

```python
from contextlib import ExitStack

import concourse.bass as bass
from concourse import mybir

F32 = mybir.dt.float32
F32R = mybir.dt.float32r
BF16 = mybir.dt.bfloat16
U8 = mybir.dt.uint8
ALU = mybir.AluOpType
ACT = mybir.ActivationFunctionType
AX = mybir.AxisListType

P = 128
NB, T, D = 4, 256, 256
NT, ND = T // P, D // P
I = 128
H, DH = 16, 128
PAIRS = H // 2
BIT = 704
BIT_FULL = BIT // P
BIT_REST = BIT - BIT_FULL * P
BIT_CHUNKS = BIT_FULL + 1
INTER, ROUTED = 1024, 128
FFN = INTER + ROUTED
FFN_CHUNKS = FFN // P
NR = 8
LN_EPS, Q_EPS, BIT_EPS = 1e-5, 1e-6, 1e-8
QMAX = 127.0
MAGIC = 1.5 * 2.0 ** 23
MASKED = 1e30
SCALE = float(DH) ** -0.5
LINKS = 30
ATT_UNITS = 2 * PAIRS
WQ_LOADS = 4
FFN_UNITS = 6


def build(nc, x_in, gu_in, guT_in, ctx_in, ctxT_in, mask_in, w12T_in, w3T_in, wqT_in, wkT_in,
          wvT_in, wo_in, routerT_in, gateT_in, upT_in, downT_in, out):
    with ExitStack() as ctx:
        def sb(name, shape, dt=F32, stack=ctx):
            return stack.enter_context(nc.sbuf_tensor(name, shape, dt))

        def sem(name):
            return ctx.enter_context(nc.semaphore(name))

        bank = {n: ctx.enter_context(nc.psum_tensor("bank_" + n, [P, 512], F32))
                for n in ("qa", "s0", "s1", "pt", "u", "o", "x0", "x1")}
        CHUNK_BANKS = (bank["s0"], bank["s1"], bank["pt"])
        NEXT_BANKS = (bank["x1"], bank["u"], bank["pt"])
        PREP_BANKS = (bank["qa"], bank["o"])

        with ExitStack() as raw:
            wq_raw = sb("wq_raw", [P, H, D], F32, raw)
            wo_raw = sb("wo_raw", [P, H, D], F32, raw)
            gate_raw = sb("gate_raw", [P, ND, FFN], F32, raw)
            up_raw = sb("up_raw", [P, ND, FFN], F32, raw)
            down_raw = sb("down_raw", [P, FFN_CHUNKS, D], F32, raw)
            xn_next = sb("xn_next", [P, H, D], F32, raw)[:, H - (NB - 1) * NT:H, :]
        a_lo = sb("a_lo", [P, H, ND, P], F32R)
        c_lo = sb("c_lo", [P, H, D], F32R)
        gate_lo = sb("gate_lo", [P, ND, FFN], F32R)
        up_lo = sb("up_lo", [P, ND, FFN], F32R)
        down_lo = sb("down_lo", [P, FFN_CHUNKS, D], F32R)
        c_hi = sb("c_hi", [P, H, D], F32R)
        a_hi = sb("a_hi", [P, H, ND, P], F32R)
        gate_hi = sb("gate_hi", [P, ND, FFN], F32R)
        up_hi = sb("up_hi", [P, ND, FFN], F32R)
        down_hi = sb("down_hi", [P, FFN_CHUNKS, D], F32R)
        RAW, HI, LO = (gate_raw, up_raw, down_raw), (gate_hi, up_hi, down_hi), (gate_lo, up_lo, down_lo)
        router_raw = sb("router_raw", [P, ND, NR])
        router_hi = sb("router_hi", [P, ND, NR], F32R)
        router_lo = sb("router_lo", [P, ND, NR], F32R)
        w12 = sb("w12", [P, ND, 2 * BIT], F32R)
        w3 = sb("w3", [P, BIT_CHUNKS, D], F32R)

        ident = sb("ident", [P, P])
        ones = sb("ones", [P, P])
        half_exp = sb("half_exp", [P, 2, NB, ND])
        x = sb("x", [P, NB, NT, D])
        mask8 = sb("mask8", [P, T], U8)
        valid_b = sb("valid_b", [P, 1])
        masked = sb("masked", [P, T])
        ln_stats = sb("ln_stats", [P, NT, 6])
        ln_mv = sb("ln_mv", [P, NT, 2])
        ln_ve = sb("ln_ve", [P, NT])
        ln_rstd = sb("ln_rstd", [P, NT])
        xn = sb("xn", [P, NT, D])
        xt_hi = sb("xt_hi", [P, ND, T], F32R)
        xt_lo = sb("xt_lo", [P, ND, T], F32R)
        gu = sb("gu", [P, 2, D])
        cx = sb("cx", [P, 2, I])
        cxT = sb("cxT", [P, T])
        qw = sb("qw", [P, 4, D])
        dg = sb("dg", [P, 4, P])
        amax0 = sb("amax0", [P, 2, NB, ND])
        ratio0 = sb("ratio0", [P, 2, NB, ND])
        root0 = sb("root0", [P, 2, NB, ND])
        lnq_stats = sb("lnq_stats", [P, NB, NT, 6])
        lnq_mv = sb("lnq_mv", [P, NB, NT, 2])
        lnq_rstd = sb("lnq_rstd", [P, NB, NT])
        amax1 = sb("amax1", [P, 2])
        ratio1 = sb("ratio1", [P, 2])
        sis = sb("sis", [P, 2, ND])
        rowmax = sb("rowmax", [P, 4])
        qscale = sb("qscale", [P, 2, 4])
        qrecip = sb("qrecip", [P, 4])
        qT = sb("qT", [P, 4, D], BF16)
        wscale = sb("wscale", [P, D])
        hs = sb("hs", [P, NT, D])
        act1 = hs[:, :, I:2 * I]
        cx_hi = sb("cx_hi", [P, 2, I], F32R)
        cx_lo = sb("cx_lo", [P, 2, I], F32R)
        cxT_hi = sb("cxT_hi", [P, T], F32R)
        cxT_lo = sb("cxT_lo", [P, T], F32R)
        row_min = sb("row_min", [P, 2, NT])
        row_sum = sb("row_sum", [P, 2, NT])
        row_inv = sb("row_inv", [P, 2, NT])
        gsum = sb("gsum", [P, 4])
        gam = sb("gam", [P, 4])
        top8 = sb("top8", [P, NT, NR])
        top_d = sb("top_d", [P, NT, 2])
        top_w = sb("top_w", [P, NT, 2])
        comb = sb("comb", [P, NT])

        with ExitStack() as first:
            guT = sb("guT", [P, NB, ND, 2 * I], F32, first)
            w12_raw = sb("w12_raw", [P, ND, 2 * BIT], F32, first)
            w3_raw = sb("w3_raw", [P, BIT_CHUNKS, D], F32, first)
            wkT = sb("wkT", [P, PAIRS, P], F32, first)
            wvT = sb("wvT", [P, PAIRS, P], F32, first)
        qa_hi = sb("qa_hi", [P, 2, 2 * T], F32R)
        qa_lo = sb("qa_lo", [P, 2, 2 * T], F32R)
        ut_hi = sb("ut_hi", [P, T], F32R)
        prob = sb("prob", [P, 2, NT, T])
        act_raw = sb("act_raw", [P, 3, T])
        act_hi = sb("act_hi", [P, 3, T], F32R)
        act_lo = sb("act_lo", [P, 3, T], F32R)
        sig = sb("sig", [P, 3, T])
        pt_hi = sb("pt_hi", [P, 2, T], F32R)
        pt_lo = sb("pt_lo", [P, 2, T], F32R)
        yt_hi = sb("yt_hi", [P, ND, T], F32R)
        yt_lo = sb("yt_lo", [P, ND, T], F32R)
        ut_lo = sb("ut_lo", [P, T], F32R)

        S = {}
        for n in """consts x0_in x_in mask_in gu_in guT0_in guT_in cx_in w12_in w3_in wk_in wv_in router_in out_done
                    abs_done gamma_mm bit_q12 bit_r3 bit_q3 w12_ready w3_ready
                    prep_mm prep_hi prep_lo ffn_w_hi ffn_w_lo_pool ffn_w_lo_dve router_hi router_lo
                    lnq_ve lnq_pow q_ratio0 lnq_xn next_xn next_turned next_read q_roots q_sis
                    lnb_ve lnb_pow lnb_xn lna_ve lna_pow lna_xn lnf_ve lnf_pow lnf_xn
                    lnb_t lnb_hi lnb_lo lna_t lna_hi lna_lo lnf_t lnf_hi lnf_lo
                    q0_xt q_xt q_ratio q_root q_diag q_spread q_scales q_rounded q_wdiag q_turned q_bf q_bf_w
                    q_prod q_wscale q_hs q_tanh q_gu q_sigm q_act dve_self
                    bit_mm bit_sig bit_prod bit_hi bit_lo bit_y bit_x
                    ctx_hi ctx_lo mask_row
                    qa_mm qa_h qa_l s_mm s_min s_exp s_inv s_norm t_mm t_h t_l u_mm u_h u_l o_mm
                    att_x route_mm route_d route_sig route_w
                    ffn_mm ffn_sig ffn_prod ffn_hi ffn_lo ffn_y ffn_x""".split():
            S[n] = sem(n)
        for i in range(WQ_LOADS):
            for n in ("wq", "wo"):
                S[f"{n}{i}"] = sem(f"{n}{i}_in")
        for i in range(FFN_UNITS):
            S[f"ffn_w{i}"] = sem(f"ffn_w{i}_in")

        def f32(ap):
            return ap.bitcast(F32)

        def ffn_unit(u, tensors):
            which, half = u // 2, u % 2
            t = tensors[which]
            if which < 2:
                return t[:, half, :]
            n = FFN_CHUNKS * D // 2
            return t[:, :, :].rearrange("p c d -> p (c d)")[:, half * n:(half + 1) * n]

        block = ctx.enter_context(nc.Block())

        @block.sync
        def _(sp):
            def expert_weights(b):
                if not (isinstance(b, int) and b == 0):
                    sp.wait_ge(S["q_rounded"], 2 * b)
                    sp.wait_ge(S["ctx_lo"], b)
                sp.dma_start(gu[:, :, :], gu_in[b].rearrange("(o p) d -> p o d", p=P)).then_inc(S["gu_in"], 16)
                sp.dma_start(cx[:, :, :], ctx_in[b].rearrange("(o p) d -> p o d", p=P)).then_inc(S["cx_in"], 16)
                sp.dma_start(cxT[:, :], ctxT_in[b]).then_inc(S["cx_in"], 16)
                sp.dma_start(mask8[:, :], mask_in[b].partition_broadcast(P)).then_inc(S["mask_in"], 16)

            def turned_expert_weights(b, done):
                sp.dma_start(guT[:, b, :, :], guT_in[b].rearrange("(k p) o -> p k o", p=P)).then_inc(S[done], 16)

            def x_rows(dram, b):
                return dram[b].rearrange("(t p) d -> p t d", p=P)

            def store(b):
                sp.wait_ge(S["ffn_x"], b + 1)
                sp.dma_start(x_rows(out, b), x[:, b, :, :]).then_inc(S["out_done"], 16)

            sp.dma_start(x[:, 0, :, :], x_rows(x_in, 0)).then_inc(S["x0_in"], 16)
            turned_expert_weights(0, "guT0_in")
            expert_weights(0)
            def attention_weights(i):
                n = H // WQ_LOADS
                for name, raw, dram in (("wq", wq_raw, wqT_in), ("wo", wo_raw, wo_in)):
                    if i == 0:
                        kv, kv_in = (wkT, wkT_in) if name == "wq" else (wvT, wvT_in)
                        sp.dma_start(kv[:, :, :], kv_in.rearrange("(g p) d -> p g d", p=P)
                                     ).then_inc(S["wk_in" if name == "wq" else "wv_in"], 16)
                    sp.dma_start(raw[:, i * n:(i + 1) * n, :],
                                 dram[i * n * P:(i + 1) * n * P].rearrange("(h p) d -> p h d", p=P)
                                 ).then_inc(S[f"{name}{i}"], 16)

            attention_weights(0)
            for b in range(1, NB):
                sp.dma_start(x[:, b, :, :], x_rows(x_in, b)).then_inc(S["x_in"], 16)
            sp.dma_start(w12_raw[:, :, :], w12T_in.rearrange("(k p) n -> p k n", p=P)).then_inc(S["w12_in"], 16)
            attention_weights(1)
            sp.dma_start(w3_raw[:, 0:BIT_FULL, :], w3T_in[0:BIT_FULL * P].rearrange("(c p) d -> p c d", p=P)
                         ).then_inc(S["w3_in"], 16)
            sp.dma_start(w3_raw[0:BIT_REST, BIT_FULL, :], w3T_in[BIT_FULL * P:BIT]).then_inc(S["w3_in"], 16)
            for b in range(1, NB):
                turned_expert_weights(b, "guT_in")
            attention_weights(2)
            attention_weights(3)
            sp.dma_start(router_raw[:, :, :], routerT_in.rearrange("(k p) n -> p k n", p=P)
                         ).then_inc(S["router_in"], 16)
            for u in range(FFN_UNITS):
                which, half = u // 2, u % 2
                n = FFN_CHUNKS * D // 2
                src = ((gateT_in, upT_in)[which][half * P:(half + 1) * P, :] if which < 2 else
                       downT_in.rearrange("(p c) d -> p (c d)", p=P)[:, half * n:(half + 1) * n])
                sp.dma_start(ffn_unit(u, RAW), src).then_inc(S[f"ffn_w{u}"], 16)
            with sp.Fori(0, NB - 1) as b:
                expert_weights(b + 1)
                store(b)
            store(NB - 1)
            sp.wait_ge(S["out_done"], 16 * NB)

        @block.tensor
        def _(pe):
            def split_mm(out_ap, w_hi, w_lo, r_hi, r_lo, start, stop):
                passes = [(w_hi, r_hi), (w_hi, r_lo), (w_lo, r_hi)]
                passes = [(w, r) for w, r in passes if w is not None and r is not None]
                for n, (w, r) in enumerate(passes):
                    last = pe.matmul(out_ap, w, r, start=start and n == 0, stop=stop and n == len(passes) - 1,
                                     skip_group_check=True)
                return last

            def turn_xn(dst):
                for t in range(NT):
                    for k in range(ND):
                        last = pe.transpose(dst[:, k * T + t * P:k * T + (t + 1) * P],
                                            xn[:, t, k * P:(k + 1) * P], ident[:, :])
                return last

            def q_turn_x0():
                pe.wait_ge(S["lnq_xn"], 1)
                turn_xn(bank["x0"]).then_inc(S["q0_xt"], 1)

            def q_turn_next():
                pe.wait_ge(S["q_wscale"], 2)
                pe.wait_ge(S["next_xn"], 1)
                for b in range(1, NB):
                    for t in range(NT):
                        for k in range(ND):
                            last = pe.transpose(NEXT_BANKS[b - 1][:, k * T + t * P:k * T + (t + 1) * P],
                                                xn_next[:, (b - 1) * NT + t, k * P:(k + 1) * P], ident[:, :])
                last.then_inc(S["next_turned"], 1)

            def q_spread(b, s):
                pe.wait_ge(S["q_diag"], 2 * b + s + 1)
                w = 512 if s == 0 else 256
                dst = bank["x0"] if s == 0 else bank["x1"]
                pe.matmul(dst[:, 0:w], ones[:, :], dg[:, 0:w // P, :].rearrange("p a c -> p (a c)"),
                          start=True, stop=True).then_inc(S["q_spread"], 1)

            def q_turn_rounded(b, s):
                pe.wait_ge(S["q_rounded"], 2 * b + s + 1)
                if s == 0:
                    for j in range(4):
                        dst = bank["x0"] if j < 2 else bank["x1"]
                        for k in range(ND):
                            last = pe.transpose(dst[:, k * 256 + (j % 2) * P:k * 256 + (j % 2 + 1) * P],
                                                qw[:, j, k * P:(k + 1) * P], ident[:, :])
                else:
                    for j in range(4):
                        last = pe.transpose(bank["x0"][:, j * P:(j + 1) * P], qw[:, j, 0:I], ident[:, :])
                last.then_inc(S["q_turned"], 1)

            def q_product(b, s):
                pe.wait_ge(S["q_bf"], 2 * b + s + 1)
                if s == 0:
                    pe.wait_ge(S["q_bf_w"], b + 1)
                for t in range(NT):
                    if s == 0:
                        for k in range(ND):
                            last = pe.matmul(bank["x0"][:, t * D:(t + 1) * D], qT[:, k, t * P:(t + 1) * P],
                                             qT[:, 2 + k, :], start=(k == 0), stop=(k == ND - 1))
                    else:
                        last = pe.matmul(bank["x0"][:, t * D:(t + 1) * D], qT[:, 0, t * P:(t + 1) * P],
                                         qT[:, 1, :], start=True, stop=True)
                pe.wait_ge(S["q_wdiag"], 2 * b + s + 1)
                pe.matmul(bank["x1"][:, 0:D], ones[:, :], dg[:, 2:4, :].rearrange("p a c -> p (a c)"),
                          start=True, stop=True).then_inc(S["q_prod"], 1)

            def q_turn_act(b):
                pe.wait_ge(S["q_act"], b + 1)
                for t in range(NT):
                    last = pe.transpose(bank["x0"][:, t * P:(t + 1) * P], act1[:, t, :], ident[:, :])
                last.then_inc(S["q_xt"], 1)

            def q_piece(n, b):
                if n == 0:
                    q_spread(b, 0)
                elif n == 1:
                    q_turn_rounded(b, 0)
                elif n == 2:
                    q_product(b, 0)
                elif n == 3:
                    q_turn_act(b)
                elif n == 4:
                    q_spread(b, 1)
                elif n == 5:
                    q_turn_rounded(b, 1)
                elif n == 6:
                    q_product(b, 1)

            def bit_up(b, c):
                if c >= 3:
                    pe.wait_ge(S["bit_prod"], BIT_CHUNKS * b + c - 2)
                dst = CHUNK_BANKS[c % 3]
                if c < BIT_FULL:
                    sides = ((0, c * P), (T, BIT + BIT_REST + c * P))
                else:
                    sides = ((0, BIT_FULL * P),)
                first = True
                for at, col in sides:
                    for k in range(ND):
                        w = w12[:, k, col:col + P]
                        last = split_mm(dst[:, at:at + T], w, None, xt_hi[:, k, :], xt_lo[:, k, :], first, k == ND - 1)
                        first = False
                last.then_inc(S["bit_mm"], 1)

            def bit_down(b, c):
                if c == 0:
                    pe.wait_ge(S["w3_ready"], 2)
                pe.wait_ge(S["bit_hi"], BIT_CHUNKS * b + c + 1)
                pe.wait_ge(S["bit_lo"], BIT_CHUNKS * b + c + 1)
                rows = P if c < BIT_FULL else BIT_REST
                for t in range(NT):
                    for half in (act_hi, act_lo):
                        last = pe.matmul(bank["u"][:, t * D:(t + 1) * D], half[0:rows, c % 3, t * P:(t + 1) * P],
                                         w3[0:rows, c, :], start=(c == 0 and t == 0 and half is act_hi),
                                         stop=(c == BIT_CHUNKS - 1), skip_group_check=True)
                last.then_inc(S["bit_y"], 1)

            def bit_turn(b):
                pe.wait_ge(S["lnb_xn"], b + 1)
                turn_xn(bank["x0"]).then_inc(S["lnb_t"], 1)

            def bit_layer(b, between=None):
                pe.wait_ge(S["lnb_hi"], b + 1)
                pe.wait_ge(S["lnb_lo"], b + 1)
                for c in range(BIT_CHUNKS + 2):
                    if c < BIT_CHUNKS:
                        bit_up(b, c)
                    if c >= 2:
                        bit_down(b, c - 2)
                    if between is not None:
                        between(c)

            def att_turn(b):
                pe.wait_ge(S["lna_xn"], b + 1)
                turn_xn(bank["x0"]).then_inc(S["lna_t"], 1)

            def queries(b, h):
                p = h // 2
                if h % 2 == 0 and p >= 1:
                    pe.wait_ge(S["qa_l"], PAIRS * b + p)
                dst = bank["qa"][:, (h % 2) * T:(h % 2 + 1) * T]
                for k in range(ND):
                    last = split_mm(dst, a_hi[:, h, k, :], a_lo[:, h, k, :], xt_hi[:, k, :], xt_lo[:, k, :],
                                    k == 0, k == ND - 1)
                if h % 2 == 1:
                    last.then_inc(S["qa_mm"], 1)

            def scores(b, h):
                pe.wait_ge(S["qa_l"], PAIRS * b + h // 2 + 1)
                if h >= 2:
                    pe.wait_ge(S["s_min"], H * b + h - 1)
                dst = bank["s0"] if h % 2 == 0 else bank["s1"]
                ring, col = (h // 2) % 2, (h % 2) * T
                for t in range(NT):
                    cols = slice(col + t * P, col + (t + 1) * P)
                    last = split_mm(dst[:, t * T:(t + 1) * T], qa_hi[:, ring, cols], qa_lo[:, ring, cols],
                                    cxT_hi[:, :], cxT_lo[:, :], True, True)
                last.then_inc(S["s_mm"], 1)

            def turn_probs(b, h):
                pe.wait_ge(S["s_norm"], H * b + h + 1)
                if h >= 1:
                    pe.wait_ge(S["t_l"], H * b + h)
                for t in range(NT):
                    for s in range(2):
                        last = pe.transpose(bank["pt"][:, s * T + t * P:s * T + (t + 1) * P],
                                            prob[:, h % 2, t, s * P:(s + 1) * P], ident[:, :])
                last.then_inc(S["t_mm"], 1)

            def mix(b, h):
                pe.wait_ge(S["t_l"], H * b + h + 1)
                if h >= 1:
                    pe.wait_ge(S["u_l"], H * b + h)
                for s in range(2):
                    last = split_mm(bank["u"][:, 0:T], cx_hi[:, s, :], cx_lo[:, s, :], pt_hi[:, s, :],
                                    pt_lo[:, s, :], s == 0, s == 1)
                last.then_inc(S["u_mm"], 1)

            def project(b, h):
                pe.wait_ge(S["u_l"], H * b + h + 1)
                for t in range(NT):
                    cols = slice(t * P, (t + 1) * P)
                    last = split_mm(bank["o"][:, t * D:(t + 1) * D], ut_hi[:, cols], ut_lo[:, cols],
                                    c_hi[:, h, :], c_lo[:, h, :], h == 0 and t == 0, h == H - 1)
                last.then_inc(S["o_mm"], 1)

            def attention(b, beside=None):
                for h in range(H):
                    turn_probs(b, h)
                    if h + 4 < H:
                        queries(b, h + 4)
                    if h + 2 < H:
                        scores(b, h + 2)
                    if beside is not None:
                        beside(h)
                    if h >= 1:
                        project(b, h - 1)
                    mix(b, h)

            def ffn_turn(b):
                pe.wait_ge(S["lnf_xn"], b + 1)
                turn_xn(bank["x0"]).then_inc(S["lnf_t"], 1)

            def route(b):
                pe.wait_ge(S["router_hi"], 1)
                pe.wait_ge(S["router_lo"], 1)
                pe.wait_ge(S["lnf_hi"], b + 1)
                pe.wait_ge(S["lnf_lo"], b + 1)
                for t in range(NT):
                    for k in range(ND):
                        cols = slice(t * P, (t + 1) * P)
                        last = split_mm(bank["x1"][:, t * NR:(t + 1) * NR], yt_hi[:, k, cols], yt_lo[:, k, cols],
                                        router_hi[:, k, :], router_lo[:, k, :], k == 0, k == ND - 1)
                last.then_inc(S["route_mm"], 1)

            def ffn_up(b, c):
                if c >= 3:
                    pe.wait_ge(S["ffn_prod"], FFN_CHUNKS * b + c - 2)
                dst = CHUNK_BANKS[c % 3]
                first = True
                for at, w_hi, w_lo in ((0, gate_hi, gate_lo), (T, up_hi, up_lo)):
                    for k in range(ND):
                        cols = slice(c * P, (c + 1) * P)
                        last = split_mm(dst[:, at:at + T], w_hi[:, k, cols], w_lo[:, k, cols], yt_hi[:, k, :],
                                        yt_lo[:, k, :], first, k == ND - 1)
                        first = False
                last.then_inc(S["ffn_mm"], 1)

            def ffn_down(b, c):
                pe.wait_ge(S["ffn_hi"], FFN_CHUNKS * b + c + 1)
                pe.wait_ge(S["ffn_lo"], FFN_CHUNKS * b + c + 1)
                routed = c == FFN_CHUNKS - 1
                dst = bank["o"] if routed else bank["u"]
                for t in range(NT):
                    cols = slice(t * P, (t + 1) * P)
                    last = split_mm(dst[:, t * D:(t + 1) * D], act_hi[:, c % 3, cols], act_lo[:, c % 3, cols],
                                    down_hi[:, c, :], down_lo[:, c, :], t == 0 and (c == 0 or routed),
                                    c >= FFN_CHUNKS - 2)
                last.then_inc(S["ffn_y"], 1)

            def ffn_layer(b, last):
                route(b)
                pe.wait_ge(S["ffn_w_lo_pool"], FFN_UNITS // 2)
                pe.wait_ge(S["ffn_w_lo_dve"], FFN_UNITS // 2)
                for c in range(FFN_CHUNKS + 2):
                    if c < FFN_CHUNKS:
                        ffn_up(b, c)
                    if not last and c == FFN_CHUNKS:
                        pe.wait_ge(S["ffn_prod"], FFN_CHUNKS * b + FFN_CHUNKS - 2)
                        pe.wait_ge(S["ctx_lo"], b + 2)
                        scores(b + 1, 0)
                    if not last and c == FFN_CHUNKS + 1:
                        pe.wait_ge(S["ffn_prod"], FFN_CHUNKS * b + FFN_CHUNKS - 1)
                        scores(b + 1, 1)
                    if c == 2 and not last:
                        pe.wait_ge(S["bit_x"], b + 2)
                    if c >= 2:
                        ffn_down(b, c - 2)
                    if not last and c == 2:
                        att_turn(b + 1)
                    if not last and c in (5, 6):
                        if c == 5:
                            pe.wait_ge(S["lna_hi"], b + 2)
                            pe.wait_ge(S["lna_lo"], b + 2)
                        queries(b + 1, 2 * (c - 5))
                        queries(b + 1, 2 * (c - 5) + 1)

            Q_STEPS = {1: 0, 4: 1, 5: 2, 8: 3, 10: 4, 12: 5, 13: 6}

            def batch(b, last):
                def beside(h):
                    if h in Q_STEPS:
                        q_piece(Q_STEPS[h], b + 1)
                attention(b, None if last else beside)
                if not last:
                    bit_turn(b + 1)
                project(b, H - 1)
                if not last:
                    bit_layer(b + 1, lambda c: ffn_turn(b) if c == 3 else None)
                else:
                    ffn_turn(b)
                ffn_layer(b, last)

            def prep_unit(k):
                p = k // 2
                pe.wait_ge(S[("wq", "wo")[k % 2] + str(p * WQ_LOADS // PAIRS)], 16)
                if k < 2:
                    pe.wait_ge(S[("wk_in", "wv_in")[k]], 16)
                if k >= 2:
                    pe.wait_ge(S["prep_lo"], k - 1)
                dst = PREP_BANKS[k % 2]
                for j in range(2):
                    raw = (wq_raw, wo_raw)[k % 2][:, 2 * p + j, :]
                    if k % 2 == 0:
                        for s in range(ND):
                            last = pe.matmul(dst[:, (j * ND + s) * P:(j * ND + s + 1) * P],
                                             raw[:, s * P:(s + 1) * P], wkT[:, p, :], start=True, stop=True)
                    else:
                        last = pe.matmul(dst[:, j * D:(j + 1) * D], wvT[:, p, :], raw, start=True, stop=True)
                last.then_inc(S["prep_mm"], 1)

            pe.wait_ge(S["consts"], 2)
            q_turn_x0()
            prep_unit(0)
            prep_unit(1)
            q_piece(0, 0)
            prep_unit(2)
            prep_unit(3)
            q_piece(1, 0)
            q_piece(2, 0)
            prep_unit(4)
            prep_unit(5)
            q_piece(3, 0)
            pe.wait_ge(S["abs_done"], 4)
            pe.matmul(bank["u"][:, 0:4], ones[:, :], gsum[:, :], start=True, stop=True).then_inc(S["gamma_mm"], 1)
            prep_unit(6)
            q_piece(4, 0)
            prep_unit(7)
            q_piece(5, 0)
            q_piece(6, 0)
            prep_unit(8)
            q_turn_next()
            prep_unit(9)
            bit_turn(0)
            prep_unit(10)
            pe.wait_ge(S["w12_ready"], 2)

            def beside_bit(c):
                if c < 3:
                    prep_unit(11 + c)
                if c == 1:
                    pe.wait_ge(S["next_read"], 1)

            bit_layer(0, beside_bit)
            prep_unit(14)
            prep_unit(15)
            att_turn(0)
            pe.wait_ge(S["lna_hi"], 1)
            pe.wait_ge(S["lna_lo"], 1)
            for h in range(4):
                queries(0, h)
            pe.wait_ge(S["ctx_hi"], 1)
            pe.wait_ge(S["ctx_lo"], 1)
            scores(0, 0)
            scores(0, 1)
            with pe.Fori(0, NB - 1) as b:
                batch(b, False)
            batch(NB - 1, True)

        @block.scalar
        def _(act):
            def split_hi(dst, src, done, scale=1.0):
                act.activation(dst, src, ACT.Copy, scale=scale).then_inc(done, 1)

            def ln_hi(b, kind, dst):
                act.wait_ge(S[kind + "_t"], b + 1)
                split_hi(dst[:, :, :].rearrange("p k t -> p (k t)"), bank["x0"][:, :], S[kind + "_hi"])

            def q_tanh(b):
                act.wait_ge(S["q_hs"], b + 1)
                act.activation(qw[:, 0:NT, 0:I], hs[:, :, 0:I], ACT.Tanh, scale=0.5).then_inc(S["q_tanh"], 1)

            def q_round(b, s):
                act.wait_ge(S["q_scales"], 2 * b + s + 1)
                w = D if s == 0 else I
                for j in range(4):
                    last = act.activation(qw[:, j, 0:w], qw[:, j, 0:w], ACT.Copy, scale=qrecip[:, j:j + 1], bias=MAGIC)
                last.then_inc(S["q_rounded"], 1)

            def q_bf(b, s):
                act.wait_ge(S["q_turned"], 2 * b + s + 1)
                act.activation(qT[:, 0:2, :].rearrange("p a n -> p (a n)"), bank["x0"][:, :], ACT.Copy,
                               bias=-MAGIC).then_inc(S["q_bf"], 1)

            def q_wscale(b, s):
                act.wait_ge(S["q_prod"], 2 * b + s + 1)
                act.copy(wscale[:, :], bank["x1"][:, 0:D]).then_inc(S["q_wscale"], 1)

            def ctx_split_hi(b):
                act.wait_ge(S["cx_in"], 32 * (b + 1))
                act.copy(cx_hi[:, :, :], cx[:, :, :])
                act.copy(cxT_hi[:, :], cxT[:, :]).then_inc(S["ctx_hi"], 1)

            def queries_hi(b, p):
                act.wait_ge(S["qa_mm"], PAIRS * b + p + 1)
                split_hi(qa_hi[:, p % 2, :], bank["qa"][:, :], S["qa_h"])

            def exps(b, h):
                act.wait_ge(S["s_min"], H * b + h + 1)
                for t in range(NT):
                    row = prob[:, h % 2, t, :]
                    last = act.activation(row, row, ACT.Exp, scale=-1.0, bias=row_min[:, h % 2, t:t + 1],
                                          accum_out=row_sum[:, h % 2, t:t + 1])
                last.then_inc(S["s_exp"], 1)

            def probs_hi(b, h):
                act.wait_ge(S["t_mm"], H * b + h + 1)
                split_hi(pt_hi[:, :, :].rearrange("p s t -> p (s t)"), bank["pt"][:, :], S["t_h"])

            def mix_hi(b, h):
                act.wait_ge(S["u_mm"], H * b + h + 1)
                split_hi(ut_hi[:, :], bank["u"][:, 0:T], S["u_h"])

            def attention(b, last):
                for h in range(H):
                    if h >= 1:
                        mix_hi(b, h - 1)
                    probs_hi(b, h)
                    if h % 2 == 1 and h + 3 < H:
                        queries_hi(b, (h + 3) // 2)
                    if h + 2 < H:
                        exps(b, h + 2)
                    if last:
                        continue
                    if h == 3:
                        q_round(b + 1, 0)
                    if h == 4:
                        q_bf(b + 1, 0)
                    if h == 5:
                        q_wscale(b + 1, 0)
                    if h == 6:
                        q_tanh(b + 1)
                    if h == 11:
                        q_round(b + 1, 1)
                    if h == 12:
                        q_bf(b + 1, 1)
                    if h == 13:
                        q_wscale(b + 1, 1)

            def bit_sig(b, c):
                act.wait_ge(S["bit_mm"], BIT_CHUNKS * b + c + 1)
                src = CHUNK_BANKS[c % 3]
                if c < BIT_FULL:
                    act.activation(sig[:, c % 3, :], src[:, 0:T], ACT.Sigmoid).then_inc(S["bit_sig"], 1)
                else:
                    act.activation(sig[BIT_REST:P, c % 3, :], src[0:BIT_REST, 0:T], ACT.Sigmoid
                                   ).then_inc(S["bit_sig"], 1)

            def bit_high(b, c):
                act.wait_ge(S["bit_prod"], BIT_CHUNKS * b + c + 1)
                rows = P if c < BIT_FULL else BIT_REST
                act.copy(act_hi[0:rows, c % 3, :], act_raw[0:rows, c % 3, :]).then_inc(S["bit_hi"], 1)

            def ffn_high(b, c):
                act.wait_ge(S["ffn_prod"], FFN_CHUNKS * b + c + 1)
                act.copy(act_hi[:, c % 3, :], act_raw[:, c % 3, :]).then_inc(S["ffn_hi"], 1)

            def ffn_sig(b, c):
                act.wait_ge(S["ffn_mm"], FFN_CHUNKS * b + c + 1)
                act.activation(sig[:, c % 3, :], CHUNK_BANKS[c % 3][:, 0:T], ACT.Sigmoid).then_inc(S["ffn_sig"], 1)


            def batch(b, last):
                attention(b, last)
                if not last:
                    ln_hi(b + 1, "lnb", xt_hi)
                mix_hi(b, H - 1)
                if not last:
                    for c in range(4):
                        bit_sig(b + 1, c)
                        bit_high(b + 1, c)
                        if c == 1:
                            ctx_split_hi(b + 1)
                ln_hi(b, "lnf", yt_hi)
                if not last:
                    for c in range(4, BIT_CHUNKS):
                        bit_sig(b + 1, c)
                        bit_high(b + 1, c)
                for c in range(FFN_CHUNKS):
                    ffn_sig(b, c)
                    ffn_high(b, c)
                    if c == 1:
                        act.wait_ge(S["route_d"], b + 1)
                        act.activation(top_w[:, :, :], top_d[:, :, :], ACT.Sigmoid).then_inc(S["route_sig"], 1)
                    if not last:
                        if c == 3:
                            ln_hi(b + 1, "lna", xt_hi)
                        if c == 5:
                            queries_hi(b + 1, 0)
                        if c == 6:
                            queries_hi(b + 1, 1)
                if not last:
                    exps(b + 1, 0)
                    exps(b + 1, 1)

            def prep_hi(k):
                act.wait_ge(S["prep_mm"], k + 1)
                dst = (a_hi[:, 2 * (k // 2):2 * (k // 2) + 2, :, :].rearrange("p h s c -> p (h s c)") if k % 2 == 0 else
                       c_hi[:, 2 * (k // 2):2 * (k // 2) + 2, :].rearrange("p h d -> p (h d)"))
                split_hi(dst, PREP_BANKS[k % 2][:, :], S["prep_hi"], scale=-SCALE if k % 2 == 0 else 1.0)

            def ffn_weights_hi(u):
                act.wait_ge(S[f"ffn_w{u}"], 16)
                act.copy(ffn_unit(u, HI), ffn_unit(u, RAW)
                         ).then_inc(S["ffn_w_hi"], 1)

            def magnitudes(w, raw, k):
                act.activation(w, raw, ACT.Abs, accum_out=gsum[0:w.shape[0], k:k + 1]).then_inc(S["abs_done"], 1)

            act.wait_ge(S["consts"], 2)
            prep_hi(0)
            prep_hi(1)
            q_round(0, 0)
            prep_hi(2)
            prep_hi(3)
            q_bf(0, 0)
            act.wait_ge(S["w12_in"], 16)
            magnitudes(w12[:, :, 0:BIT], w12_raw[:, :, 0:BIT], 0)
            q_wscale(0, 0)
            q_tanh(0)
            magnitudes(w12[:, :, BIT:2 * BIT], w12_raw[:, :, BIT:2 * BIT], 1)
            act.wait_ge(S["w3_in"], 32)
            magnitudes(w3[:, 0:BIT_FULL, :], w3_raw[:, 0:BIT_FULL, :], 2)
            magnitudes(w3[0:BIT_REST, BIT_FULL, :], w3_raw[0:BIT_REST, BIT_FULL, :], 3)
            prep_hi(4)
            prep_hi(5)
            prep_hi(6)
            q_round(0, 1)
            prep_hi(7)
            q_bf(0, 1)
            q_wscale(0, 1)
            prep_hi(8)
            act.wait_ge(S["bit_q12"], 1)
            for j in range(2):
                act.activation(w12[:, :, j * BIT:(j + 1) * BIT], w12_raw[:, :, j * BIT:(j + 1) * BIT], ACT.Copy,
                               bias=-MAGIC).then_inc(S["w12_ready"], 1)
                if j == 0:
                    prep_hi(9)
            ln_hi(0, "lnb", xt_hi)
            act.wait_ge(S["bit_q3"], 1)
            act.activation(w3[:, 0:BIT_FULL, :], w3_raw[:, 0:BIT_FULL, :], ACT.Copy, bias=-MAGIC
                           ).then_inc(S["w3_ready"], 1)
            act.activation(w3[0:BIT_REST, BIT_FULL, :], w3_raw[0:BIT_REST, BIT_FULL, :], ACT.Copy,
                           bias=-MAGIC).then_inc(S["w3_ready"], 1)
            prep_hi(10)
            act.wait_ge(S["w3_ready"], 2)
            for c in range(BIT_CHUNKS):
                bit_sig(0, c)
                bit_high(0, c)
                if c < 3:
                    prep_hi(11 + c)
                elif c < 5:
                    ffn_weights_hi(c - 3)
            prep_hi(14)
            prep_hi(15)
            act.wait_ge(S["router_in"], 16)
            act.copy(router_hi[:, :, :], router_raw[:, :, :]).then_inc(S["router_hi"], 1)
            ctx_split_hi(0)
            ffn_weights_hi(2)
            ln_hi(0, "lna", xt_hi)
            queries_hi(0, 0)
            queries_hi(0, 1)
            exps(0, 0)
            exps(0, 1)
            for u in range(3, FFN_UNITS):
                ffn_weights_hi(u)
            with act.Fori(0, NB - 1) as b:
                batch(b, False)
            batch(NB - 1, True)

        @block.gpsimd
        def _(pool):
            def power(b, kind):
                pool.wait_ge(S[kind + "_ve"], b + 1)
                pool.tensor_tensor(ln_rstd[:, :], ln_ve[:, :], half_exp[:, 1, 0, :], ALU.pow
                                   ).then_inc(S[kind + "_pow"], 1)

            def q_roots(b0, b1):
                for sign in range(2):
                    last = pool.tensor_tensor(root0[:, sign, b0:b1, :], ratio0[:, sign, b0:b1, :],
                                              half_exp[:, sign, b0:b1, :], ALU.pow)
                last.then_inc(S["q_roots"], 1)

            def lnq_power(b0, b1):
                pool.wait_ge(S["lnq_ve"], 1 if b0 == 0 else 2)
                pool.tensor_tensor(lnq_rstd[:, b0:b1, :], lnq_rstd[:, b0:b1, :], half_exp[:, 1, b0:b1, :], ALU.pow
                                   ).then_inc(S["lnq_pow"], 1)

            def q_spread_diagonals(b, s):
                if s == 0:
                    pool.wait_ge(S["q_sis"], b + 1)
                    columns = [sis[:, i, k:k + 1] for i in range(2) for k in range(ND)]
                else:
                    pool.wait_ge(S["q_ratio"], b + 1)
                    pool.tensor_tensor(sis[:, :, 0], ratio1[:, :], half_exp[:, :, 0, 0], ALU.pow
                                       ).then_inc(S["q_root"], 1)
                    pool.wait_ge(S["q_root"], b + 1)
                    columns = [sis[:, i, 0:1] for i in range(2)]
                pool.nop(nofuse=True)
                for j, column in enumerate(columns):
                    last = pool.tensor_scalar(dg[:, j, :], ident[:, :], column, 1.0, ALU.mult, ALU.mult)
                last.then_inc(S["q_diag"], 1)

            def q_scale_diagonals(b, s):
                pool.wait_ge(S["q_scales"], 2 * b + s + 1)
                pool.nop(nofuse=True)
                for j in (2, 3):
                    last = pool.tensor_scalar(dg[:, j, :], ident[:, :], qscale[:, s, j:j + 1], 1.0, ALU.mult, ALU.mult)
                last.then_inc(S["q_wdiag"], 1)

            def q_gate_up(b):
                pool.wait_ge(S["q_hs"], b + 1)
                pool.tensor_tensor(act1[:, :, :], hs[:, :, 0:I], hs[:, :, I:2 * I], ALU.mult).then_inc(S["q_gu"], 1)

            def q_act(b):
                pool.wait_ge(S["q_gu"], b + 1)
                pool.wait_ge(S["q_sigm"], b + 1)
                pool.tensor_tensor(act1[:, :, :], act1[:, :, :], qw[:, 0:NT, 0:I], ALU.mult).then_inc(S["q_act"], 1)

            def normalise(b, h):
                pool.wait_ge(S["s_inv"], H * b + h + 1)
                pool.nop(nofuse=True)
                for t in range(NT):
                    row = prob[:, h % 2, t, :]
                    last = pool.tensor_scalar(row, row, row_inv[:, h % 2, t:t + 1], valid_b[:, 0:1],
                                              ALU.mult, ALU.mult)
                last.then_inc(S["s_norm"], 1)

            def bit_low(b, c):
                pool.wait_ge(S["bit_hi"], BIT_CHUNKS * b + c + 1)
                rows = P if c < BIT_FULL else BIT_REST
                pool.tensor_tensor(act_lo[0:rows, c % 3, :], act_raw[0:rows, c % 3, :],
                                   f32(act_hi[0:rows, c % 3, :]), ALU.subtract).then_inc(S["bit_lo"], 1)

            def ffn_low(b, c):
                pool.wait_ge(S["ffn_hi"], FFN_CHUNKS * b + c + 1)
                pool.tensor_tensor(act_lo[:, c % 3, :], act_raw[:, c % 3, :], f32(act_hi[:, c % 3, :]),
                                   ALU.subtract).then_inc(S["ffn_lo"], 1)

            def batch(b, last):
                for h in range(H):
                    if h + 1 < H:
                        normalise(b, h + 1)
                    if last:
                        continue
                    if h == 0:
                        q_spread_diagonals(b + 1, 0)
                    if h == 3:
                        q_scale_diagonals(b + 1, 0)
                    if h == 6:
                        q_gate_up(b + 1)
                    if h == 7:
                        q_act(b + 1)
                    if h == 9:
                        q_spread_diagonals(b + 1, 1)
                    if h == 11:
                        q_scale_diagonals(b + 1, 1)
                    if h == 14:
                        power(b + 1, "lnb")
                power(b, "lnf")
                if not last:
                    for c in range(BIT_CHUNKS):
                        bit_low(b + 1, c)
                    power(b + 1, "lna")
                for c in range(FFN_CHUNKS):
                    ffn_low(b, c)
                if not last:
                    normalise(b + 1, 0)

            pool.memset(ones[:, :], 1.0).then_inc(S["consts"], 1)
            pool.memset(gsum[:, :], 0.0)
            pool.memset(half_exp[:, 0, :, :], 0.5)
            pool.memset(half_exp[:, 1, :, :], -0.5)
            pool.wait_ge(S["consts"], 1)
            pool.affine_select(out=ident[:, :], in_=ones[:, :], compare_op=ALU.is_equal, fill=0.0, base=0,
                               pattern=[[-1, P]], channel_multiplier=1).then_inc(S["consts"], 1)
            pool.wait_ge(S["consts"], 2)
            lnq_power(0, 1)
            pool.wait_ge(S["q_ratio0"], 1)
            q_roots(0, 1)
            q_spread_diagonals(0, 0)
            q_scale_diagonals(0, 0)
            q_gate_up(0)
            q_act(0)
            lnq_power(1, NB)
            pool.wait_ge(S["lnq_pow"], 2)
            pool.wait_ge(S["x_in"], 16 * (NB - 1))
            pool.nop(nofuse=True)
            for b in range(1, NB):
                for t in range(NT):
                    last = pool.tensor_scalar(xn_next[:, (b - 1) * NT + t, :], x[:, b, t, :], lnq_mv[:, b, t, 0:1],
                                              lnq_rstd[:, b, t:t + 1], ALU.subtract, ALU.mult)
                if b == 1:
                    q_spread_diagonals(0, 1)
                if b == 2:
                    q_scale_diagonals(0, 1)
            last.then_inc(S["next_xn"], 1)
            power(0, "lnb")

            def ffn_weights_lo(u):
                pool.wait_ge(S["ffn_w_hi"], u + 1)
                pool.tensor_tensor(ffn_unit(u, LO), ffn_unit(u, RAW), f32(ffn_unit(u, HI)), ALU.subtract
                                   ).then_inc(S["ffn_w_lo_pool"], 1)

            for c in range(BIT_CHUNKS):
                bit_low(0, c)
            power(0, "lna")
            pool.wait_ge(S["q_ratio0"], 2)
            q_roots(1, NB)
            normalise(0, 0)
            for u in range(0, FFN_UNITS // 2):
                ffn_weights_lo(u)
            with pool.Fori(0, NB - 1) as b:
                batch(b, False)
            batch(NB - 1, True)

        @block.vector
        def _(dve):
            links = {"base": 0, "n": 0}

            def link(ins):
                links["n"] += 1
                ins.then_inc(S["dve_self"], 1)
                dve.wait_ge(S["dve_self"], links["base"] + links["n"])

            def hold():
                dve.nop(nofuse=True)

            def ln_stats_of(b, kind):
                hold()
                for t in range(NT):
                    last = dve.bn_stats(ln_stats[:, t, :], x[:, b, t, :])
                link(last)
                hold()
                for t in range(NT):
                    last = dve.bn_aggr(ln_mv[:, t, :], ln_stats[:, t, :])
                link(last)
                dve.tensor_scalar(ln_ve[:, :], ln_mv[:, :, 1], LN_EPS, None, ALU.add).then_inc(S[kind + "_ve"], 1)

            def ln_apply(b, kind):
                dve.wait_ge(S[kind + "_pow"], b + 1)
                for t in range(NT):
                    last = dve.tensor_scalar(xn[:, t, :], x[:, b, t, :], ln_mv[:, t, 0:1], ln_rstd[:, t:t + 1],
                                             ALU.subtract, ALU.mult)
                last.then_inc(S[kind + "_xn"], 1)

            def ln_lo(b, kind, hi, lo):
                dve.wait_ge(S[kind + "_hi"], b + 1)
                dve.tensor_tensor(lo[:, :, :].rearrange("p k t -> p (k t)"), bank["x0"][:, :],
                                  f32(hi[:, :, :].rearrange("p k t -> p (k t)")), ALU.subtract
                                  ).then_inc(S[kind + "_lo"], 1)

            def lnq_stats_of(batches):
                hold()
                for b in batches:
                    for t in range(NT):
                        last = dve.bn_stats(lnq_stats[:, b, t, :], x[:, b, t, :])
                link(last)
                hold()
                for b in batches:
                    for t in range(NT):
                        last = dve.bn_aggr(lnq_mv[:, b, t, :], lnq_stats[:, b, t, :])
                link(last)
                rows = slice(batches[0], batches[-1] + 1)
                dve.tensor_scalar(lnq_rstd[:, rows, :], lnq_mv[:, rows, :, 1], LN_EPS, None, ALU.add
                                  ).then_inc(S["lnq_ve"], 1)

            def lnq_apply(b, dst):
                for t in range(NT):
                    last = dve.tensor_scalar(dst[:, t, :], x[:, b, t, :], lnq_mv[:, b, t, 0:1],
                                             lnq_rstd[:, b, t:t + 1], ALU.subtract, ALU.mult)
                return last

            def q_amax0_x(b, src):
                return dve.tensor_reduce(amax0[:, 0, b, :], src[:, :].rearrange("p (k t) -> p k t", k=ND), AX.X,
                                         ALU.max, apply_absolute_value=True)

            def q_amax0_w(b):
                return dve.tensor_reduce(amax0[:, 1, b, :], guT[:, b, :, :], AX.X, ALU.max,
                                         apply_absolute_value=True)

            def q_ratio0(b0, b1):
                ax, aw = amax0[:, 0, b0:b1, :], amax0[:, 1, b0:b1, :]
                link(dve.tensor_scalar(amax0[:, :, b0:b1, :], amax0[:, :, b0:b1, :], Q_EPS, None, ALU.max))
                link(dve.reciprocal(aw, aw))
                link(dve.tensor_tensor(ax, ax, aw, ALU.mult))
                for sign in range(2):
                    last = dve.tensor_scalar(ratio0[:, sign, b0:b1, :], ax, Q_EPS * Q_EPS, None, ALU.max)
                last.then_inc(S["q_ratio0"], 1)

            def q_take(b):
                if isinstance(b, int):
                    dve.wait_ge(S["q_roots"], 1)
                dve.tensor_copy(sis[:, :, :], root0[:, :, b, :]).then_inc(S["q_sis"], 1)

            def q_ratio1(b):
                dve.wait_ge(S["q_xt"], b + 1)
                link(dve.tensor_reduce(amax1[:, 0:1], bank["x0"][:, 0:T], AX.X, ALU.max, apply_absolute_value=True))
                link(dve.tensor_scalar(amax1[:, :], amax1[:, :], Q_EPS, None, ALU.max))
                link(dve.reciprocal(amax1[:, 1:2], amax1[:, 1:2]))
                link(dve.tensor_tensor(amax1[:, 0:1], amax1[:, 0:1], amax1[:, 1:2], ALU.mult))
                for sign in range(2):
                    last = dve.tensor_scalar(ratio1[:, sign:sign + 1], amax1[:, 0:1], Q_EPS * Q_EPS, None, ALU.max)
                last.then_inc(S["q_ratio"], 1)

            def q_ctx_amax(b):
                dve.wait_ge(S["cx_in"], 32 * (b + 1))
                dve.tensor_reduce(amax1[:, 1:2], cxT[:, :], AX.X, ALU.max, apply_absolute_value=True)

            def q_scaled_w(b, s):
                if s == 0:
                    dve.wait_ge(S["gu_in"], 16 * (b + 1))
                dve.wait_ge(S["q_spread"], 2 * b + s + 1)
                w = D if s == 0 else I
                s_row = (bank["x0"] if s == 0 else bank["x1"])[:, 0:w]
                for j in range(2):
                    dve.tensor_tensor(qw[:, 2 + j, 0:w], gu[:, j, :] if s == 0 else cx[:, j, :], s_row, ALU.mult)

            def q_scaled_x(b, s):
                w = D if s == 0 else I
                inv_row = (bank["x0"] if s == 0 else bank["x1"])[:, w:2 * w]
                for j in range(2):
                    last = dve.tensor_tensor(qw[:, j, 0:w], xn[:, j, :] if s == 0 else act1[:, j, :], inv_row, ALU.mult)
                link(last)

            def q_scales(b, s):
                w = D if s == 0 else I
                link(dve.tensor_reduce(rowmax[:, :], qw[:, :, 0:w], AX.X, ALU.max, apply_absolute_value=True))
                link(dve.tensor_scalar(qscale[:, s, :], rowmax[:, :], Q_EPS, 1.0 / QMAX, ALU.max, ALU.mult))
                dve.reciprocal(qrecip[:, :], qscale[:, s, :]).then_inc(S["q_scales"], 1)

            def q_bf_w(b):
                dve.wait_ge(S["q_turned"], 2 * b + 1)
                dve.tensor_scalar(qT[:, 2:4, :].rearrange("p a n -> p (a n)"), bank["x1"][:, :], -MAGIC, None, ALU.add
                                  ).then_inc(S["q_bf_w"], 1)

            def q_dequant(b, s):
                dve.wait_ge(S["q_wscale"], 2 * b + s + 1)
                for t in range(NT):
                    last = dve.scalar_tensor_tensor(out=hs[:, t, :], in0=bank["x0"][:, t * D:(t + 1) * D],
                                                    scalar=qscale[:, s, t:t + 1], in1=wscale[:, :],
                                                    op0=ALU.mult, op1=ALU.mult)
                return last

            def q_sigmoid(b):
                dve.wait_ge(S["q_tanh"], b + 1)
                e = qw[:, 0:NT, 0:I]
                dve.tensor_scalar(e, e, 0.5, 0.5, ALU.mult, ALU.add).then_inc(S["q_sigm"], 1)

            def q_residual(b):
                link(q_dequant(b, 1))
                link(dve.tensor_tensor(x[:, b, :, :], x[:, b, :, :], hs[:, :, :], ALU.add))

            def bit_act(b, c):
                n = BIT_CHUNKS * b + c + 1
                dve.wait_ge(S["bit_sig"], n)
                src, r = CHUNK_BANKS[c % 3], c % 3
                if c < BIT_FULL:
                    rows = P
                    last = dve.tensor_tensor(act_raw[:, r, :], sig[:, r, :], src[:, T:2 * T], ALU.mult)
                else:
                    rows = BIT_REST
                    last = dve.tensor_tensor(act_raw[0:rows, r, :], sig[rows:P, r, :], src[rows:P, 0:T], ALU.mult)
                last.then_inc(S["bit_prod"], 1)

            def add_bank(b, which, done):
                dve.tensor_tensor(x[:, b, :, :].rearrange("p t d -> p (t d)"), bank[which][:, :],
                                  x[:, b, :, :].rearrange("p t d -> p (t d)"), ALU.add).then_inc(S[done], 1)

            def bit_residual(b):
                dve.wait_ge(S["bit_y"], BIT_CHUNKS * (b + 1))
                add_bank(b, "u", "bit_x")
                dve.wait_ge(S["bit_x"], b + 1)

            def ctx_split_lo(b):
                dve.wait_ge(S["ctx_hi"], b + 1)
                dve.tensor_tensor(cx_lo[:, :, :], cx[:, :, :], f32(cx_hi[:, :, :]), ALU.subtract)
                dve.tensor_tensor(cxT_lo[:, :], cxT[:, :], f32(cxT_hi[:, :]), ALU.subtract).then_inc(S["ctx_lo"], 1)

            def mask_row(b):
                dve.wait_ge(S["mask_in"], 16 * (b + 1))
                dve.tensor_reduce(valid_b[:, :], mask8[:, :], AX.X, ALU.max)
                dve.tensor_scalar(masked[:, :], mask8[:, :], -MASKED, MASKED, ALU.mult, ALU.add
                                  ).then_inc(S["mask_row"], 1)

            def queries_lo(b, p):
                dve.wait_ge(S["qa_h"], PAIRS * b + p + 1)
                dve.tensor_tensor(qa_lo[:, p % 2, :], bank["qa"][:, :], f32(qa_hi[:, p % 2, :]), ALU.subtract
                                  ).then_inc(S["qa_l"], 1)

            def row_minima(b, h):
                if h == 0:
                    dve.wait_ge(S["mask_row"], b + 1)
                dve.wait_ge(S["s_mm"], H * b + h + 1)
                hold()
                src = bank["s0"] if h % 2 == 0 else bank["s1"]
                for t in range(NT):
                    last = dve.tensor_tensor_reduce(out=prob[:, h % 2, t, :], in0=src[:, t * T:(t + 1) * T],
                                                    in1=masked[:, :], scale=1.0, scalar=3.0e38, op0=ALU.add,
                                                    op1=ALU.min, accum_out=row_min[:, h % 2, t:t + 1])
                last.then_inc(S["s_min"], 1)

            def row_inverses(b, h):
                dve.wait_ge(S["s_exp"], H * b + h + 1)
                dve.reciprocal(row_inv[:, h % 2, :], row_sum[:, h % 2, :]).then_inc(S["s_inv"], 1)

            def probs_lo(b, h):
                dve.wait_ge(S["t_h"], H * b + h + 1)
                dve.tensor_tensor(pt_lo[:, :, :].rearrange("p s t -> p (s t)"), bank["pt"][:, :],
                                  f32(pt_hi[:, :, :].rearrange("p s t -> p (s t)")), ALU.subtract
                                  ).then_inc(S["t_l"], 1)

            def mix_lo(b, h):
                dve.wait_ge(S["u_h"], H * b + h + 1)
                dve.tensor_tensor(ut_lo[:, :], bank["u"][:, 0:T], f32(ut_hi[:, :]), ALU.subtract
                                  ).then_inc(S["u_l"], 1)

            def attention(b, beside):
                for h in range(H):
                    if h >= 1:
                        mix_lo(b, h - 1)
                    if h + 1 < H:
                        row_inverses(b, h + 1)
                    probs_lo(b, h)
                    if h + 2 < H:
                        row_minima(b, h + 2)
                    if h % 2 == 1 and h + 3 < H:
                        queries_lo(b, (h + 3) // 2)
                    beside(h)

            def ffn_act(b, c):
                n = FFN_CHUNKS * b + c + 1
                dve.wait_ge(S["ffn_sig"], n)
                src, r = CHUNK_BANKS[c % 3], c % 3
                link(dve.tensor_tensor(sig[:, r, :], sig[:, r, :], src[:, 0:T], ALU.mult))
                dve.tensor_tensor(act_raw[:, r, :], sig[:, r, :], src[:, T:2 * T], ALU.mult
                                  ).then_inc(S["ffn_prod"], 1)

            def route_top(b):
                dve.wait_ge(S["route_mm"], b + 1)
                hold()
                for t in range(NT):
                    last = dve.max(top8[:, t, :], bank["x1"][:, t * NR:(t + 1) * NR])
                link(last)
                dve.tensor_tensor(top_d[:, :, 0:1], top8[:, :, 0:1], top8[:, :, 1:2], ALU.subtract)
                dve.tensor_tensor(top_d[:, :, 1:2], top8[:, :, 1:2], top8[:, :, 0:1], ALU.subtract
                                  ).then_inc(S["route_d"], 1)

            def route_sum(b):
                dve.wait_ge(S["route_sig"], b + 1)
                link(dve.tensor_tensor(comb[:, :], top_w[:, :, 0], top_w[:, :, 1], ALU.add))

            def ffn_residual(b):
                dve.wait_ge(S["ffn_y"], FFN_CHUNKS * (b + 1))
                for t in range(NT):
                    last = dve.scalar_tensor_tensor(out=x[:, b, t, :], in0=bank["o"][:, t * D:(t + 1) * D],
                                                    scalar=comb[:, t:t + 1], in1=x[:, b, t, :],
                                                    op0=ALU.mult, op1=ALU.add)
                link(last)
                add_bank(b, "u", "ffn_x")

            def batch(b, last):
                nxt = b + 1

                def beside(h):
                    if last:
                        return
                    if h == 0:
                        q_take(nxt)
                        lnq_apply(nxt, xn)
                    elif h == 1:
                        q_scaled_w(nxt, 0)
                    elif h == 2:
                        q_scaled_x(nxt, 0)
                        q_scales(nxt, 0)
                    elif h == 3:
                        q_ctx_amax(nxt)
                    elif h == 4:
                        q_bf_w(nxt)
                    elif h == 6:
                        q_dequant(nxt, 0).then_inc(S["q_hs"], 1)
                    elif h == 7:
                        q_sigmoid(nxt)
                    elif h == 8:
                        q_ratio1(nxt)
                    elif h == 10:
                        q_scaled_w(nxt, 1)
                        q_scaled_x(nxt, 1)
                        q_scales(nxt, 1)
                    elif h == 13:
                        q_residual(nxt)
                    elif h == 14:
                        ln_stats_of(nxt, "lnb")
                    elif h == 15:
                        ln_apply(nxt, "lnb")

                attention(b, beside)
                if not last:
                    ln_lo(nxt, "lnb", xt_hi, xt_lo)
                mix_lo(b, H - 1)
                dve.wait_ge(S["o_mm"], H * (b + 1))
                add_bank(b, "o", "att_x")
                dve.wait_ge(S["att_x"], b + 1)
                ln_stats_of(b, "lnf")
                if not last:
                    bit_act(nxt, 0)
                ln_apply(b, "lnf")
                if not last:
                    bit_act(nxt, 1)
                    bit_act(nxt, 2)
                    mask_row(nxt)
                    bit_act(nxt, 3)
                    ctx_split_lo(nxt)
                    bit_act(nxt, 4)
                ln_lo(b, "lnf", yt_hi, yt_lo)
                if not last:
                    bit_act(nxt, 5)
                    bit_residual(nxt)
                    ln_stats_of(nxt, "lna")
                ffn_act(b, 0)
                if not last:
                    ln_apply(nxt, "lna")
                route_top(b)
                for c in range(1, FFN_CHUNKS):
                    ffn_act(b, c)
                    if c == 2:
                        route_sum(b)
                    if not last:
                        if c == 3:
                            ln_lo(nxt, "lna", xt_hi, xt_lo)
                        if c == 5:
                            queries_lo(nxt, 0)
                        if c == 6:
                            queries_lo(nxt, 1)
                if not last:
                    row_minima(nxt, 0)
                    row_minima(nxt, 1)
                    row_inverses(nxt, 0)
                ffn_residual(b)

            def prep_lo(k):
                dve.wait_ge(S["prep_hi"], k + 1)
                p = k // 2
                lo, hi = ((t[:, 2 * p:2 * p + 2, :, :].rearrange("p h s c -> p (h s c)") for t in (a_lo, a_hi))
                          if k % 2 == 0 else
                          (t[:, 2 * p:2 * p + 2, :].rearrange("p h d -> p (h d)") for t in (c_lo, c_hi)))
                dve.scalar_tensor_tensor(out=lo, in0=PREP_BANKS[k % 2][:, :], scalar=-SCALE if k % 2 == 0 else 1.0,
                                         in1=f32(hi), op0=ALU.mult, op1=ALU.subtract).then_inc(S["prep_lo"], 1)

            def ternary_scales():
                dve.wait_ge(S["gamma_mm"], 1)
                link(dve.tensor_scalar(gam[:, :], bank["u"][:, 0:4], 1.0 / (BIT * D), None, ALU.mult))
                link(dve.tensor_tensor(gam[:, 2:3], gam[:, 2:3], gam[:, 3:4], ALU.add))
                link(dve.tensor_scalar(gam[:, 0:3], gam[:, 0:3], BIT_EPS, None, ALU.add))
                link(dve.reciprocal(gam[:, 0:3], gam[:, 0:3]))

            def ternary(part):
                lo, hi = MAGIC - 1.0, MAGIC + 1.0
                if part == 0:
                    for j in range(2):
                        w = w12_raw[:, :, j * BIT:(j + 1) * BIT]
                        last = dve.tensor_scalar(w, w, gam[:, j:j + 1], MAGIC, ALU.mult, ALU.add)
                    link(last)
                elif part == 1:
                    dve.tensor_scalar(w12_raw[:, :, :], w12_raw[:, :, :], hi, lo, ALU.min, ALU.max
                                      ).then_inc(S["bit_q12"], 1)
                else:
                    main, rest = w3_raw[:, 0:BIT_FULL, :], w3_raw[0:BIT_REST, BIT_FULL, :]
                    dve.tensor_scalar(main, main, gam[:, 2:3], MAGIC, ALU.mult, ALU.add)
                    link(dve.tensor_scalar(rest, rest, gam[0:BIT_REST, 2:3], MAGIC, ALU.mult, ALU.add))
                    dve.tensor_scalar(main, main, hi, lo, ALU.min, ALU.max)
                    dve.tensor_scalar(rest, rest, hi, lo, ALU.min, ALU.max).then_inc(S["bit_q3"], 1)

            dve.wait_ge(S["x0_in"], 16)
            lnq_stats_of([0])
            dve.wait_ge(S["lnq_pow"], 1)
            lnq_apply(0, xn).then_inc(S["lnq_xn"], 1)
            dve.wait_ge(S["guT0_in"], 16)
            q_amax0_w(0)
            dve.wait_ge(S["q0_xt"], 1)
            link(q_amax0_x(0, bank["x0"]))
            q_ratio0(0, 1)
            q_take(0)
            q_ctx_amax(0)
            prep_lo(0)
            q_scaled_w(0, 0)
            q_scaled_x(0, 0)
            q_scales(0, 0)
            prep_lo(1)
            prep_lo(2)
            prep_lo(3)
            q_bf_w(0)
            dve.wait_ge(S["x_in"], 16 * (NB - 1))
            lnq_stats_of(range(1, NB))
            q_dequant(0, 0).then_inc(S["q_hs"], 1)
            q_sigmoid(0)
            q_ratio1(0)
            ternary_scales()
            prep_lo(4)
            prep_lo(5)
            q_scaled_w(0, 1)
            q_scaled_x(0, 1)
            q_scales(0, 1)
            prep_lo(6)
            ternary(0)
            prep_lo(7)
            ternary(1)
            q_residual(0)
            ln_stats_of(0, "lnb")
            prep_lo(8)
            ln_apply(0, "lnb")
            ternary(2)
            ln_lo(0, "lnb", xt_hi, xt_lo)
            prep_lo(9)
            dve.wait_ge(S["next_turned"], 1)
            for b in range(1, NB):
                last = q_amax0_x(b, NEXT_BANKS[b - 1])
            last.then_inc(S["next_read"], 1)
            prep_lo(10)

            def ffn_weights_lo(u):
                dve.wait_ge(S["ffn_w_hi"], u + 1)
                dve.tensor_tensor(ffn_unit(u, LO), ffn_unit(u, RAW), f32(ffn_unit(u, HI)), ALU.subtract
                                  ).then_inc(S["ffn_w_lo_dve"], 1)

            for c in range(BIT_CHUNKS):
                bit_act(0, c)
                if c < 3:
                    prep_lo(11 + c)
                elif c < 5:
                    if c == 3:
                        dve.wait_ge(S["guT_in"], 16 * (NB - 1))
                    q_amax0_w(c - 2)
            bit_residual(0)
            ln_stats_of(0, "lna")
            prep_lo(14)
            ln_apply(0, "lna")
            prep_lo(15)
            link(q_amax0_w(3))
            q_ratio0(1, NB)
            mask_row(0)
            ctx_split_lo(0)
            dve.wait_ge(S["router_hi"], 1)
            dve.tensor_tensor(router_lo[:, :, :], router_raw[:, :, :], f32(router_hi[:, :, :]), ALU.subtract
                              ).then_inc(S["router_lo"], 1)
            ln_lo(0, "lna", xt_hi, xt_lo)
            queries_lo(0, 0)
            queries_lo(0, 1)
            row_minima(0, 0)
            row_minima(0, 1)
            row_inverses(0, 0)
            for u in range(FFN_UNITS // 2, FFN_UNITS):
                ffn_weights_lo(u)
            dve.wait_ge(S["q_roots"], 2)
            start = links["n"]
            with dve.Fori(0, NB - 1) as b:
                links["base"], links["n"] = b * LINKS + start, 0
                batch(b, False)
                assert links["n"] == LINKS, links["n"]
            links["base"], links["n"] = start + (NB - 1) * LINKS, 0
            batch(NB - 1, True)


def kernel(**inputs):
    import numpy as np
    import concourse.bacc as bacc
    from concourse.bass_utils import run_bass_kernel_spmd

    def t(a):
        return np.ascontiguousarray(np.swapaxes(np.asarray(a), -1, -2))

    w1T, w2T = t(inputs["L0_ffn_w1"]), t(inputs["L0_ffn_w2"])
    full = BIT_FULL * P
    layout = {
        "x": inputs["x"],
        "gu": inputs["fside_BxS2xS2_0"],
        "guT": t(inputs["fside_BxS2xS2_0"]),
        "ctx": inputs["ctx_1024"],
        "ctxT": t(inputs["ctx_1024"]),
        "mask": np.asarray(inputs["mask_BxS2_bf1"]).view(np.uint8),
        "w12T": np.concatenate([w1T, w2T[:, full:], w2T[:, :full]], axis=1),
        "w3T": t(inputs["L0_ffn_w3"]),
        "wqT": t(inputs["L1_xattn_Wq"]),
        "wkT": t(inputs["L1_xattn_Wk"]),
        "wvT": t(inputs["L1_xattn_Wv"]),
        "wo": inputs["L1_xattn_Wo"],
        "routerT": t(inputs["L1_ffn_router_weight"]),
        "gateT": np.concatenate([t(inputs["L1_ffn_sh_gate"]), t(inputs["L1_ffn_r_gate"])], axis=1),
        "upT": np.concatenate([t(inputs["L1_ffn_sh_up"]), t(inputs["L1_ffn_r_up"])], axis=1),
        "downT": np.concatenate([t(inputs["L1_ffn_sh_down"]), t(inputs["L1_ffn_r_down"])], axis=0)
                   .reshape(FFN_CHUNKS, P, D).transpose(1, 0, 2).reshape(FFN, D),
    }
    nc = bacc.Bacc("TRN2", target_bir_lowering=False, num_devices=1)
    arrays, args = {}, []
    for name, a in layout.items():
        a = np.ascontiguousarray(a)
        arrays[f"in_{name}"] = a
        args.append(nc.dram_tensor(f"in_{name}", a.shape, mybir.dt.from_np(a.dtype), kind="ExternalInput").ap())
    args.append(nc.dram_tensor("out_x", (NB, T, D), F32, kind="ExternalOutput").ap())
    build(nc, *args)
    return run_bass_kernel_spmd(nc, [arrays], core_ids=[0]).results[0]["out_x"]
```

```python
from contextlib import ExitStack

import concourse.bass as bass
from concourse import mybir

F32 = mybir.dt.float32
F32R = mybir.dt.float32r
BF16 = mybir.dt.bfloat16
U8 = mybir.dt.uint8
ALU = mybir.AluOpType
ACT = mybir.ActivationFunctionType
AX = mybir.AxisListType

P = 128
NB, T, D = 4, 256, 256
NT, ND = T // P, D // P
I = 128
H, DH = 16, 128
PAIRS = H // 2
BIT = 704
BIT_FULL = BIT // P
BIT_REST = BIT - BIT_FULL * P
BIT_CHUNKS = BIT_FULL + 1
INTER, ROUTED = 1024, 128
FFN = INTER + ROUTED
FFN_CHUNKS = FFN // P
NR = 8
LN_EPS, Q_EPS, BIT_EPS = 1e-5, 1e-6, 1e-8
QMAX = 127.0
MAGIC = 1.5 * 2.0 ** 23
MASKED = 1e30
SCALE = float(DH) ** -0.5
LINKS = 29
ATT_UNITS = 2 * PAIRS
WQ_LOADS = 4
ROUTE_LATE = 3
FFN_UNITS = 6
FFN_LO_POOL, FFN_LO_DVE = (0, 1, 3, 5), (2, 4)


def build(nc, x_in, gu_in, guT_in, ctx_in, ctxT_in, mask_in, w12T_in, w3T_in, wqT_in, wkT_in,
          wvT_in, wo_in, routerT_in, gateT_in, upT_in, downT_in, out):
    with ExitStack() as ctx:
        def sb(name, shape, dt=F32, stack=ctx):
            return stack.enter_context(nc.sbuf_tensor(name, shape, dt))

        def sem(name):
            return ctx.enter_context(nc.semaphore(name))

        bank = {n: ctx.enter_context(nc.psum_tensor("bank_" + n, [P, 512], F32))
                for n in ("qa", "s0", "s1", "pt", "u", "o", "x0", "x1")}
        CHUNK_BANKS = (bank["s0"], bank["s1"], bank["pt"])
        NEXT_BANKS = (bank["x1"], bank["u"], bank["pt"])
        PREP_BANKS = (bank["qa"], bank["o"])

        with ExitStack() as raw:
            wq_raw = sb("wq_raw", [P, H, D], F32, raw)
            wo_raw = sb("wo_raw", [P, H, D], F32, raw)
            gate_raw = sb("gate_raw", [P, ND, FFN], F32, raw)
            up_raw = sb("up_raw", [P, ND, FFN], F32, raw)
            down_raw = sb("down_raw", [P, FFN_CHUNKS, D], F32, raw)
            xn_next = sb("xn_next", [P, H, D], F32, raw)[:, H - (NB - 1) * NT:H, :]
        a_lo = sb("a_lo", [P, H, ND, P], F32R)
        c_lo = sb("c_lo", [P, H, D], F32R)
        gate_lo = sb("gate_lo", [P, ND, FFN], F32R)
        up_lo = sb("up_lo", [P, ND, FFN], F32R)
        down_lo = sb("down_lo", [P, FFN_CHUNKS, D], F32R)
        c_hi = sb("c_hi", [P, H, D], F32R)
        a_hi = sb("a_hi", [P, H, ND, P], F32R)
        gate_hi = sb("gate_hi", [P, ND, FFN], F32R)
        up_hi = sb("up_hi", [P, ND, FFN], F32R)
        down_hi = sb("down_hi", [P, FFN_CHUNKS, D], F32R)
        RAW, HI, LO = (gate_raw, up_raw, down_raw), (gate_hi, up_hi, down_hi), (gate_lo, up_lo, down_lo)
        router_raw = sb("router_raw", [P, ND, NR])
        router_hi = sb("router_hi", [P, ND, NR], F32R)
        router_lo = sb("router_lo", [P, ND, NR], F32R)
        w12 = sb("w12", [P, ND, 2 * BIT], F32R)
        w3 = sb("w3", [P, BIT_CHUNKS, D], F32R)

        ident = sb("ident", [P, P])
        ones = sb("ones", [P, P])
        half_exp = sb("half_exp", [P, 2, NB, ND])
        x = sb("x", [P, NB, NT, D])
        mask8 = sb("mask8", [P, T], U8)
        valid_b = sb("valid_b", [P, 1])
        masked = sb("masked", [P, T])
        ln_stats = sb("ln_stats", [P, NT, 6])
        ln_mv = sb("ln_mv", [P, NT, 2])
        ln_ve = sb("ln_ve", [P, NT])
        ln_rstd = sb("ln_rstd", [P, NT])
        xn = sb("xn", [P, NT, D])
        xt_hi = sb("xt_hi", [P, ND, T], F32R)
        xt_lo = sb("xt_lo", [P, ND, T], F32R)
        gu = sb("gu", [P, 2, D])
        cx = sb("cx", [P, 2, I])
        cxT = sb("cxT", [P, T])
        qw = sb("qw", [P, 4, D])
        dg = sb("dg", [P, 4, P])
        amax0 = sb("amax0", [P, 2, NB, ND])
        ratio0 = sb("ratio0", [P, 2, NB, ND])
        root0 = sb("root0", [P, 2, NB, ND])
        lnq_stats = sb("lnq_stats", [P, NB, NT, 6])
        lnq_mv = sb("lnq_mv", [P, NB, NT, 2])
        lnq_rstd = sb("lnq_rstd", [P, NB, NT])
        lnq_shift = sb("lnq_shift", [P, NB, NT])
        amax1 = sb("amax1", [P, 2])
        ratio1 = sb("ratio1", [P, 2])
        sis = sb("sis", [P, 2, ND])
        rowmax = sb("rowmax", [P, 4])
        qscale = sb("qscale", [P, 2, 4])
        qrecip = sb("qrecip", [P, 4])
        qT = sb("qT", [P, 4, D], BF16)
        wscale = sb("wscale", [P, D])
        hs = sb("hs", [P, NT, D])
        act1 = hs[:, :, I:2 * I]
        cx_hi = sb("cx_hi", [P, 2, I], F32R)
        cx_lo = sb("cx_lo", [P, 2, I], F32R)
        cxT_hi = sb("cxT_hi", [P, T], F32R)
        cxT_lo = sb("cxT_lo", [P, T], F32R)
        row_min = sb("row_min", [P, 2, NT])
        row_sum = sb("row_sum", [P, 2, NT])
        row_inv = sb("row_inv", [P, 2, NT])
        gsum = sb("gsum", [P, 4])
        gam = sb("gam", [P, 4])
        top8 = sb("top8", [P, NT, NR])
        top_d = sb("top_d", [P, NT, 2])
        top_w = sb("top_w", [P, NT, 2])
        comb = sb("comb", [P, NT])

        with ExitStack() as first:
            guT = sb("guT", [P, NB, ND, 2 * I], F32, first)
            w12_raw = sb("w12_raw", [P, ND, 2 * BIT], F32, first)
            w3_raw = sb("w3_raw", [P, BIT_CHUNKS, D], F32, first)
            wkT = sb("wkT", [P, PAIRS, P], F32, first)
            wvT = sb("wvT", [P, PAIRS, P], F32, first)
        qa_hi = sb("qa_hi", [P, 2, 2 * T], F32R)
        qa_lo = sb("qa_lo", [P, 2, 2 * T], F32R)
        ut_hi = sb("ut_hi", [P, T], F32R)
        prob = sb("prob", [P, 2, NT, T])
        act_raw = sb("act_raw", [P, 3, T])
        act_hi = sb("act_hi", [P, 3, T], F32R)
        act_lo = sb("act_lo", [P, 3, T], F32R)
        sig = sb("sig", [P, 3, T])
        pt_hi = sb("pt_hi", [P, 2, T], F32R)
        pt_lo = sb("pt_lo", [P, 2, T], F32R)
        yt_hi = sb("yt_hi", [P, ND, T], F32R)
        yt_lo = sb("yt_lo", [P, ND, T], F32R)
        ut_lo = sb("ut_lo", [P, T], F32R)

        S = {}
        for n in """consts x0_in x_in mask_in gu_in guT0_in guT_in cx_in w12_in w3_in wk_in wv_in router_in out_done
                    abs_done gamma_mm gamma_inv bit_q12 bit_r3 bit_q3 w12_ready w3_ready
                    prep_mm prep_hi prep_lo ffn_w_hi ffn_w_lo_pool ffn_w_lo_dve router_hi router_lo
                    lnq_ve lnq_pow q_ratio0 lnq_xn lnq_shift next_xn next_turned next_read q_roots q_sis
                    lnb_ve lnb_pow lnb_xn lna_ve lna_pow lna_xn lnf_ve lnf_pow lnf_xn
                    lnb_t lnb_hi lnb_lo lna_t lna_hi lna_lo lnf_t lnf_hi lnf_lo
                    q0_xt q_xt q_ratio q_root q_diag q_spread q_scales q_rounded q0_rounded_w q_wdiag q_turned q_bf q_bf_w
                    q_prod q_wscale q_hs q_tanh q_gu q_sigm q_act q_out q_x dve_self
                    bit_mm bit_sig bit_prod bit_hi bit_lo bit_y bit_x
                    ctx_hi ctx_lo mask_row
                    qa_mm qa_h qa_l s_mm s_min s_exp s_inv s_norm t_mm t_h t_l u_mm u_h u_l o_mm
                    att_x route_mm route_d route_sig route_w
                    ffn_mm ffn_sig ffn_prod ffn_hi ffn_lo ffn_lo_last ffn_y shared_x ffn_x""".split():
            S[n] = sem(n)
        for i in range(WQ_LOADS):
            for n in ("wq", "wo"):
                S[f"{n}{i}"] = sem(f"{n}{i}_in")
        for i in range(FFN_UNITS):
            S[f"ffn_w{i}"] = sem(f"ffn_w{i}_in")

        def f32(ap):
            return ap.bitcast(F32)

        def ffn_unit(u, tensors):
            which, half = u // 2, u % 2
            t = tensors[which]
            if which < 2:
                return t[:, half, :]
            n = FFN_CHUNKS * D // 2
            return t[:, :, :].rearrange("p c d -> p (c d)")[:, half * n:(half + 1) * n]

        block = ctx.enter_context(nc.Block())

        @block.sync
        def _(sp):
            def expert_weights(b):
                if not (isinstance(b, int) and b == 0):
                    sp.wait_ge(S["q_rounded"], 2 * b)
                    sp.wait_ge(S["ctx_lo"], b)
                    sp.wait_ge(S["mask_row"], b)
                sp.dma_start(gu[:, :, :], gu_in[b].rearrange("(o p) d -> p o d", p=P)).then_inc(S["gu_in"], 16)
                sp.dma_start(cx[:, :, :], ctx_in[b].rearrange("(o p) d -> p o d", p=P)).then_inc(S["cx_in"], 16)
                sp.dma_start(cxT[:, :], ctxT_in[b]).then_inc(S["cx_in"], 16)
                sp.dma_start(mask8[:, :], mask_in[b].partition_broadcast(P)).then_inc(S["mask_in"], 16)

            def turned_expert_weights(b, done):
                sp.dma_start(guT[:, b, :, :], guT_in[b].rearrange("(k p) o -> p k o", p=P)).then_inc(S[done], 16)

            def x_rows(dram, b):
                return dram[b].rearrange("(t p) d -> p t d", p=P)

            def store(b):
                sp.wait_ge(S["ffn_x"], b + 1)
                sp.dma_start(x_rows(out, b), x[:, b, :, :]).then_inc(S["out_done"], 16)

            sp.dma_start(x[:, 0, :, :], x_rows(x_in, 0)).then_inc(S["x0_in"], 16)
            turned_expert_weights(0, "guT0_in")
            expert_weights(0)
            def attention_weights(i):
                n = H // WQ_LOADS
                for name, raw, dram in (("wq", wq_raw, wqT_in), ("wo", wo_raw, wo_in)):
                    if i == 0:
                        kv, kv_in = (wkT, wkT_in) if name == "wq" else (wvT, wvT_in)
                        sp.dma_start(kv[:, :, :], kv_in.rearrange("(g p) d -> p g d", p=P)
                                     ).then_inc(S["wk_in" if name == "wq" else "wv_in"], 16)
                    sp.dma_start(raw[:, i * n:(i + 1) * n, :],
                                 dram[i * n * P:(i + 1) * n * P].rearrange("(h p) d -> p h d", p=P)
                                 ).then_inc(S[f"{name}{i}"], 16)

            attention_weights(0)
            for b in range(1, NB):
                sp.dma_start(x[:, b, :, :], x_rows(x_in, b)).then_inc(S["x_in"], 16)
            sp.dma_start(w12_raw[:, :, :], w12T_in.rearrange("(k p) n -> p k n", p=P)).then_inc(S["w12_in"], 16)
            attention_weights(1)
            sp.dma_start(w3_raw[:, 0:BIT_FULL, :], w3T_in[0:BIT_FULL * P].rearrange("(c p) d -> p c d", p=P)
                         ).then_inc(S["w3_in"], 16)
            sp.dma_start(w3_raw[0:BIT_REST, BIT_FULL, :], w3T_in[BIT_FULL * P:BIT]).then_inc(S["w3_in"], 16)
            for b in range(1, NB):
                turned_expert_weights(b, "guT_in")
            attention_weights(2)
            attention_weights(3)
            sp.dma_start(router_raw[:, :, :], routerT_in.rearrange("(k p) n -> p k n", p=P)
                         ).then_inc(S["router_in"], 16)
            for u in range(FFN_UNITS):
                which, half = u // 2, u % 2
                n = FFN_CHUNKS * D // 2
                src = ((gateT_in, upT_in)[which][half * P:(half + 1) * P, :] if which < 2 else
                       downT_in.rearrange("(p c) d -> p (c d)", p=P)[:, half * n:(half + 1) * n])
                sp.dma_start(ffn_unit(u, RAW), src).then_inc(S[f"ffn_w{u}"], 16)
            with sp.Fori(0, NB - 1) as b:
                expert_weights(b + 1)
                store(b)
            store(NB - 1)
            sp.wait_ge(S["out_done"], 16 * NB)

        @block.tensor
        def _(pe):
            def split_mm(out_ap, w_hi, w_lo, r_hi, r_lo, start, stop):
                passes = [(w_hi, r_hi), (w_hi, r_lo), (w_lo, r_hi)]
                passes = [(w, r) for w, r in passes if w is not None and r is not None]
                for n, (w, r) in enumerate(passes):
                    last = pe.matmul(out_ap, w, r, start=start and n == 0, stop=stop and n == len(passes) - 1,
                                     skip_group_check=True)
                return last

            def turn_xn(dst):
                for t in range(NT):
                    for k in range(ND):
                        last = pe.transpose(dst[:, k * T + t * P:k * T + (t + 1) * P],
                                            xn[:, t, k * P:(k + 1) * P], ident[:, :])
                return last

            def q_turn_x0():
                pe.wait_ge(S["lnq_xn"], 1)
                turn_xn(bank["x0"]).then_inc(S["q0_xt"], 1)

            def q_turn_next():
                pe.wait_ge(S["q_wscale"], 2)
                pe.wait_ge(S["next_xn"], 1)
                for b in range(1, NB):
                    for t in range(NT):
                        for k in range(ND):
                            last = pe.transpose(NEXT_BANKS[b - 1][:, k * T + t * P:k * T + (t + 1) * P],
                                                xn_next[:, (b - 1) * NT + t, k * P:(k + 1) * P], ident[:, :])
                last.then_inc(S["next_turned"], 1)

            def q_spread(b, s):
                pe.wait_ge(S["q_diag"], 2 * b + s + 1)
                w = 512 if s == 0 else 256
                dst = bank["x0"] if s == 0 else bank["x1"]
                pe.matmul(dst[:, 0:w], ones[:, :], dg[:, 0:w // P, :].rearrange("p a c -> p (a c)"),
                          start=True, stop=True).then_inc(S["q_spread"], 1)

            def q_turn_rounded(b, s):
                pe.wait_ge(S["q_rounded"], 2 * b + s + 1)
                if isinstance(b, int) and b == 0:
                    pe.wait_ge(S["q0_rounded_w"], s + 1)
                if s == 0:
                    for j in range(4):
                        dst = bank["x0"] if j < 2 else bank["x1"]
                        for k in range(ND):
                            last = pe.transpose(dst[:, k * 256 + (j % 2) * P:k * 256 + (j % 2 + 1) * P],
                                                qw[:, j, k * P:(k + 1) * P], ident[:, :])
                else:
                    for j in range(4):
                        last = pe.transpose(bank["x0"][:, j * P:(j + 1) * P], qw[:, j, 0:I], ident[:, :])
                last.then_inc(S["q_turned"], 1)

            def q_product(b, s):
                pe.wait_ge(S["q_bf"], 2 * b + s + 1)
                if s == 0:
                    pe.wait_ge(S["q_bf_w"], b + 1)
                for t in range(NT):
                    if s == 0:
                        for k in range(ND):
                            last = pe.matmul(bank["x0"][:, t * D:(t + 1) * D], qT[:, k, t * P:(t + 1) * P],
                                             qT[:, 2 + k, :], start=(k == 0), stop=(k == ND - 1))
                    else:
                        last = pe.matmul(bank["x0"][:, t * D:(t + 1) * D], qT[:, 0, t * P:(t + 1) * P],
                                         qT[:, 1, :], start=True, stop=True)
                pe.wait_ge(S["q_wdiag"], 2 * b + s + 1)
                pe.matmul(bank["x1"][:, 0:D], ones[:, :], dg[:, 2:4, :].rearrange("p a c -> p (a c)"),
                          start=True, stop=True).then_inc(S["q_prod"], 1)

            def q_turn_act(b):
                pe.wait_ge(S["q_act"], b + 1)
                for t in range(NT):
                    last = pe.transpose(bank["x0"][:, t * P:(t + 1) * P], act1[:, t, :], ident[:, :])
                last.then_inc(S["q_xt"], 1)

            def q_piece(n, b):
                if n == 0:
                    q_spread(b, 0)
                elif n == 1:
                    q_turn_rounded(b, 0)
                elif n == 2:
                    q_product(b, 0)
                elif n == 3:
                    q_turn_act(b)
                elif n == 4:
                    q_spread(b, 1)
                elif n == 5:
                    q_turn_rounded(b, 1)
                elif n == 6:
                    q_product(b, 1)

            def bit_up(b, c):
                if c == 0:
                    pe.wait_ge(S["lnb_hi"], b + 1)
                    pe.wait_ge(S["lnb_lo"], b + 1)
                if c >= 3:
                    pe.wait_ge(S["bit_prod"], BIT_CHUNKS * b + c - 2)
                dst = CHUNK_BANKS[c % 3]
                if c < BIT_FULL:
                    sides = ((0, c * P), (T, BIT + BIT_REST + c * P))
                else:
                    sides = ((0, BIT_FULL * P),)
                first = True
                for at, col in sides:
                    for k in range(ND):
                        w = w12[:, k, col:col + P]
                        last = split_mm(dst[:, at:at + T], w, None, xt_hi[:, k, :], xt_lo[:, k, :], first, k == ND - 1)
                        first = False
                last.then_inc(S["bit_mm"], 1)

            def bit_down(b, c):
                if c == 0:
                    pe.wait_ge(S["w3_ready"], 2)
                pe.wait_ge(S["bit_hi"], BIT_CHUNKS * b + c + 1)
                pe.wait_ge(S["bit_lo"], BIT_CHUNKS * b + c + 1)
                rows = P if c < BIT_FULL else BIT_REST
                for t in range(NT):
                    for half in (act_hi, act_lo):
                        last = pe.matmul(bank["u"][:, t * D:(t + 1) * D], half[0:rows, c % 3, t * P:(t + 1) * P],
                                         w3[0:rows, c, :], start=(c == 0 and t == 0 and half is act_hi),
                                         stop=(c == BIT_CHUNKS - 1), skip_group_check=True)
                last.then_inc(S["bit_y"], 1)

            def bit_turn(b):
                pe.wait_ge(S["lnb_xn"], b + 1)
                turn_xn(bank["x0"]).then_inc(S["lnb_t"], 1)

            def bit_layer(b, between=None, begun=0):
                for c in range(begun, BIT_CHUNKS + 2):
                    if c < BIT_CHUNKS:
                        bit_up(b, c)
                    if c >= 2:
                        bit_down(b, c - 2)
                    if between is not None:
                        between(c)

            def att_turn(b):
                pe.wait_ge(S["lna_xn"], b + 1)
                turn_xn(bank["x0"]).then_inc(S["lna_t"], 1)

            def queries(b, h):
                p = h // 2
                if h % 2 == 0 and p >= 1:
                    pe.wait_ge(S["qa_l"], PAIRS * b + p)
                dst = bank["qa"][:, (h % 2) * T:(h % 2 + 1) * T]
                for k in range(ND):
                    last = split_mm(dst, a_hi[:, h, k, :], a_lo[:, h, k, :], xt_hi[:, k, :], xt_lo[:, k, :],
                                    k == 0, k == ND - 1)
                if h % 2 == 1:
                    last.then_inc(S["qa_mm"], 1)

            def scores(b, h):
                pe.wait_ge(S["qa_l"], PAIRS * b + h // 2 + 1)
                if h >= 2:
                    pe.wait_ge(S["s_min"], H * b + h - 1)
                dst = bank["s0"] if h % 2 == 0 else bank["s1"]
                ring, col = (h // 2) % 2, (h % 2) * T
                for t in range(NT):
                    cols = slice(col + t * P, col + (t + 1) * P)
                    last = split_mm(dst[:, t * T:(t + 1) * T], qa_hi[:, ring, cols], qa_lo[:, ring, cols],
                                    cxT_hi[:, :], cxT_lo[:, :], True, True)
                last.then_inc(S["s_mm"], 1)

            def turn_probs(b, h):
                pe.wait_ge(S["s_norm"], H * b + h + 1)
                if h >= 1:
                    pe.wait_ge(S["t_l"], H * b + h)
                for t in range(NT):
                    for s in range(2):
                        last = pe.transpose(bank["pt"][:, s * T + t * P:s * T + (t + 1) * P],
                                            prob[:, h % 2, t, s * P:(s + 1) * P], ident[:, :])
                last.then_inc(S["t_mm"], 1)

            def mix(b, h):
                pe.wait_ge(S["t_l"], H * b + h + 1)
                if h >= 1:
                    pe.wait_ge(S["u_l"], H * b + h)
                for s in range(2):
                    last = split_mm(bank["u"][:, 0:T], cx_hi[:, s, :], cx_lo[:, s, :], pt_hi[:, s, :],
                                    pt_lo[:, s, :], s == 0, s == 1)
                last.then_inc(S["u_mm"], 1)

            def project(b, h):
                pe.wait_ge(S["u_l"], H * b + h + 1)
                for t in range(NT):
                    cols = slice(t * P, (t + 1) * P)
                    last = split_mm(bank["o"][:, t * D:(t + 1) * D], ut_hi[:, cols], ut_lo[:, cols],
                                    c_hi[:, h, :], c_lo[:, h, :], h == 0 and t == 0, h == H - 1)
                last.then_inc(S["o_mm"], 1)

            def attention(b, beside=None):
                for h in range(H):
                    turn_probs(b, h)
                    if h + 4 < H:
                        queries(b, h + 4)
                    if h + 2 < H:
                        scores(b, h + 2)
                    if beside is not None:
                        beside(h, 0)
                    if h >= 1:
                        project(b, h - 1)
                    mix(b, h)
                    if beside is not None:
                        beside(h, 1)

            def ffn_turn(b):
                pe.wait_ge(S["lnf_xn"], b + 1)
                turn_xn(bank["x0"]).then_inc(S["lnf_t"], 1)

            def route(b):
                pe.wait_ge(S["router_hi"], 1)
                pe.wait_ge(S["router_lo"], 1)
                for t in range(NT):
                    for k in range(ND):
                        cols = slice(t * P, (t + 1) * P)
                        last = split_mm(bank["x1"][:, t * NR:(t + 1) * NR], yt_hi[:, k, cols], yt_lo[:, k, cols],
                                        router_hi[:, k, :], router_lo[:, k, :], k == 0, k == ND - 1)
                last.then_inc(S["route_mm"], 1)

            def ffn_up(b, c):
                if c >= 3:
                    pe.wait_ge(S["ffn_prod"], FFN_CHUNKS * b + c - 2)
                dst = CHUNK_BANKS[c % 3]
                first = True
                for at, w_hi, w_lo in ((0, gate_hi, gate_lo), (T, up_hi, up_lo)):
                    for k in range(ND):
                        cols = slice(c * P, (c + 1) * P)
                        last = split_mm(dst[:, at:at + T], w_hi[:, k, cols], w_lo[:, k, cols], yt_hi[:, k, :],
                                        yt_lo[:, k, :], first, k == ND - 1)
                        first = False
                last.then_inc(S["ffn_mm"], 1)

            def ffn_down(b, c):
                pe.wait_ge(S["ffn_hi"], FFN_CHUNKS * b + c + 1)
                routed = c == FFN_CHUNKS - 1
                if routed:
                    pe.wait_ge(S["ffn_lo_last"], b + 1)
                else:
                    pe.wait_ge(S["ffn_lo"], (FFN_CHUNKS - 1) * b + c + 1)
                dst = bank["o"] if routed else bank["u"]
                for t in range(NT):
                    cols = slice(t * P, (t + 1) * P)
                    last = split_mm(dst[:, t * D:(t + 1) * D], act_hi[:, c % 3, cols], act_lo[:, c % 3, cols],
                                    down_hi[:, c, :], down_lo[:, c, :], t == 0 and (c == 0 or routed),
                                    c >= FFN_CHUNKS - 2)
                last.then_inc(S["ffn_y"], 1)

            def ffn_begin(b, last=False):
                pe.wait_ge(S["lnf_hi"], b + 1)
                pe.wait_ge(S["ffn_w_lo_pool"], len(FFN_LO_POOL))
                pe.wait_ge(S["ffn_w_lo_dve"], len(FFN_LO_DVE))
                if not last:
                    pe.wait_ge(S["bit_prod"], BIT_CHUNKS * (b + 1) + 4)
                dst, first = CHUNK_BANKS[0], True
                for y, halves in ((yt_hi, 2), (yt_lo, 1)):
                    if y is yt_lo:
                        pe.wait_ge(S["lnf_lo"], b + 1)
                    for at, weights in ((0, (gate_hi, gate_lo)), (T, (up_hi, up_lo))):
                        for k in range(ND):
                            for w in weights[:halves]:
                                last_mm = pe.matmul(dst[:, at:at + T], w[:, k, 0:P], y[:, k, :], start=first,
                                                    stop=(y is yt_lo and k == ND - 1), skip_group_check=True)
                                first = False
                last_mm.then_inc(S["ffn_mm"], 1)

            def ffn_layer(b, last):
                if not last:
                    route(b)
                for c in range(FFN_CHUNKS + 2):
                    if not last and c in (1, 2):
                        pe.wait_ge(S["bit_prod"], BIT_CHUNKS * (b + 1) + 4 + c)
                    if 1 <= c < FFN_CHUNKS:
                        ffn_up(b, c)
                    if last and c == ROUTE_LATE:
                        route(b)
                    if c == 2 and not last:
                        pe.wait_ge(S["bit_x"], b + 2)
                    if not last and c == 2:
                        att_turn(b + 1)
                    if c >= 2:
                        ffn_down(b, c - 2)
                    if not last and c == 5:
                        pe.wait_ge(S["lna_hi"], b + 2)
                        pe.wait_ge(S["lna_lo"], b + 2)
                        queries(b + 1, 0)
                        queries(b + 1, 1)
                    if not last and c == 7:
                        pe.wait_ge(S["ffn_prod"], FFN_CHUNKS * b + FFN_CHUNKS - 2)
                        pe.wait_ge(S["ctx_lo"], b + 2)
                        scores(b + 1, 0)
                    if not last and c == 8:
                        pe.wait_ge(S["ffn_prod"], FFN_CHUNKS * b + FFN_CHUNKS - 1)
                        scores(b + 1, 1)
                        queries(b + 1, 2)
                        queries(b + 1, 3)

            Q_STEPS = {(0, 1): 0, (5, 0): 1, (5, 1): 2, (8, 0): 3, (9, 1): 4, (11, 1): 5, (12, 0): 6}

            def batch(b, last):
                def beside(h, part):
                    if (h, part) in Q_STEPS:
                        q_piece(Q_STEPS[h, part], b + 1)
                    if (h, part) == (14, 1):
                        bit_turn(b + 1)
                    if (h, part) == (15, 1):
                        pe.wait_ge(S["s_min"], H * (b + 1))
                        bit_up(b + 1, 0)
                attention(b, None if last else beside)
                project(b, H - 1)
                if not last:
                    bit_up(b + 1, 1)
                    pe.wait_ge(S["t_l"], H * (b + 1))
                    bit_up(b + 1, 2)
                    bit_down(b + 1, 0)
                    bit_layer(b + 1, lambda c: ffn_turn(b) if c == 4 else ffn_begin(b) if c == 5 else None, begun=3)
                else:
                    ffn_turn(b)
                    ffn_begin(b, last)
                ffn_layer(b, last)

            def prep_unit(k):
                p = k // 2
                pe.wait_ge(S[("wq", "wo")[k % 2] + str(p * WQ_LOADS // PAIRS)], 16)
                if k < 2:
                    pe.wait_ge(S[("wk_in", "wv_in")[k]], 16)
                if k >= 2:
                    pe.wait_ge(S["prep_lo"], k - 1)
                dst = PREP_BANKS[k % 2]
                for j in range(2):
                    raw = (wq_raw, wo_raw)[k % 2][:, 2 * p + j, :]
                    if k % 2 == 0:
                        for s in range(ND):
                            last = pe.matmul(dst[:, (j * ND + s) * P:(j * ND + s + 1) * P],
                                             raw[:, s * P:(s + 1) * P], wkT[:, p, :], start=True, stop=True)
                    else:
                        last = pe.matmul(dst[:, j * D:(j + 1) * D], wvT[:, p, :], raw, start=True, stop=True)
                last.then_inc(S["prep_mm"], 1)

            pe.wait_ge(S["consts"], 2)
            q_turn_x0()
            prep_unit(0)
            q_piece(0, 0)
            prep_unit(1)
            prep_unit(2)
            q_piece(1, 0)
            prep_unit(3)
            q_piece(2, 0)
            prep_unit(4)
            prep_unit(5)
            q_piece(3, 0)
            pe.wait_ge(S["abs_done"], 4)
            pe.matmul(bank["u"][:, 0:4], ones[:, :], gsum[:, :], start=True, stop=True).then_inc(S["gamma_mm"], 1)
            q_piece(4, 0)
            prep_unit(6)
            prep_unit(7)
            q_piece(5, 0)
            prep_unit(8)
            q_piece(6, 0)
            q_turn_next()
            prep_unit(9)
            prep_unit(10)
            bit_turn(0)
            prep_unit(11)
            pe.wait_ge(S["w12_ready"], 2)

            def beside_bit(c):
                if c == 0:
                    prep_unit(12)
                if c == 1:
                    pe.wait_ge(S["next_read"], 1)

            bit_layer(0, beside_bit)
            prep_unit(13)
            prep_unit(14)
            att_turn(0)
            prep_unit(15)
            pe.wait_ge(S["lna_hi"], 1)
            pe.wait_ge(S["lna_lo"], 1)
            queries(0, 0)
            queries(0, 1)
            pe.wait_ge(S["ctx_hi"], 1)
            pe.wait_ge(S["ctx_lo"], 1)
            scores(0, 0)
            scores(0, 1)
            queries(0, 2)
            queries(0, 3)
            with pe.Fori(0, NB - 1) as b:
                batch(b, False)
            batch(NB - 1, True)

        @block.scalar
        def _(act):
            def split_hi(dst, src, done, scale=1.0):
                act.activation(dst, src, ACT.Copy, scale=scale).then_inc(done, 1)

            def ln_hi(b, kind, dst):
                act.wait_ge(S[kind + "_t"], b + 1)
                split_hi(dst[:, :, :].rearrange("p k t -> p (k t)"), bank["x0"][:, :], S[kind + "_hi"])

            def q_tanh(b):
                act.wait_ge(S["q_hs"], b + 1)
                act.activation(qw[:, 0:NT, 0:I], hs[:, :, 0:I], ACT.Tanh, scale=0.5).then_inc(S["q_tanh"], 1)

            def q_bf(b, s):
                act.wait_ge(S["q_turned"], 2 * b + s + 1)
                act.activation(qT[:, 0:2, :].rearrange("p a n -> p (a n)"), bank["x0"][:, :], ACT.Copy,
                               bias=-MAGIC).then_inc(S["q_bf"], 1)

            def q_wscale(b, s):
                act.wait_ge(S["q_prod"], 2 * b + s + 1)
                act.copy(wscale[:, :], bank["x1"][:, 0:D]).then_inc(S["q_wscale"], 1)

            def ctx_split_hi(b):
                act.wait_ge(S["cx_in"], 32 * (b + 1))
                act.copy(cx_hi[:, :, :], cx[:, :, :])
                act.copy(cxT_hi[:, :], cxT[:, :]).then_inc(S["ctx_hi"], 1)

            def queries_hi(b, p):
                act.wait_ge(S["qa_mm"], PAIRS * b + p + 1)
                split_hi(qa_hi[:, p % 2, :], bank["qa"][:, :], S["qa_h"])

            def exps(b, h, between=None):
                act.wait_ge(S["s_min"], H * b + h + 1)
                for t in range(NT):
                    row = prob[:, h % 2, t, :]
                    last = act.activation(row, row, ACT.Exp, scale=-1.0, bias=row_min[:, h % 2, t:t + 1],
                                          accum_out=row_sum[:, h % 2, t:t + 1])
                    if t == 0 and between is not None:
                        between()
                last.then_inc(S["s_exp"], 1)

            def probs_hi(b, h):
                act.wait_ge(S["t_mm"], H * b + h + 1)
                split_hi(pt_hi[:, :, :].rearrange("p s t -> p (s t)"), bank["pt"][:, :], S["t_h"])

            def mix_hi(b, h):
                act.wait_ge(S["u_mm"], H * b + h + 1)
                split_hi(ut_hi[:, :], bank["u"][:, 0:T], S["u_h"])

            MIX_AMID = (11, 12, 13)

            def attention(b, last):
                for h in range(H):
                    if h >= 1 and h - 1 not in MIX_AMID:
                        mix_hi(b, h - 1)
                    if not last and h == 12:
                        q_bf(b + 1, 1)
                    if not last and h == 15:
                        ln_hi(b + 1, "lnb", xt_hi)
                    probs_hi(b, h)
                    if h == 0:
                        exps(b, 1)
                    if h % 2 == 1 and h + 3 < H:
                        queries_hi(b, (h + 3) // 2)
                    if not last:
                        if h == 5:
                            q_bf(b + 1, 0)
                        if h == 6:
                            q_wscale(b + 1, 0)
                        if h == 12:
                            q_wscale(b + 1, 1)
                    if h + 2 < H:
                        exps(b, h + 2, (lambda: mix_hi(b, h)) if h in MIX_AMID else None)
                    if not last:
                        if h == 6:
                            q_tanh(b + 1)

            def bit_sig(b, c):
                act.wait_ge(S["bit_mm"], BIT_CHUNKS * b + c + 1)
                src = CHUNK_BANKS[c % 3]
                if c < BIT_FULL:
                    act.activation(sig[:, c % 3, :], src[:, 0:T], ACT.Tanh, scale=0.5).then_inc(S["bit_sig"], 1)
                else:
                    act.activation(sig[BIT_REST:P, c % 3, :], src[0:BIT_REST, 0:T], ACT.Tanh, scale=0.5
                                   ).then_inc(S["bit_sig"], 1)

            def bit_high(b, c):
                act.wait_ge(S["bit_prod"], BIT_CHUNKS * b + c + 1)
                rows = P if c < BIT_FULL else BIT_REST
                act.copy(act_hi[0:rows, c % 3, :], act_raw[0:rows, c % 3, :]).then_inc(S["bit_hi"], 1)

            def ffn_high(b, c):
                act.wait_ge(S["ffn_prod"], FFN_CHUNKS * b + c + 1)
                act.copy(act_hi[:, c % 3, :], act_raw[:, c % 3, :]).then_inc(S["ffn_hi"], 1)

            def ffn_sig(b, c):
                act.wait_ge(S["ffn_mm"], FFN_CHUNKS * b + c + 1)
                act.activation(sig[:, c % 3, :], CHUNK_BANKS[c % 3][:, 0:T], ACT.Tanh, scale=0.5
                               ).then_inc(S["ffn_sig"], 1)

            def batch(b, last):
                attention(b, last)
                mix_hi(b, H - 1)
                if not last:
                    for c in range(BIT_CHUNKS):
                        bit_sig(b + 1, c)
                        if c == 4:
                            ln_hi(b, "lnf", yt_hi)
                        bit_high(b + 1, c)
                else:
                    ln_hi(b, "lnf", yt_hi)
                for c in range(FFN_CHUNKS):
                    ffn_sig(b, c)
                    if not last and c == 8:
                        exps(b + 1, 0)
                    ffn_high(b, c)
                    if c == (ROUTE_LATE + 1 if last else 1):
                        act.wait_ge(S["route_d"], b + 1)
                        act.activation(top_w[:, :, :], top_d[:, :, :], ACT.Tanh, scale=0.5).then_inc(S["route_sig"], 1)
                    if not last:
                        if c == 2:
                            ctx_split_hi(b + 1)
                        if c == 3:
                            ln_hi(b + 1, "lna", xt_hi)
                        if c == 5:
                            queries_hi(b + 1, 0)
                if not last:
                    queries_hi(b + 1, 1)

            def prep_hi(k):
                act.wait_ge(S["prep_mm"], k + 1)
                dst = (a_hi[:, 2 * (k // 2):2 * (k // 2) + 2, :, :].rearrange("p h s c -> p (h s c)") if k % 2 == 0 else
                       c_hi[:, 2 * (k // 2):2 * (k // 2) + 2, :].rearrange("p h d -> p (h d)"))
                split_hi(dst, PREP_BANKS[k % 2][:, :], S["prep_hi"], scale=-SCALE if k % 2 == 0 else 1.0)

            def ffn_weights_hi(u):
                act.wait_ge(S[f"ffn_w{u}"], 16)
                act.copy(ffn_unit(u, HI), ffn_unit(u, RAW)
                         ).then_inc(S["ffn_w_hi"], 1)

            def magnitudes(w, raw, k):
                act.activation(w, raw, ACT.Abs, accum_out=gsum[0:w.shape[0], k:k + 1]).then_inc(S["abs_done"], 1)

            act.wait_ge(S["consts"], 2)
            prep_hi(0)
            prep_hi(1)
            prep_hi(2)
            q_bf(0, 0)
            prep_hi(3)
            q_wscale(0, 0)
            act.wait_ge(S["w12_in"], 16)
            magnitudes(w12[:, :, 0:BIT], w12_raw[:, :, 0:BIT], 0)
            q_tanh(0)
            magnitudes(w12[:, :, BIT:2 * BIT], w12_raw[:, :, BIT:2 * BIT], 1)
            act.wait_ge(S["w3_in"], 32)
            magnitudes(w3[:, 0:BIT_FULL, :], w3_raw[:, 0:BIT_FULL, :], 2)
            magnitudes(w3[0:BIT_REST, BIT_FULL, :], w3_raw[0:BIT_REST, BIT_FULL, :], 3)
            prep_hi(4)
            prep_hi(5)
            act.wait_ge(S["lnq_shift"], 1)
            for b in range(1, NB):
                for t in range(NT):
                    last = act.activation(xn_next[:, (b - 1) * NT + t, :], x[:, b, t, :], ACT.Identity,
                                          scale=lnq_rstd[:, b, t:t + 1], bias=lnq_shift[:, b, t:t + 1])
            last.then_inc(S["next_xn"], 1)
            prep_hi(6)
            prep_hi(7)
            q_bf(0, 1)
            q_wscale(0, 1)
            prep_hi(8)
            act.wait_ge(S["bit_q12"], 1)
            for j in range(2):
                act.activation(w12[:, :, j * BIT:(j + 1) * BIT], w12_raw[:, :, j * BIT:(j + 1) * BIT], ACT.Copy,
                               bias=-MAGIC).then_inc(S["w12_ready"], 1)
                if j == 0:
                    prep_hi(9)
            prep_hi(10)
            ln_hi(0, "lnb", xt_hi)
            act.wait_ge(S["bit_q3"], 1)
            act.activation(w3[:, 0:BIT_FULL, :], w3_raw[:, 0:BIT_FULL, :], ACT.Copy, scale=0.5, bias=-0.5 * MAGIC
                           ).then_inc(S["w3_ready"], 1)
            act.activation(w3[0:BIT_REST, BIT_FULL, :], w3_raw[0:BIT_REST, BIT_FULL, :], ACT.Copy,
                           scale=0.5, bias=-0.5 * MAGIC).then_inc(S["w3_ready"], 1)
            prep_hi(11)
            act.wait_ge(S["w3_ready"], 2)
            for c in range(BIT_CHUNKS):
                bit_sig(0, c)
                bit_high(0, c)
                if c == 0:
                    prep_hi(12)
            for u in range(3):
                ffn_weights_hi(u)
            prep_hi(13)
            prep_hi(14)
            ctx_split_hi(0)
            ffn_weights_hi(3)
            ln_hi(0, "lna", xt_hi)
            act.wait_ge(S["router_in"], 16)
            act.copy(router_hi[:, :, :], router_raw[:, :, :]).then_inc(S["router_hi"], 1)
            ffn_weights_hi(4)
            prep_hi(15)
            ffn_weights_hi(5)
            queries_hi(0, 0)
            exps(0, 0)
            queries_hi(0, 1)
            with act.Fori(0, NB - 1) as b:
                batch(b, False)
            batch(NB - 1, True)

        @block.gpsimd
        def _(pool):
            def power(b, kind):
                pool.wait_ge(S[kind + "_ve"], b + 1)
                pool.tensor_tensor(ln_rstd[:, :], ln_ve[:, :], half_exp[:, 1, 0, :], ALU.pow
                                   ).then_inc(S[kind + "_pow"], 1)

            def q_roots(b0, b1):
                for sign in range(2):
                    last = pool.tensor_tensor(root0[:, sign, b0:b1, :], ratio0[:, sign, b0:b1, :],
                                              half_exp[:, sign, b0:b1, :], ALU.pow)
                last.then_inc(S["q_roots"], 1)

            def lnq_power(b0, b1):
                pool.wait_ge(S["lnq_ve"], 1 if b0 == 0 else 2)
                pool.tensor_tensor(lnq_rstd[:, b0:b1, :], lnq_rstd[:, b0:b1, :], half_exp[:, 1, b0:b1, :], ALU.pow
                                   ).then_inc(S["lnq_pow"], 1)

            def q_spread_diagonals(b, s):
                if s == 0:
                    pool.wait_ge(S["q_sis"], b + 1)
                    columns = [sis[:, i, k:k + 1] for i in range(2) for k in range(ND)]
                else:
                    pool.wait_ge(S["q_ratio"], b + 1)
                    pool.tensor_tensor(sis[:, :, 0], ratio1[:, :], half_exp[:, :, 0, 0], ALU.pow
                                       ).then_inc(S["q_root"], 1)
                    pool.wait_ge(S["q_root"], b + 1)
                    columns = [sis[:, i, 0:1] for i in range(2)]
                pool.nop(nofuse=True)
                for j, column in enumerate(columns):
                    last = pool.tensor_scalar(dg[:, j, :], ident[:, :], column, 1.0, ALU.mult, ALU.mult)
                last.then_inc(S["q_diag"], 1)

            def q_scale_diagonals(b, s):
                pool.wait_ge(S["q_scales"], 2 * b + s + 1)
                pool.nop(nofuse=True)
                for j in (2, 3):
                    last = pool.tensor_scalar(dg[:, j, :], ident[:, :], qscale[:, s, j:j + 1], 1.0, ALU.mult, ALU.mult)
                last.then_inc(S["q_wdiag"], 1)

            def q_round(b, s, part):
                pool.wait_ge(S["q_scales"], 2 * b + s + 1)
                pool.nop(nofuse=True)
                w = D if s == 0 else I
                for j in (2 * part, 2 * part + 1):
                    last = pool.tensor_scalar(qw[:, j, 0:w], qw[:, j, 0:w], qrecip[:, j:j + 1], MAGIC,
                                              ALU.mult, ALU.add)
                if part == 1 or (isinstance(b, int) and b == 0):
                    last.then_inc(S["q_rounded"], 1)

            def q_gate_up(b):
                pool.wait_ge(S["q_hs"], b + 1)
                pool.tensor_tensor(act1[:, :, :], hs[:, :, 0:I], hs[:, :, I:2 * I], ALU.mult).then_inc(S["q_gu"], 1)

            def q_act(b):
                pool.wait_ge(S["q_gu"], b + 1)
                pool.wait_ge(S["q_sigm"], b + 1)
                pool.tensor_tensor(act1[:, :, :], act1[:, :, :], qw[:, 0:NT, 0:I], ALU.mult).then_inc(S["q_act"], 1)

            def q_residual(b):
                pool.wait_ge(S["q_out"], b + 1)
                pool.tensor_tensor(x[:, b, :, :], x[:, b, :, :], hs[:, :, :], ALU.add).then_inc(S["q_x"], 1)

            def normalise(b, h):
                pool.wait_ge(S["s_inv"], H * b + h + 1)
                pool.nop(nofuse=True)
                for t in range(NT):
                    row = prob[:, h % 2, t, :]
                    last = pool.tensor_scalar(row, row, row_inv[:, h % 2, t:t + 1], valid_b[:, 0:1],
                                              ALU.mult, ALU.mult)
                last.then_inc(S["s_norm"], 1)

            def bit_low(b, c):
                pool.wait_ge(S["bit_hi"], BIT_CHUNKS * b + c + 1)
                rows = P if c < BIT_FULL else BIT_REST
                pool.tensor_tensor(act_lo[0:rows, c % 3, :], act_raw[0:rows, c % 3, :],
                                   f32(act_hi[0:rows, c % 3, :]), ALU.subtract).then_inc(S["bit_lo"], 1)

            def ffn_low(b, c):
                pool.wait_ge(S["ffn_hi"], FFN_CHUNKS * b + c + 1)
                pool.tensor_tensor(act_lo[:, c % 3, :], act_raw[:, c % 3, :], f32(act_hi[:, c % 3, :]),
                                   ALU.subtract).then_inc(S["ffn_lo"], 1)

            def batch(b, last):
                for h in range(H):
                    if not last and h in (0, 9):
                        q_spread_diagonals(b + 1, 0 if h == 0 else 1)
                    if h + 1 < H:
                        normalise(b, h + 1)
                    if last:
                        continue
                    if h == 3:
                        q_round(b + 1, 0, 0)
                    if h == 4:
                        q_round(b + 1, 0, 1)
                        q_scale_diagonals(b + 1, 0)
                    if h == 6:
                        q_gate_up(b + 1)
                    if h == 7:
                        q_act(b + 1)
                    if h == 10:
                        q_round(b + 1, 1, 0)
                        q_round(b + 1, 1, 1)
                    if h == 11:
                        q_scale_diagonals(b + 1, 1)
                    if h == 12:
                        q_residual(b + 1)
                    if h == 13:
                        power(b + 1, "lnb")
                if not last:
                    bit_low(b + 1, 0)
                    bit_low(b + 1, 1)
                power(b, "lnf")
                if not last:
                    for c in range(2, BIT_CHUNKS):
                        bit_low(b + 1, c)
                    power(b + 1, "lna")
                for c in range(FFN_CHUNKS - 1):
                    ffn_low(b, c)
                if not last:
                    normalise(b + 1, 0)

            def ternary3_round():
                pool.wait_ge(S["gamma_inv"], 1)
                pool.wait_ge(S["abs_done"], 4)
                pool.nop(nofuse=True)
                main, rest = w3_raw[:, 0:BIT_FULL, :], w3_raw[0:BIT_REST, BIT_FULL, :]
                pool.tensor_scalar(main, main, gam[:, 2:3], MAGIC, ALU.mult, ALU.add)
                pool.tensor_scalar(rest, rest, gam[0:BIT_REST, 2:3], MAGIC, ALU.mult, ALU.add
                                   ).then_inc(S["bit_r3"], 1)

            pool.memset(ones[:, :], 1.0).then_inc(S["consts"], 1)
            pool.memset(gsum[:, :], 0.0)
            pool.memset(half_exp[:, 0, :, :], 0.5)
            pool.memset(half_exp[:, 1, :, :], -0.5)
            pool.wait_ge(S["consts"], 1)
            pool.affine_select(out=ident[:, :], in_=ones[:, :], compare_op=ALU.is_equal, fill=0.0, base=0,
                               pattern=[[-1, P]], channel_multiplier=1).then_inc(S["consts"], 1)
            pool.wait_ge(S["consts"], 2)
            lnq_power(0, 1)
            pool.wait_ge(S["q_ratio0"], 1)
            q_roots(0, 1)
            q_spread_diagonals(0, 0)
            q_round(0, 0, 0)
            q_scale_diagonals(0, 0)
            q_gate_up(0)
            q_act(0)
            lnq_power(1, NB)
            q_spread_diagonals(0, 1)
            q_round(0, 1, 0)
            q_scale_diagonals(0, 1)
            ternary3_round()
            power(0, "lnb")

            def ffn_weights_lo(u):
                pool.wait_ge(S["ffn_w_hi"], u + 1)
                pool.tensor_tensor(ffn_unit(u, LO), ffn_unit(u, RAW), f32(ffn_unit(u, HI)), ALU.subtract
                                   ).then_inc(S["ffn_w_lo_pool"], 1)

            for c in range(BIT_CHUNKS):
                bit_low(0, c)
            ffn_weights_lo(FFN_LO_POOL[0])
            power(0, "lna")
            for u in FFN_LO_POOL[1:-1]:
                ffn_weights_lo(u)
            pool.wait_ge(S["q_ratio0"], 2)
            q_roots(1, NB)
            normalise(0, 0)
            ffn_weights_lo(FFN_LO_POOL[-1])
            with pool.Fori(0, NB - 1) as b:
                batch(b, False)
            batch(NB - 1, True)

        @block.vector
        def _(dve):
            links = {"base": 0, "n": 0}

            def link(ins):
                links["n"] += 1
                ins.then_inc(S["dve_self"], 1)
                dve.wait_ge(S["dve_self"], links["base"] + links["n"])

            def hold():
                dve.nop(nofuse=True)

            def ln_stats_of(b, kind):
                if kind == "lnb":
                    dve.wait_ge(S["q_x"], b + 1)
                hold()
                for t in range(NT):
                    last = dve.bn_stats(ln_stats[:, t, :], x[:, b, t, :])
                link(last)
                hold()
                for t in range(NT):
                    last = dve.bn_aggr(ln_mv[:, t, :], ln_stats[:, t, :])
                link(last)
                dve.tensor_scalar(ln_ve[:, :], ln_mv[:, :, 1], LN_EPS, None, ALU.add).then_inc(S[kind + "_ve"], 1)

            def ln_apply(b, kind):
                dve.wait_ge(S[kind + "_pow"], b + 1)
                for t in range(NT):
                    last = dve.tensor_scalar(xn[:, t, :], x[:, b, t, :], ln_mv[:, t, 0:1], ln_rstd[:, t:t + 1],
                                             ALU.subtract, ALU.mult)
                last.then_inc(S[kind + "_xn"], 1)

            def ln_lo(b, kind, hi, lo):
                dve.wait_ge(S[kind + "_hi"], b + 1)
                dve.tensor_tensor(lo[:, :, :].rearrange("p k t -> p (k t)"), bank["x0"][:, :],
                                  f32(hi[:, :, :].rearrange("p k t -> p (k t)")), ALU.subtract
                                  ).then_inc(S[kind + "_lo"], 1)

            def lnq_stats_of(batches):
                hold()
                for b in batches:
                    for t in range(NT):
                        last = dve.bn_stats(lnq_stats[:, b, t, :], x[:, b, t, :])
                return last

            def lnq_variances(batches):
                hold()
                for b in batches:
                    for t in range(NT):
                        last = dve.bn_aggr(lnq_mv[:, b, t, :], lnq_stats[:, b, t, :])
                link(last)
                rows = slice(batches[0], batches[-1] + 1)
                dve.tensor_scalar(lnq_rstd[:, rows, :], lnq_mv[:, rows, :, 1], LN_EPS, None, ALU.add
                                  ).then_inc(S["lnq_ve"], 1)

            def lnq_apply(b, dst):
                for t in range(NT):
                    last = dve.tensor_scalar(dst[:, t, :], x[:, b, t, :], lnq_mv[:, b, t, 0:1],
                                             lnq_rstd[:, b, t:t + 1], ALU.subtract, ALU.mult)
                return last

            def q_amax0_x(b, src):
                return dve.tensor_reduce(amax0[:, 0, b, :], src[:, :].rearrange("p (k t) -> p k t", k=ND), AX.X,
                                         ALU.max, apply_absolute_value=True)

            def q_amax0_w(b):
                return dve.tensor_reduce(amax0[:, 1, b, :], guT[:, b, :, :], AX.X, ALU.max,
                                         apply_absolute_value=True)

            def q_ratio0(b0, b1):
                ax, aw = amax0[:, 0, b0:b1, :], amax0[:, 1, b0:b1, :]
                link(dve.tensor_scalar(amax0[:, :, b0:b1, :], amax0[:, :, b0:b1, :], Q_EPS, None, ALU.max))
                link(dve.reciprocal(aw, aw))
                link(dve.tensor_tensor(ax, ax, aw, ALU.mult))
                for sign in range(2):
                    last = dve.tensor_scalar(ratio0[:, sign, b0:b1, :], ax, Q_EPS * Q_EPS, None, ALU.max)
                last.then_inc(S["q_ratio0"], 1)

            def q_take(b):
                if isinstance(b, int):
                    dve.wait_ge(S["q_roots"], 1)
                dve.tensor_copy(sis[:, :, :], root0[:, :, b, :]).then_inc(S["q_sis"], 1)

            def q_ratio1(b):
                dve.wait_ge(S["q_xt"], b + 1)
                link(dve.tensor_reduce(amax1[:, 0:1], bank["x0"][:, 0:T], AX.X, ALU.max, apply_absolute_value=True))
                link(dve.tensor_scalar(amax1[:, :], amax1[:, :], Q_EPS, None, ALU.max))
                link(dve.reciprocal(amax1[:, 1:2], amax1[:, 1:2]))
                link(dve.tensor_tensor(amax1[:, 0:1], amax1[:, 0:1], amax1[:, 1:2], ALU.mult))
                for sign in range(2):
                    last = dve.tensor_scalar(ratio1[:, sign:sign + 1], amax1[:, 0:1], Q_EPS * Q_EPS, None, ALU.max)
                last.then_inc(S["q_ratio"], 1)

            def q_ctx_amax(b):
                dve.wait_ge(S["cx_in"], 32 * (b + 1))
                dve.tensor_reduce(amax1[:, 1:2], cxT[:, :], AX.X, ALU.max, apply_absolute_value=True)

            def q_scaled_w(b, s):
                if s == 0:
                    dve.wait_ge(S["gu_in"], 16 * (b + 1))
                dve.wait_ge(S["q_spread"], 2 * b + s + 1)
                w = D if s == 0 else I
                s_row = (bank["x0"] if s == 0 else bank["x1"])[:, 0:w]
                for j in range(2):
                    dve.tensor_tensor(qw[:, 2 + j, 0:w], gu[:, j, :] if s == 0 else cx[:, j, :], s_row, ALU.mult)

            def q_scaled_x(b, s):
                if s == 0:
                    dve.wait_ge(S["lnq_xn"], b + 1)
                w = D if s == 0 else I
                inv_row = (bank["x0"] if s == 0 else bank["x1"])[:, w:2 * w]
                for j in range(2):
                    last = dve.tensor_tensor(qw[:, j, 0:w], xn[:, j, :] if s == 0 else act1[:, j, :], inv_row, ALU.mult)
                link(last)

            def q_rowmax(b, s, rows):
                w = D if s == 0 else I
                link(dve.tensor_reduce(rowmax[:, rows], qw[:, rows, 0:w], AX.X, ALU.max, apply_absolute_value=True))

            def q_scales(b, s):
                link(dve.tensor_scalar(qscale[:, s, :], rowmax[:, :], Q_EPS, 1.0 / QMAX, ALU.max, ALU.mult))
                dve.reciprocal(qrecip[:, :], qscale[:, s, :]).then_inc(S["q_scales"], 1)

            def q_round_w0(s):
                dve.wait_ge(S["q_scales"], s + 1)
                w = D if s == 0 else I
                for j in (2, 3):
                    last = dve.tensor_scalar(qw[:, j, 0:w], qw[:, j, 0:w], qrecip[:, j:j + 1], MAGIC,
                                             ALU.mult, ALU.add)
                last.then_inc(S["q0_rounded_w"], 1)

            def q_bf_w(b):
                dve.wait_ge(S["q_turned"], 2 * b + 1)
                dve.tensor_scalar(qT[:, 2:4, :].rearrange("p a n -> p (a n)"), bank["x1"][:, :], -MAGIC, None, ALU.add
                                  ).then_inc(S["q_bf_w"], 1)

            def q_dequant(b, s):
                dve.wait_ge(S["q_wscale"], 2 * b + s + 1)
                for t in range(NT):
                    last = dve.scalar_tensor_tensor(out=hs[:, t, :], in0=bank["x0"][:, t * D:(t + 1) * D],
                                                    scalar=qscale[:, s, t:t + 1], in1=wscale[:, :],
                                                    op0=ALU.mult, op1=ALU.mult)
                return last

            def q_residual0():
                dve.wait_ge(S["q_out"], 1)
                dve.tensor_tensor(x[:, 0, :, :], x[:, 0, :, :], hs[:, :, :], ALU.add).then_inc(S["q_x"], 1)

            def q_sigmoid(b):
                dve.wait_ge(S["q_tanh"], b + 1)
                e = qw[:, 0:NT, 0:I]
                dve.tensor_scalar(e, e, 0.5, 0.5, ALU.mult, ALU.add).then_inc(S["q_sigm"], 1)

            def bit_act(b, c):
                n = BIT_CHUNKS * b + c + 1
                dve.wait_ge(S["bit_sig"], n)
                src, r = CHUNK_BANKS[c % 3], c % 3
                if c < BIT_FULL:
                    rows = P
                    last = dve.scalar_tensor_tensor(out=act_raw[:, r, :], in0=sig[:, r, :], scalar=1.0,
                                                    in1=src[:, T:2 * T], op0=ALU.add, op1=ALU.mult)
                else:
                    rows = BIT_REST
                    last = dve.scalar_tensor_tensor(out=act_raw[0:rows, r, :], in0=sig[rows:P, r, :], scalar=1.0,
                                                    in1=src[rows:P, 0:T], op0=ALU.add, op1=ALU.mult)
                last.then_inc(S["bit_prod"], 1)

            def add_bank(b, which, done):
                dve.tensor_tensor(x[:, b, :, :].rearrange("p t d -> p (t d)"), bank[which][:, :],
                                  x[:, b, :, :].rearrange("p t d -> p (t d)"), ALU.add).then_inc(S[done], 1)

            def bit_residual(b):
                dve.wait_ge(S["bit_y"], BIT_CHUNKS * (b + 1))
                add_bank(b, "u", "bit_x")
                dve.wait_ge(S["bit_x"], b + 1)

            def ctx_split_lo(b):
                dve.wait_ge(S["ctx_hi"], b + 1)
                dve.tensor_tensor(cx_lo[:, :, :], cx[:, :, :], f32(cx_hi[:, :, :]), ALU.subtract)
                dve.tensor_tensor(cxT_lo[:, :], cxT[:, :], f32(cxT_hi[:, :]), ALU.subtract).then_inc(S["ctx_lo"], 1)

            def mask_row(b):
                dve.wait_ge(S["mask_in"], 16 * (b + 1))
                dve.tensor_reduce(valid_b[:, :], mask8[:, :], AX.X, ALU.max)
                dve.tensor_scalar(masked[:, :], mask8[:, :], -MASKED, MASKED, ALU.mult, ALU.add
                                  ).then_inc(S["mask_row"], 1)

            def queries_lo(b, p):
                dve.wait_ge(S["qa_h"], PAIRS * b + p + 1)
                dve.tensor_tensor(qa_lo[:, p % 2, :], bank["qa"][:, :], f32(qa_hi[:, p % 2, :]), ALU.subtract
                                  ).then_inc(S["qa_l"], 1)

            def row_minima(b, h):
                if h == 0:
                    dve.wait_ge(S["mask_row"], b + 1)
                dve.wait_ge(S["s_mm"], H * b + h + 1)
                hold()
                src = bank["s0"] if h % 2 == 0 else bank["s1"]
                for t in range(NT):
                    last = dve.tensor_tensor_reduce(out=prob[:, h % 2, t, :], in0=src[:, t * T:(t + 1) * T],
                                                    in1=masked[:, :], scale=1.0, scalar=3.0e38, op0=ALU.add,
                                                    op1=ALU.min, accum_out=row_min[:, h % 2, t:t + 1])
                last.then_inc(S["s_min"], 1)

            def row_inverses(b, h):
                dve.wait_ge(S["s_exp"], H * b + h + 1)
                dve.reciprocal(row_inv[:, h % 2, :], row_sum[:, h % 2, :]).then_inc(S["s_inv"], 1)

            def probs_lo(b, h):
                dve.wait_ge(S["t_h"], H * b + h + 1)
                dve.tensor_tensor(pt_lo[:, :, :].rearrange("p s t -> p (s t)"), bank["pt"][:, :],
                                  f32(pt_hi[:, :, :].rearrange("p s t -> p (s t)")), ALU.subtract
                                  ).then_inc(S["t_l"], 1)

            def mix_lo(b, h):
                dve.wait_ge(S["u_h"], H * b + h + 1)
                dve.tensor_tensor(ut_lo[:, :], bank["u"][:, 0:T], f32(ut_hi[:, :]), ALU.subtract
                                  ).then_inc(S["u_l"], 1)

            def attention(b, before, beside):
                for h in range(H):
                    before(h)
                    if h >= 1:
                        mix_lo(b, h - 1)
                    if 1 <= h < H - 1:
                        row_inverses(b, h + 1)
                    probs_lo(b, h)
                    if h == 0:
                        row_inverses(b, 1)
                    if h + 2 < H:
                        row_minima(b, h + 2)
                    if h % 2 == 1 and h + 3 < H:
                        queries_lo(b, (h + 3) // 2)
                    beside(h)

            def ffn_act(b, c):
                n = FFN_CHUNKS * b + c + 1
                dve.wait_ge(S["ffn_sig"], n)
                src, r = CHUNK_BANKS[c % 3], c % 3
                link(dve.scalar_tensor_tensor(out=sig[:, r, :], in0=sig[:, r, :], scalar=1.0, in1=src[:, 0:T],
                                              op0=ALU.add, op1=ALU.mult))
                dve.scalar_tensor_tensor(out=act_raw[:, r, :], in0=sig[:, r, :], scalar=0.5, in1=src[:, T:2 * T],
                                         op0=ALU.mult, op1=ALU.mult).then_inc(S["ffn_prod"], 1)

            def route_top(b):
                dve.wait_ge(S["route_mm"], b + 1)
                hold()
                for t in range(NT):
                    last = dve.max(top8[:, t, :], bank["x1"][:, t * NR:(t + 1) * NR])
                link(last)
                dve.tensor_tensor(top_d[:, :, 0:1], top8[:, :, 0:1], top8[:, :, 1:2], ALU.subtract)
                dve.tensor_tensor(top_d[:, :, 1:2], top8[:, :, 1:2], top8[:, :, 0:1], ALU.subtract
                                  ).then_inc(S["route_d"], 1)

            def route_sum(b):
                dve.wait_ge(S["route_sig"], b + 1)
                link(dve.tensor_scalar(top_w[:, :, :], top_w[:, :, :], 0.5, 0.5, ALU.mult, ALU.add))
                link(dve.tensor_tensor(comb[:, :], top_w[:, :, 0], top_w[:, :, 1], ALU.add))

            def shared_residual(b):
                dve.wait_ge(S["ffn_y"], FFN_CHUNKS * b + FFN_CHUNKS - 1)
                add_bank(b, "u", "shared_x")

            def routed_residual(b):
                dve.wait_ge(S["ffn_y"], FFN_CHUNKS * (b + 1))
                dve.wait_ge(S["shared_x"], b + 1)
                for t in range(NT):
                    last = dve.scalar_tensor_tensor(out=x[:, b, t, :], in0=bank["o"][:, t * D:(t + 1) * D],
                                                    scalar=comb[:, t:t + 1], in1=x[:, b, t, :],
                                                    op0=ALU.mult, op1=ALU.add)
                last.then_inc(S["ffn_x"], 1)

            def batch(b, last):
                nxt = b + 1

                def beside(h):
                    if last:
                        return
                    if h == 0:
                        lnq_apply(nxt, xn).then_inc(S["lnq_xn"], 1)
                    elif h == 1:
                        q_scaled_w(nxt, 0)
                    elif h == 2:
                        q_scaled_x(nxt, 0)
                        q_rowmax(nxt, 0, slice(2, 4))
                    elif h == 3:
                        q_rowmax(nxt, 0, slice(0, 2))
                        q_scales(nxt, 0)
                    elif h == 4:
                        q_ctx_amax(nxt)
                    elif h == 5:
                        q_bf_w(nxt)
                    elif h == 6:
                        q_dequant(nxt, 0).then_inc(S["q_hs"], 1)
                    elif h == 8:
                        q_ratio1(nxt)
                    elif h == 10:
                        q_scaled_w(nxt, 1)
                        q_scaled_x(nxt, 1)
                        q_rowmax(nxt, 1, slice(0, 4))
                        q_scales(nxt, 1)
                    elif h == 12:
                        q_dequant(nxt, 1).then_inc(S["q_out"], 1)
                    elif h == 13:
                        ln_stats_of(nxt, "lnb")
                    elif h == 14:
                        ln_apply(nxt, "lnb")
                    elif h == 15:
                        ln_lo(nxt, "lnb", xt_hi, xt_lo)

                def before(h):
                    if last:
                        return
                    if h == 0:
                        q_take(nxt)
                    elif h == 7:
                        q_sigmoid(nxt)

                attention(b, before, beside)
                mix_lo(b, H - 1)
                if not last:
                    bit_act(nxt, 0)
                dve.wait_ge(S["o_mm"], H * (b + 1))
                add_bank(b, "o", "att_x")
                if not last:
                    bit_act(nxt, 1)
                dve.wait_ge(S["att_x"], b + 1)
                ln_stats_of(b, "lnf")
                if not last:
                    bit_act(nxt, 2)
                ln_apply(b, "lnf")
                if not last:
                    bit_act(nxt, 3)
                    bit_act(nxt, 4)
                ln_lo(b, "lnf", yt_hi, yt_lo)
                if not last:
                    bit_act(nxt, 5)
                    bit_residual(nxt)
                    ln_stats_of(nxt, "lna")
                ffn_act(b, 0)
                if not last:
                    ln_apply(nxt, "lna")
                if not last:
                    route_top(b)
                for c in range(1, FFN_CHUNKS):
                    ffn_act(b, c)
                    if last and c == ROUTE_LATE:
                        route_top(b)
                    if c == (ROUTE_LATE + 2 if last else 2):
                        route_sum(b)
                    if not last:
                        if c == 3:
                            ln_lo(nxt, "lna", xt_hi, xt_lo)
                            ctx_split_lo(nxt)
                        if c == 4:
                            mask_row(nxt)
                        if c == 5:
                            queries_lo(nxt, 0)
                        if c == 7:
                            row_minima(nxt, 0)
                if not last:
                    row_inverses(nxt, 0)
                dve.wait_ge(S["ffn_hi"], FFN_CHUNKS * (b + 1))
                r = (FFN_CHUNKS - 1) % 3
                dve.tensor_tensor(act_lo[:, r, :], act_raw[:, r, :], f32(act_hi[:, r, :]), ALU.subtract
                                  ).then_inc(S["ffn_lo_last"], 1)
                shared_residual(b)
                if not last:
                    queries_lo(nxt, 1)
                routed_residual(b)
                if not last:
                    row_minima(nxt, 1)

            def prep_lo(k):
                dve.wait_ge(S["prep_hi"], k + 1)
                p = k // 2
                lo, hi = ((t[:, 2 * p:2 * p + 2, :, :].rearrange("p h s c -> p (h s c)") for t in (a_lo, a_hi))
                          if k % 2 == 0 else
                          (t[:, 2 * p:2 * p + 2, :].rearrange("p h d -> p (h d)") for t in (c_lo, c_hi)))
                dve.scalar_tensor_tensor(out=lo, in0=PREP_BANKS[k % 2][:, :], scalar=-SCALE if k % 2 == 0 else 1.0,
                                         in1=f32(hi), op0=ALU.mult, op1=ALU.subtract).then_inc(S["prep_lo"], 1)

            def ternary_scales():
                dve.wait_ge(S["gamma_mm"], 1)
                link(dve.tensor_scalar(gam[:, :], bank["u"][:, 0:4], 1.0 / (BIT * D), None, ALU.mult))
                link(dve.tensor_tensor(gam[:, 2:3], gam[:, 2:3], gam[:, 3:4], ALU.add))
                link(dve.tensor_scalar(gam[:, 0:3], gam[:, 0:3], BIT_EPS, None, ALU.add))
                dve.reciprocal(gam[:, 0:3], gam[:, 0:3]).then_inc(S["gamma_inv"], 1)
                dve.wait_ge(S["gamma_inv"], 1)

            def ternary3_clip():
                dve.wait_ge(S["bit_r3"], 1)
                for w in (w3_raw[:, 0:BIT_FULL, :], w3_raw[0:BIT_REST, BIT_FULL, :]):
                    last = dve.tensor_scalar(w, w, MAGIC + 1.0, MAGIC - 1.0, ALU.min, ALU.max)
                last.then_inc(S["bit_q3"], 1)

            def ternary(part):
                if part == 0:
                    for j in range(2):
                        w = w12_raw[:, :, j * BIT:(j + 1) * BIT]
                        last = dve.tensor_scalar(w, w, gam[:, j:j + 1], MAGIC, ALU.mult, ALU.add)
                    link(last)
                else:
                    dve.tensor_scalar(w12_raw[:, :, :], w12_raw[:, :, :], MAGIC + 1.0, MAGIC - 1.0, ALU.min, ALU.max
                                      ).then_inc(S["bit_q12"], 1)

            dve.wait_ge(S["x0_in"], 16)
            link(lnq_stats_of([0]))
            lnq_variances([0])
            dve.wait_ge(S["lnq_pow"], 1)
            lnq_apply(0, xn).then_inc(S["lnq_xn"], 1)
            dve.wait_ge(S["guT0_in"], 16)
            q_amax0_w(0)
            dve.wait_ge(S["q0_xt"], 1)
            link(q_amax0_x(0, bank["x0"]))
            q_ratio0(0, 1)
            q_take(0)
            q_ctx_amax(0)
            prep_lo(0)
            q_scaled_w(0, 0)
            q_scaled_x(0, 0)
            q_rowmax(0, 0, slice(0, 4))
            q_scales(0, 0)
            q_round_w0(0)
            prep_lo(1)
            prep_lo(2)
            q_bf_w(0)
            dve.wait_ge(S["x_in"], 16 * (NB - 1))
            lnq_stats_of([1, 2])
            q_dequant(0, 0).then_inc(S["q_hs"], 1)
            prep_lo(3)
            q_sigmoid(0)
            link(lnq_stats_of([3]))
            lnq_variances(range(1, NB))
            q_ratio1(0)
            dve.wait_ge(S["lnq_pow"], 2)
            dve.scalar_tensor_tensor(out=lnq_shift[:, 1:NB, :], in0=lnq_mv[:, 1:NB, :, 0], scalar=-1.0,
                                     in1=lnq_rstd[:, 1:NB, :], op0=ALU.mult, op1=ALU.mult
                                     ).then_inc(S["lnq_shift"], 1)
            ternary_scales()
            prep_lo(4)
            prep_lo(5)
            q_scaled_w(0, 1)
            q_scaled_x(0, 1)
            q_rowmax(0, 1, slice(0, 4))
            q_scales(0, 1)
            q_round_w0(1)
            prep_lo(6)
            ternary(0)
            prep_lo(7)
            ternary(1)
            q_dequant(0, 1).then_inc(S["q_out"], 1)
            q_residual0()
            prep_lo(8)
            ln_stats_of(0, "lnb")
            prep_lo(9)
            ln_apply(0, "lnb")
            ternary3_clip()
            ln_lo(0, "lnb", xt_hi, xt_lo)
            prep_lo(10)
            dve.wait_ge(S["next_turned"], 1)
            for b in range(1, NB):
                last = q_amax0_x(b, NEXT_BANKS[b - 1])
            last.then_inc(S["next_read"], 1)
            prep_lo(11)

            def ffn_weights_lo(u):
                dve.wait_ge(S["ffn_w_hi"], u + 1)
                dve.tensor_tensor(ffn_unit(u, LO), ffn_unit(u, RAW), f32(ffn_unit(u, HI)), ALU.subtract
                                  ).then_inc(S["ffn_w_lo_dve"], 1)

            for c in range(BIT_CHUNKS):
                bit_act(0, c)
                if c == 0:
                    prep_lo(12)
                elif 2 <= c < 5:
                    if c == 2:
                        dve.wait_ge(S["guT_in"], 16 * (NB - 1))
                    q_amax0_w(c - 1)
            bit_residual(0)
            ln_stats_of(0, "lna")
            prep_lo(13)
            ln_apply(0, "lna")
            prep_lo(14)
            ln_lo(0, "lna", xt_hi, xt_lo)
            ctx_split_lo(0)
            prep_lo(15)
            q_ratio0(1, NB)
            mask_row(0)
            queries_lo(0, 0)
            ffn_weights_lo(FFN_LO_DVE[0])
            dve.wait_ge(S["router_hi"], 1)
            dve.tensor_tensor(router_lo[:, :, :], router_raw[:, :, :], f32(router_hi[:, :, :]), ALU.subtract
                              ).then_inc(S["router_lo"], 1)
            row_minima(0, 0)
            row_minima(0, 1)
            row_inverses(0, 0)
            queries_lo(0, 1)
            ffn_weights_lo(FFN_LO_DVE[1])
            dve.wait_ge(S["q_roots"], 2)
            start = links["n"]
            with dve.Fori(0, NB - 1) as b:
                links["base"], links["n"] = b * LINKS + start, 0
                batch(b, False)
                assert links["n"] == LINKS, links["n"]
            links["base"], links["n"] = start + (NB - 1) * LINKS, 0
            batch(NB - 1, True)


def kernel(**inputs):
    import numpy as np
    import concourse.bacc as bacc
    from concourse.bass_utils import run_bass_kernel_spmd

    def t(a):
        return np.ascontiguousarray(np.swapaxes(np.asarray(a), -1, -2))

    w1T, w2T = t(inputs["L0_ffn_w1"]), t(inputs["L0_ffn_w2"])
    full = BIT_FULL * P
    layout = {
        "x": inputs["x"],
        "gu": inputs["fside_BxS2xS2_0"],
        "guT": t(inputs["fside_BxS2xS2_0"]),
        "ctx": inputs["ctx_1024"],
        "ctxT": t(inputs["ctx_1024"]),
        "mask": np.asarray(inputs["mask_BxS2_bf1"]).view(np.uint8),
        "w12T": np.concatenate([w1T, w2T[:, full:], w2T[:, :full]], axis=1),
        "w3T": t(inputs["L0_ffn_w3"]),
        "wqT": t(inputs["L1_xattn_Wq"]),
        "wkT": t(inputs["L1_xattn_Wk"]),
        "wvT": t(inputs["L1_xattn_Wv"]),
        "wo": inputs["L1_xattn_Wo"],
        "routerT": t(inputs["L1_ffn_router_weight"]),
        "gateT": np.concatenate([t(inputs["L1_ffn_sh_gate"]), t(inputs["L1_ffn_r_gate"])], axis=1),
        "upT": np.concatenate([t(inputs["L1_ffn_sh_up"]), t(inputs["L1_ffn_r_up"])], axis=1),
        "downT": np.concatenate([t(inputs["L1_ffn_sh_down"]), t(inputs["L1_ffn_r_down"])], axis=0)
                   .reshape(FFN_CHUNKS, P, D).transpose(1, 0, 2).reshape(FFN, D),
    }
    nc = bacc.Bacc("TRN2", target_bir_lowering=False, num_devices=1)
    arrays, args = {}, []
    for name, a in layout.items():
        a = np.ascontiguousarray(a)
        arrays[f"in_{name}"] = a
        args.append(nc.dram_tensor(f"in_{name}", a.shape, mybir.dt.from_np(a.dtype), kind="ExternalInput").ap())
    args.append(nc.dram_tensor("out_x", (NB, T, D), F32, kind="ExternalOutput").ap())
    build(nc, *args)
    return run_bass_kernel_spmd(nc, [arrays], core_ids=[0]).results[0]["out_x"]
```
